# Optimizing a Trainium2 kernel written in Bass

```python
import numpy as np
import jax
import jax.numpy as jnp

def _softmax(x, axis=-1):
    return jax.nn.softmax(x, axis=axis)

def _gelu(x):
    return jax.nn.gelu(x, approximate=True)

def _silu(x):
    return jax.nn.silu(x)

def _sigmoid(x):
    return jax.nn.sigmoid(x)

def _layernorm(x, axis=-1, eps=1e-05):
    m = jnp.mean(x, axis=axis, keepdims=True)
    v = jnp.var(x, axis=axis, keepdims=True)
    return (x - m) / jnp.sqrt(v + eps)

def _scatter_add(tgt, idx, src, axis=0):
    return tgt.at[idx].add(src)

def _segment_sum(src, seg, n):
    return jax.ops.segment_sum(src, seg, n)
kernel_name = 'mk_hybrid_d1_jaxref_r8_ff60ff'

def setup_inputs(seed: int=0):
    np.random.seed(seed)
    _w = jnp.asarray

    def _L0_attn_a_setup():
        import jax, jax.numpy as jnp
        import numpy as np
        EMB = 256
        H = 16
        Q_RANK = 192
        KV_RANK = 64
        ROPE_D = 64
        NOPE_D = 64
        V_D = 128
        QK_D = ROPE_D + NOPE_D
        ROPE_BASE = 10000.0
        SCALING = 1.0

        def apply_rope(x):
            S, D = (x.shape[1], x.shape[-1])
            theta = 1.0 / ROPE_BASE ** (jnp.arange(0, D, 2, dtype=jnp.float32) / D)
            ang = jnp.arange(S, dtype=jnp.float32)[:, None] * theta[None, :]
            cos = jnp.cos(ang)[None, :, None, :]
            sin = jnp.sin(ang)[None, :, None, :]
            xf = x.astype(jnp.float32).reshape(*x.shape[:-1], D // 2, 2)
            x0, x1 = (xf[..., 0], xf[..., 1])
            out = jnp.stack([x0 * cos - x1 * sin, x1 * cos + x0 * sin], axis=-1)
            return out.reshape(x.shape).astype(x.dtype)
        key = jax.random.key(seed)
        ks = jax.random.split(key, 6)
        s = lambda fan_in: 1.0 / np.sqrt(fan_in)
        return {'x': jax.random.normal(ks[0], (2, 256, EMB), dtype=jnp.float32), 'q_a_w': jax.random.uniform(ks[1], (Q_RANK, EMB), jnp.float32, -s(EMB), s(EMB)), 'q_b_w': jax.random.uniform(ks[2], (H * QK_D, Q_RANK), jnp.float32, -s(Q_RANK), s(Q_RANK)), 'kv_a_w': jax.random.uniform(ks[3], (KV_RANK + ROPE_D, EMB), jnp.float32, -s(EMB), s(EMB)), 'kv_b_w': jax.random.uniform(ks[4], (H * (NOPE_D + V_D), KV_RANK), jnp.float32, -s(KV_RANK), s(KV_RANK)), 'o_w': jax.random.uniform(ks[5], (EMB, H * V_D), jnp.float32, -s(H * V_D), s(H * V_D))}
    _L0_attn_a_in = _L0_attn_a_setup()

    def _L0_attn_b_setup():
        import jax, jax.numpy as jnp
        import numpy as np
        INFTY_APPROX = 1e+30
        ROTARY_BASE = 10000.0
        ATTN_SCALE = 1.0 / 128.0

        def rope(x):
            T, D = (x.shape[-2], x.shape[-1])
            half = D // 2
            pos = jnp.arange(T, dtype=jnp.float32)[:, None]
            freqs = jnp.power(ROTARY_BASE, -jnp.arange(half, dtype=jnp.float32) / half)[None, :]
            rad = pos * freqs
            cos = jnp.cos(rad).astype(x.dtype)
            sin = jnp.sin(rad).astype(x.dtype)
            even, odd = jnp.split(x, 2, axis=-1)
            r_even = even * cos - odd * sin
            r_odd = even * sin + odd * cos
            return jnp.concatenate([r_even, r_odd], axis=-1)
        key = jax.random.key(seed)
        ks = jax.random.split(key, 5)
        B, T, M, H, D = (2, 256, 256, 16, 128)
        stddev = M ** (-0.5)
        return {'x': jax.random.normal(ks[0], (B, T, M), dtype=jnp.float32), 'wq': stddev * jax.random.normal(ks[1], (M, H, D), dtype=jnp.float32), 'wk': stddev * jax.random.normal(ks[2], (M, H, D), dtype=jnp.float32), 'wv': stddev * jax.random.normal(ks[3], (M, H, D), dtype=jnp.float32), 'wo': stddev * jax.random.normal(ks[4], (H, D, M), dtype=jnp.float32)}
    _L0_attn_b_in = _L0_attn_b_setup()

    def _L0_ffn_setup():
        import jax, jax.numpy as jnp
        import numpy as np
        GOLDEN_CENTER = 1.0 / np.e
        GOLDEN_LOWER = 0.5 - np.log(4.0 / 3.0)
        GOLDEN_UPPER = 0.5

        def _golden_weights(x, Wr, temperature):
            inh = jax.nn.sigmoid(x @ Wr / temperature)
            in_zone = (inh >= GOLDEN_LOWER) & (inh <= GOLDEN_UPPER)
            distance = jnp.abs(inh - GOLDEN_CENTER)
            weights = jnp.exp(-distance / 0.1) * in_zone.astype(x.dtype)
            wsum = jnp.sum(weights, axis=-1, keepdims=True)
            no_expert = wsum < 1e-08
            fb = jnp.exp(-distance / 0.3)
            _, top2 = jax.lax.top_k(fb, 2)
            fb_mask = jnp.sum(jax.nn.one_hot(top2, weights.shape[-1], dtype=x.dtype), axis=-2)
            fb_w = fb * fb_mask
            fb_w = fb_w / jnp.maximum(jnp.sum(fb_w, axis=-1, keepdims=True), 1e-08)
            weights = jnp.where(no_expert, fb_w, weights)
            weights = weights / jnp.maximum(jnp.sum(weights, axis=-1, keepdims=True), 1e-08)
            return weights
        key = jax.random.key(seed)
        ks = jax.random.split(key, 5)
        B, T, D, E, F = (2, 256, 256, 8, 256)
        s_in = 1.0 / np.sqrt(D)
        s_f = 1.0 / np.sqrt(F)
        return {'x': jax.random.normal(ks[0], (B, T, D), dtype=jnp.float32), 'Wg': jax.random.normal(ks[1], (E, D, F), dtype=jnp.float32) * s_in, 'Wu': jax.random.normal(ks[2], (E, D, F), dtype=jnp.float32) * s_in, 'Wd': jax.random.normal(ks[3], (E, F, D), dtype=jnp.float32) * s_f, 'Wr': jax.random.normal(ks[4], (D, E), dtype=jnp.float32) * s_in, 'temperature': jnp.ones((1,), dtype=jnp.float32)}
    _L0_ffn_in = _L0_ffn_setup()
    _d = {'L0_attn_a_x': _L0_attn_a_in['x'], 'L0_attn_a_q_a_w': _L0_attn_a_in['q_a_w'], 'L0_attn_a_q_b_w': _L0_attn_a_in['q_b_w'], 'L0_attn_a_kv_a_w': _L0_attn_a_in['kv_a_w'], 'L0_attn_a_kv_b_w': _L0_attn_a_in['kv_b_w'], 'L0_attn_a_o_w': _L0_attn_a_in['o_w'], 'L0_attn_b_wq': _L0_attn_b_in['wq'], 'L0_attn_b_wk': _L0_attn_b_in['wk'], 'L0_attn_b_wv': _L0_attn_b_in['wv'], 'L0_attn_b_wo': _L0_attn_b_in['wo'], 'L0_ffn_Wg': _L0_ffn_in['Wg'], 'L0_ffn_Wu': _L0_ffn_in['Wu'], 'L0_ffn_Wd': _L0_ffn_in['Wd'], 'L0_ffn_Wr': _L0_ffn_in['Wr'], 'L0_ffn_temperature': _L0_ffn_in['temperature']}
    _x0 = _d['L0_attn_a_x']
    _d['L0_attn_a_x'] = jax.random.normal(jax.random.fold_in(jax.random.key(seed), 1), (8, 256, 256), dtype=_x0.dtype)
    del _x0
    return _d

def reference(L0_attn_a_x, L0_attn_a_q_a_w, L0_attn_a_q_b_w, L0_attn_a_kv_a_w, L0_attn_a_kv_b_w, L0_attn_a_o_w, L0_attn_b_wq, L0_attn_b_wk, L0_attn_b_wv, L0_attn_b_wo, L0_ffn_Wg, L0_ffn_Wu, L0_ffn_Wd, L0_ffn_Wr, L0_ffn_temperature):

    def _L0_attn_a_ref(x, q_a_w, q_b_w, kv_a_w, kv_b_w, o_w):
        import jax, jax.numpy as jnp
        import numpy as np
        EMB = 256
        H = 16
        Q_RANK = 192
        KV_RANK = 64
        ROPE_D = 64
        NOPE_D = 64
        V_D = 128
        QK_D = ROPE_D + NOPE_D
        ROPE_BASE = 10000.0
        SCALING = 1.0

        def apply_rope(x):
            S, D = (x.shape[1], x.shape[-1])
            theta = 1.0 / ROPE_BASE ** (jnp.arange(0, D, 2, dtype=jnp.float32) / D)
            ang = jnp.arange(S, dtype=jnp.float32)[:, None] * theta[None, :]
            cos = jnp.cos(ang)[None, :, None, :]
            sin = jnp.sin(ang)[None, :, None, :]
            xf = x.astype(jnp.float32).reshape(*x.shape[:-1], D // 2, 2)
            x0, x1 = (xf[..., 0], xf[..., 1])
            out = jnp.stack([x0 * cos - x1 * sin, x1 * cos + x0 * sin], axis=-1)
            return out.reshape(x.shape).astype(x.dtype)
        B, S, _ = x.shape
        q = x @ q_a_w.T @ q_b_w.T
        q = q.reshape(B, S, H, QK_D).transpose(0, 2, 1, 3)
        q_pass, q_rot = (q[..., :NOPE_D], q[..., NOPE_D:])
        ckv = x @ kv_a_w.T
        k_pass_c, k_rot = (ckv[..., :KV_RANK], ckv[..., KV_RANK:])
        kvb = (k_pass_c @ kv_b_w.T).reshape(B, S, H, NOPE_D + V_D).transpose(0, 2, 1, 3)
        k_pass, v = (kvb[..., :NOPE_D], kvb[..., NOPE_D:])
        q_rot = apply_rope(q_rot.transpose(0, 2, 1, 3)).transpose(0, 2, 1, 3)
        k_rot = apply_rope(k_rot[:, :, None, :])
        k_rot = jnp.broadcast_to(k_rot.transpose(0, 2, 1, 3), (B, H, S, ROPE_D))
        query = jnp.concatenate([q_pass, q_rot], axis=-1)
        key = jnp.concatenate([k_pass, k_rot], axis=-1)
        scores = jnp.einsum('bhqd,bhkd->bhqk', query, key) * SCALING
        attn = jax.nn.softmax(scores.astype(jnp.float32), axis=-1).astype(query.dtype)
        out = jnp.einsum('bhqk,bhkd->bhqd', attn, v)
        out = out.transpose(0, 2, 1, 3).reshape(B, S, H * V_D)
        return out @ o_w.T

    def _L0_attn_b_ref(x, wq, wk, wv, wo):
        import jax, jax.numpy as jnp
        import numpy as np
        INFTY_APPROX = 1e+30
        ROTARY_BASE = 10000.0
        ATTN_SCALE = 1.0 / 128.0

        def rope(x):
            T, D = (x.shape[-2], x.shape[-1])
            half = D // 2
            pos = jnp.arange(T, dtype=jnp.float32)[:, None]
            freqs = jnp.power(ROTARY_BASE, -jnp.arange(half, dtype=jnp.float32) / half)[None, :]
            rad = pos * freqs
            cos = jnp.cos(rad).astype(x.dtype)
            sin = jnp.sin(rad).astype(x.dtype)
            even, odd = jnp.split(x, 2, axis=-1)
            r_even = even * cos - odd * sin
            r_odd = even * sin + odd * cos
            return jnp.concatenate([r_even, r_odd], axis=-1)
        T = x.shape[1]
        q = jnp.einsum('bim,mhd->bhid', x, wq)
        k = jnp.einsum('bim,mhd->bhid', x, wk)
        v = jnp.einsum('bim,mhd->bhid', x, wv)
        q = rope(q)
        k = rope(k)
        mult = jnp.asarray(ATTN_SCALE ** 0.5, dtype=x.dtype)
        s = jnp.einsum('bhid,bhjd->bhij', q * mult, k * mult)
        i = jnp.arange(T)[:, None]
        j = jnp.arange(T)[None, :]
        mask = jnp.less(i, j).astype(s.dtype)[None, None, :, :]
        s = s - jnp.asarray(INFTY_APPROX, dtype=s.dtype) * mask
        p = jax.nn.softmax(s, axis=-1)
        o = jnp.einsum('bhij,bhjd->bhid', p, v)
        r = jnp.einsum('bhid,hdm->bim', o, wo)
        return r

    def _L0_ffn_ref(x, Wg, Wu, Wd, Wr, temperature):
        import jax, jax.numpy as jnp
        import numpy as np
        GOLDEN_CENTER = 1.0 / np.e
        GOLDEN_LOWER = 0.5 - np.log(4.0 / 3.0)
        GOLDEN_UPPER = 0.5

        def _golden_weights(x, Wr, temperature):
            inh = jax.nn.sigmoid(x @ Wr / temperature)
            in_zone = (inh >= GOLDEN_LOWER) & (inh <= GOLDEN_UPPER)
            distance = jnp.abs(inh - GOLDEN_CENTER)
            weights = jnp.exp(-distance / 0.1) * in_zone.astype(x.dtype)
            wsum = jnp.sum(weights, axis=-1, keepdims=True)
            no_expert = wsum < 1e-08
            fb = jnp.exp(-distance / 0.3)
            _, top2 = jax.lax.top_k(fb, 2)
            fb_mask = jnp.sum(jax.nn.one_hot(top2, weights.shape[-1], dtype=x.dtype), axis=-2)
            fb_w = fb * fb_mask
            fb_w = fb_w / jnp.maximum(jnp.sum(fb_w, axis=-1, keepdims=True), 1e-08)
            weights = jnp.where(no_expert, fb_w, weights)
            weights = weights / jnp.maximum(jnp.sum(weights, axis=-1, keepdims=True), 1e-08)
            return weights
        weights = _golden_weights(x, Wr, temperature)
        gate = jnp.einsum('btd,edf->betf', x, Wg)
        up = jnp.einsum('btd,edf->betf', x, Wu)
        h = jax.nn.silu(gate) * up
        e_out = jnp.einsum('betf,efd->betd', h, Wd)
        out = jnp.einsum('bte,betd->btd', weights, e_out)
        return out
    x = L0_attn_a_x
    x = x + _L0_attn_a_ref(_layernorm(x, axis=-1), L0_attn_a_q_a_w, L0_attn_a_q_b_w, L0_attn_a_kv_a_w, L0_attn_a_kv_b_w, L0_attn_a_o_w)
    x = x + _L0_ffn_ref(_layernorm(x, axis=-1), L0_ffn_Wg, L0_ffn_Wu, L0_ffn_Wd, L0_ffn_Wr, L0_ffn_temperature)
    x = x + _L0_attn_b_ref(_layernorm(x, axis=-1), L0_attn_b_wq, L0_attn_b_wk, L0_attn_b_wv, L0_attn_b_wo)
    x = x + _L0_ffn_ref(_layernorm(x, axis=-1), L0_ffn_Wg, L0_ffn_Wu, L0_ffn_Wd, L0_ffn_Wr, L0_ffn_temperature)
    return x

_drawn_inputs = setup_inputs


def setup_inputs(seed=0):
    import zlib

    import numpy as np

    out = dict(_drawn_inputs(seed))
    spreads = {}
    factors = {}
    for name, (base, spread) in spreads.items():
        noise = np.random.default_rng([zlib.crc32(name.encode()), seed]).standard_normal(out[name].shape)
        drawn = base * np.exp(spread * noise) if base else spread * noise
        out[name] = jnp.asarray(drawn.astype(out[name].dtype))
    for name, factor in factors.items():
        out[name] = (out[name] * factor).astype(out[name].dtype)
    return out
```

```python
from contextlib import ExitStack

import concourse.bass as bass
from concourse import mybir
import numpy as np

ALU = mybir.AluOpType
ACT = mybir.ActivationFunctionType
AX = mybir.AxisListType.X
F32 = mybir.dt.float32
F32R = mybir.dt.float32r
BF16 = mybir.dt.bfloat16

P = 128
B, T, D = 8, 256, 256
N = B * T
NT = N // P
KD = D // P
G = 512
NG = N // G
TG = G // P
BG = G // T
H = 16
HP = H // 2
QR, KVR, ROT, NOPE, VD = 192, 64, 64, 64, 128
E, F = 8, 256
EPS = 1e-5
GOLDEN_CENTER = 1.0 / np.e
GOLDEN_LOWER = 0.5 - np.log(4.0 / 3.0)
LOGIT_LOWER = float(np.log(GOLDEN_LOWER / (1.0 - GOLDEN_LOWER)))

A_PASS, A_K, A_ROT, A_V, A_O = 0, 256, 320, 576, 704
A_COLS = 1216
C_COSA, C_SINA, C_COSB, C_SINB, C_IDENT, C_MASK = 0, 256, 512, 768, 1024, 1152
C_COLS = 1280
S_QA, S_KVA, S_WR = 0, 256, 384
S_COLS = 392


class Core:
    pass


def layer_norm(nc, c, name, prepare=None):
    with ExitStack() as ctx:
        sem = lambda n: ctx.enter_context(nc.semaphore(f"{name}_{n}"))
        sb = lambda n, s, d=F32: ctx.enter_context(nc.sbuf_tensor(f"{name}_{n}", s, d))
        moments = sb("moments", [P, NT, 6])
        meanvar = sb("meanvar", [P, NT, 2])
        shifted = sb("shifted", [P, NT])
        rstd = sb("rstd", [P, NT])
        minus_half = sb("minus_half", [P, NT])
        normed = sb("normed", [P, 2, TG, D])
        stats_done, var_done, rstd_done = sem("stats_done"), sem("var_done"), sem("rstd_done")
        half_set, normed_done, turned = sem("half_set"), sem("normed_done"), sem("turned")
        hi_done, lo_done = sem("hi_done"), sem("lo_done")

        def bank(g, k):
            return c.ps[:, 4 * (g % 2) + k, :]

        block = ctx.enter_context(nc.Block())

        def lo_parts(dve, g):
            for k in range(KD):
                dve.wait_ge(hi_done, KD * g + k + 1)
                s = slice(g * G, (g + 1) * G)
                nc.vector.tensor_tensor(c.xl[:, k, s], bank(g, k), c.xh[:, k, s].bitcast(F32), ALU.subtract).then_inc(lo_done, 1)

        @block.gpsimd
        def _(pool):
            nc.gpsimd.memset(minus_half[:], -0.5).then_inc(half_set, 1)
            pool.wait_ge(half_set, 1)
            for g in range(NG):
                t = slice(g * TG, (g + 1) * TG)
                pool.wait_ge(var_done, g + 1)
                nc.gpsimd.tensor_tensor(rstd[:, t], shifted[:, t], minus_half[:, t], ALU.pow).then_inc(rstd_done, 1)

        @block.vector
        def _(dve):
            stats = 0
            for g in range(NG):
                for t in range(g * TG, (g + 1) * TG):
                    nc.vector.bn_stats(moments[:, t, :], c.x[:, t, :]).then_inc(stats_done, 1)
                stats += TG
                dve.wait_ge(stats_done, stats)
                for t in range(g * TG, (g + 1) * TG):
                    nc.vector.bn_aggr(meanvar[:, t, :], moments[:, t, :]).then_inc(stats_done, 1)
                stats += TG
                dve.wait_ge(stats_done, stats)
                t = slice(g * TG, (g + 1) * TG)
                nc.vector.tensor_scalar(shifted[:, t], meanvar[:, t, 1], EPS, None, ALU.add).then_inc(var_done, 1)

            for g in range(NG):
                dve.wait_ge(rstd_done, g + 1)
                if g >= 2:
                    dve.wait_ge(turned, KD * (g - 1))
                for i in range(TG):
                    t = g * TG + i
                    ins = nc.vector.tensor_scalar(normed[:, g % 2, i, :], c.x[:, t, :], meanvar[:, t, 0:1], rstd[:, t:t + 1], ALU.subtract, ALU.mult)
                ins.then_inc(normed_done, 1)
                if g >= 1:
                    lo_parts(dve, g - 1)
            lo_parts(dve, NG - 1)

        @block.tensor
        def _(pe):
            for g in range(NG):
                pe.wait_ge(normed_done, g + 1)
                if g >= 2:
                    pe.wait_ge(lo_done, KD * (g - 1))
                for k in range(KD):
                    for i in range(TG):
                        ins = nc.tensor.transpose(bank(g, k)[:, i * P:(i + 1) * P], normed[:, g % 2, i, k * P:(k + 1) * P], c.ident)
                    ins.then_inc(turned, 1)

        @block.scalar
        def _(act):
            for g in range(NG):
                for k in range(KD):
                    act.wait_ge(turned, KD * g + k + 1)
                    nc.scalar.copy(c.xh[:, k, g * G:(g + 1) * G], bank(g, k)).then_inc(hi_done, 1)


def matmul3(nc, out, left, right, start, stop):
    (lh, ll), (rh, rl) = left, right
    nc.tensor.matmul(out, ll, rh, start=start, stop=False)
    nc.tensor.matmul(out, lh, rl, start=False, stop=False)
    return nc.tensor.matmul(out, lh, rh, start=False, stop=stop)


def latents(nc, c, name, a):
    with ExitStack() as ctx:
        sem = lambda n: ctx.enter_context(nc.semaphore(f"{name}_{n}"))
        sb = lambda n, s, d=F32: ctx.enter_context(nc.sbuf_tensor(f"{name}_{n}", s, d))
        swapped = sb("swapped", [P, 2, G])
        proj_ready, hi_done, lo_done = sem("proj_ready"), sem("hi_done"), sem("lo_done")
        rope_read, rotated, turned, values_done = sem("rope_read"), sem("rotated"), sem("turned"), sem("values_done")
        qa = lambda w, k, m: w[:, k, S_QA + m * P:S_QA + (m + 1) * P]
        block = ctx.enter_context(nc.Block())

        def slot(g):
            return slice(g * G, (g + 1) * G)

        @block.tensor
        def _(pe):
            for g in range(NG):
                for m in range(3):
                    if g >= 2 and m < 2:
                        pe.wait_ge(lo_done, 2 * (g - 2) + m + 1)
                    if g >= 2 and m == 2:
                        pe.wait_ge(rope_read, g - 1)
                    out = c.ps[:, 3 * (g % 2) + m, :]
                    col = slice(m * P, (m + 1) * P)
                    for k in range(KD):
                        ins = matmul3(nc, out, (c.sh[:, k, col], c.sl[:, k, col]), (c.xh[:, k, slot(g)], c.xl[:, k, slot(g)]), k == 0, k == KD - 1)
                    ins.then_inc(proj_ready, 1)
            for g in range(NG):
                pe.wait_ge(rope_read, g + 1)
                for i in range(TG):
                    t = g * TG + i
                    ins = nc.tensor.transpose(c.ps[:, 6 + g % 2, i * KVR:(i + 1) * KVR], a.keys[0:KVR, t * P:(t + 1) * P], c.ident[0:KVR, 0:KVR])
                ins.then_inc(turned, 1)
                if g + 2 < NG + 1 and g >= 1:
                    pe.wait_ge(values_done, g)

        @block.scalar
        def _(act):
            for g in range(NG):
                act.wait_ge(proj_ready, 3 * g + 1)
                nc.scalar.copy(a.q1h[:, slot(g)], c.ps[:, 3 * (g % 2), :]).then_inc(hi_done, 1)
                act.wait_ge(proj_ready, 3 * g + 2)
                nc.scalar.copy(a.q2[:, slot(g)], c.ps[:, 3 * (g % 2) + 1, :]).then_inc(hi_done, 1)
            for g in range(NG):
                act.wait_ge(turned, g + 1)
                nc.scalar.copy(a.values[:, g * TG:(g + 1) * TG, :], c.ps[:, 6 + g % 2, 0:TG * KVR].rearrange("p (t d) -> p t d", d=KVR)).then_inc(values_done, 1)

        @block.vector
        def _(dve):
            for g in range(NG):
                dve.wait_ge(hi_done, 2 * g + 1)
                nc.vector.tensor_tensor(a.q1l[:, slot(g)], c.ps[:, 3 * (g % 2), :], a.q1h[:, slot(g)].bitcast(F32), ALU.subtract).then_inc(lo_done, 1)
                dve.wait_ge(hi_done, 2 * g + 2)
                nc.vector.tensor_tensor(a.q2[64:128, slot(g)], c.ps[64:128, 3 * (g % 2) + 1, :], a.q2[64:128, slot(g)].bitcast(F32), ALU.subtract).then_inc(lo_done, 1)
                dve.wait_ge(proj_ready, 3 * g + 3)
                if g >= 2:
                    dve.wait_ge(rotated, g - 1)
                rope_a(nc, c, c.ps[:, 3 * (g % 2) + 2, :], a.keys[:, slot(g)], swapped[:, g % 2, :]).then_inc(rope_read, 1)

        @block.gpsimd
        def _(pool):
            for g in range(NG):
                pool.wait_ge(rope_read, g + 1)
                nc.gpsimd.tensor_tensor(a.keys[64:128, slot(g)], a.keys[64:128, slot(g)], swapped[64:128, g % 2, :], ALU.add).then_inc(rotated, 1)


def by_batch(ap):
    return ap.rearrange("p (b t) -> p b t", t=T)


def table(c, rows, col):
    return c.const[rows, col:col + T].unsqueeze(1).to_broadcast([rows.stop - rows.start, BG, T])


def rope_a(nc, c, src, out, swapped):
    nc.vector.tensor_tensor(by_batch(out), by_batch(src), table(c, slice(0, P), C_COSA), ALU.mult)
    nc.vector.tensor_tensor(by_batch(swapped[64:96]), by_batch(src[96:128]), table(c, slice(96, 128), C_SINA), ALU.mult)
    return nc.vector.tensor_tensor(by_batch(swapped[96:128]), by_batch(src[64:96]), table(c, slice(64, 96), C_SINA), ALU.mult)


def rope_b(nc, c, src, out, swapped):
    nc.vector.tensor_tensor(by_batch(out), by_batch(src), table(c, slice(0, P), C_COSB), ALU.mult)
    nc.vector.tensor_tensor(by_batch(swapped[0:64]), by_batch(src[64:128]), table(c, slice(64, 128), C_SINB), ALU.mult)
    return nc.vector.tensor_tensor(by_batch(swapped[64:128]), by_batch(src[0:64]), table(c, slice(0, 64), C_SINB), ALU.mult)


def attention_a(nc, c, name, a, weights):
    with ExitStack() as ctx:
        sem = lambda n: ctx.enter_context(nc.semaphore(f"{name}_{n}"))
        sb = lambda n, s, d=F32: ctx.enter_context(nc.sbuf_tensor(f"{name}_{n}", s, d))
        stage = sb("stage", [P, A_COLS])
        wh, wl = sb("wh", [P, 2, 2, P], F32R), sb("wl", [P, 2, 2, P], F32R)
        wo = sb("wo", [P, D])
        queries = sb("queries", [P, 2, 2, G])
        swapped = sb("swapped", [P, 2, G])
        negmax, total, inv = sb("negmax", [P, 2, 2]), sb("total", [P, 2, 2]), sb("inv", [P, 2, 2])
        probs = sb("probs", [P, 2, 2, T])
        probsT = sb("probsT", [P, 2, 2, T])
        mixed = sb("mixed", [P, 2, G])
        stage_in, fold_ready, fold_hi, fold_lo = sem("stage_in"), sem("fold_ready"), sem("fold_hi"), sem("fold_lo")
        wo_ready, wo_done = sem("wo_ready"), sem("wo_done")
        proj_ready, rope_read, rotated = sem("proj_ready"), sem("rope_read"), sem("rotated")
        scores_ready, maxed, exp_done, inv_done, scaled = sem("scores_ready"), sem("maxed"), sem("exp_done"), sem("inv_done"), sem("scaled")
        turned, probsT_done, pv_done, mixed_done = sem("turned"), sem("probsT_done"), sem("pv_done"), sem("mixed_done")
        out_ready, out_added = sem("out_ready"), sem("out_added")
        S = lambda j: c.ps[:, j % 2, :]
        TURN = c.ps[:, 2, :]
        PROJ = lambda h: c.ps[:, 3 + h, :]
        MIX = c.ps[:, 5, :]
        OUT = lambda i: c.ps[:, 6 + i, :]
        block = ctx.enter_context(nc.Block())


        @block.sync
        def _(sp):
            sp.dma_start(stage[:], weights[0]).then_inc(stage_in, 16)
            with sp.Fori(1, HP) as it:
                sp.wait_ge(wo_ready, it)
                sp.dma_start(stage[:], weights[bass.ds(it, 1)].squeeze(0)).then_inc(stage_in, 16)

        @block.tensor
        def _(pe):
            def fold_query(it):
                pe.wait_ge(stage_in, 16 * (it + 1))
                for m in range(2):
                    for h in range(2):
                        r = slice(64 * h, 64 * h + 64)
                        ins = nc.tensor.matmul(FOLD(m, h), stage[r, A_PASS + m * P:A_PASS + (m + 1) * P], stage[r, A_K:A_K + KVR], start=True, stop=True)
                ins.then_inc(fold_ready, 1)

            def fold_output(it):
                for h in range(2):
                    ins = nc.tensor.matmul(PROJ(0)[64 * h:64 * h + 64, 0:D], stage[:, A_V + h * KVR:A_V + (h + 1) * KVR], stage[:, A_O + h * D:A_O + (h + 1) * D], start=True, stop=True)
                ins.then_inc(wo_ready, 1)

            def project(it, s, h):
                n = it * NG + s
                if h == 0 and s == 0:
                    pe.wait_ge(fold_lo, 2 * it + 2)
                g = slice(s * G, (s + 1) * G)
                if not (s == 0 and isinstance(it, int) and it == 0):
                    pe.wait_ge(rope_read, 2 * n + h - 1)
                out = PROJ(h)
                nc.tensor.matmul(out, wl[:, 0, h, :], a.q1h[:, g], start=True, stop=False)
                nc.tensor.matmul(out, wh[:, 0, h, :], a.q1l[:, g], start=False, stop=False)
                nc.tensor.matmul(out, wl[:, 1, h, :], a.q2[:, g], start=False, stop=False)
                nc.tensor.matmul(out, wh[:, 1, h, :], a.q2[:, g], start=False, stop=False)
                nc.tensor.matmul(out, wh[:, 0, h, :], a.q1h[:, g], start=False, stop=True).then_inc(proj_ready, 1)

            def scores(it, s, j, first):
                n = it * NG + s
                h, b = j // 2, j % 2
                if j == 0 or j == 2:
                    pe.wait_ge(rotated, 2 * n + h + 1)
                if not (first and j < 2):
                    pe.wait_ge(exp_done, 4 * n + j - 1)
                for q in range(2):
                    ins = nc.tensor.matmul(S(j)[:, q * T:(q + 1) * T], queries[:, s % 2, h, b * T + q * P:b * T + (q + 1) * P], a.keys[:, s * G + b * T:s * G + (b + 1) * T], start=True, stop=True)
                ins.then_inc(scores_ready, 1)

            def turn(it, s, j, first):
                n = it * NG + s
                pe.wait_ge(scaled, 4 * n + j + 1)
                if not (first and j == 0):
                    pe.wait_ge(probsT_done, 4 * n + j)
                for q in range(2):
                    for k in range(2):
                        ins = nc.tensor.transpose(TURN[:, k * T + q * P:k * T + (q + 1) * P], probs[:, j % 2, q, k * P:(k + 1) * P], c.ident)
                ins.then_inc(turned, 1)

            def mix(it, s, j, first):
                n = it * NG + s
                h, b = j // 2, j % 2
                pe.wait_ge(probsT_done, 4 * n + j + 1)
                if j == 0 and not first:
                    pe.wait_ge(mixed_done, n)
                for k in range(2):
                    ins = nc.tensor.matmul(MIX[64 * h:64 * h + 64, b * T:(b + 1) * T], a.values[:, s * TG + b * 2 + k, :], probsT[:, j % 2, k, :], start=(k == 0), stop=(k == 1))
                ins.then_inc(pv_done, 1)

            def output(it, s, first):
                n = it * NG + s
                pe.wait_ge(mixed_done, n + 1)
                if s == 0:
                    pe.wait_ge(wo_done, it + 1)
                for i in range(2):
                    if not first:
                        pe.wait_ge(out_added, 2 * n + i - 1)
                    for t in range(2):
                        col = (2 * i + t) * P
                        ins = nc.tensor.matmul(OUT(i)[:, t * D:(t + 1) * D], mixed[:, s % 2, col:col + P], wo[:], start=True, stop=True)
                    ins.then_inc(out_ready, 1)

            FOLD = lambda m, h: PROJ(h)[:, m * KVR:(m + 1) * KVR]

            def pair(it, first, last):
                for s in range(NG):
                    f = first and s == 0
                    nxt = (it, s + 1) if s + 1 < NG else (it + 1, 0)
                    more = not (last and s == NG - 1)
                    scores(it, s, 0, f)
                    scores(it, s, 1, f)
                    if s == 0:
                        pe.wait_ge(rope_read, 2 * (it * NG + s) + 2)
                        fold_output(it)
                    if s == NG - 1 and more:
                        pe.wait_ge(rope_read, 2 * (it * NG + s) + 2)
                        fold_query(it + 1)
                    turn(it, s, 0, f)
                    scores(it, s, 2, f)
                    turn(it, s, 1, f)
                    mix(it, s, 0, f)
                    scores(it, s, 3, f)
                    mix(it, s, 1, f)
                    turn(it, s, 2, f)
                    if more:
                        if s == 0:
                            pe.wait_ge(wo_done, it + 1)
                        project(*nxt, 0)
                    turn(it, s, 3, f)
                    mix(it, s, 2, f)
                    mix(it, s, 3, f)
                    if more:
                        project(*nxt, 1)
                    output(it, s, f)

            fold_query(0)
            project(0, 0, 0)
            project(0, 0, 1)
            pair(0, True, False)
            with pe.Fori(1, HP - 1) as it:
                pair(it, False, False)
            pair(HP - 1, False, True)

        @block.scalar
        def _(act):
            fold = lambda h: PROJ(h)[:, 0:2 * KVR].rearrange("p (m d) -> p m d", m=2)
            rot = stage[:, A_ROT:A_ROT + 4 * ROT].rearrange("p (m h d) -> p m h d", m=2, h=2)

            def fold_query(it):
                act.wait_ge(fold_ready, it + 1)
                for h in range(2):
                    nc.scalar.copy(wh[:, :, h, 0:KVR], fold(h))
                    ins = nc.scalar.copy(wh[:, :, h, KVR:P], rot[:, :, h])
                ins.then_inc(fold_hi, 1)

            def fold_output(it):
                act.wait_ge(wo_ready, it + 1)
                nc.scalar.copy(wo[:], PROJ(0)[:, 0:D]).then_inc(wo_done, 1)

            def exps(it, s, j, first):
                n = it * NG + s
                act.wait_ge(maxed, 4 * n + j + 1)
                if not (first and j < 2):
                    act.wait_ge(turned, 4 * n + j - 1)
                for q in range(2):
                    ins = nc.scalar.activation(probs[:, j % 2, q, :], S(j)[:, q * T:(q + 1) * T], ACT.Exp, bias=negmax[:, j % 2, q:q + 1], accum_out=total[:, j % 2, q:q + 1])
                ins.then_inc(exp_done, 1)

            def take_turned(it, s, j, first):
                n = it * NG + s
                act.wait_ge(turned, 4 * n + j + 1)
                if not (first and j < 2):
                    act.wait_ge(pv_done, 4 * n + j - 1)
                nc.scalar.copy(probsT[:, j % 2].rearrange("p k t -> p (k t)"), TURN).then_inc(probsT_done, 1)

            def take_mixed(it, s, first):
                n = it * NG + s
                act.wait_ge(pv_done, 4 * n + 4)
                nc.scalar.copy(mixed[:, s % 2, :], MIX).then_inc(mixed_done, 1)

            def pair(it, first, last):
                for s in range(NG):
                    f = first and s == 0
                    exps(it, s, 0, f)
                    exps(it, s, 1, f)
                    if s == 0:
                        fold_output(it)
                    if s == NG - 1 and not last:
                        fold_query(it + 1)
                    take_turned(it, s, 0, f)
                    exps(it, s, 2, f)
                    take_turned(it, s, 1, f)
                    exps(it, s, 3, f)
                    take_turned(it, s, 2, f)
                    take_turned(it, s, 3, f)
                    take_mixed(it, s, f)

            fold_query(0)
            pair(0, True, False)
            with act.Fori(1, HP - 1) as it:
                pair(it, False, False)
            pair(HP - 1, False, True)

        @block.vector
        def _(dve):
            fold = lambda h: PROJ(h)[:, 0:2 * KVR].rearrange("p (m d) -> p m d", m=2)
            rot = stage[:, A_ROT:A_ROT + 4 * ROT].rearrange("p (m h d) -> p m h d", m=2, h=2)

            def fold_query(it):
                dve.wait_ge(fold_hi, it + 1)
                for h in range(2):
                    nc.vector.tensor_tensor(wl[:, :, h, 0:KVR], fold(h), wh[:, :, h, 0:KVR].bitcast(F32), ALU.subtract)
                    nc.vector.tensor_tensor(wl[:, :, h, KVR:P], rot[:, :, h], wh[:, :, h, KVR:P].bitcast(F32), ALU.subtract).then_inc(fold_lo, 1)

            def rope(it, s, h, first):
                n = it * NG + s
                dve.wait_ge(proj_ready, 2 * n + h + 1)
                if not first:
                    dve.wait_ge(rotated, 2 * n + h - 1)
                rope_a(nc, c, PROJ(h), queries[:, s % 2, h, :], swapped[:, h, :]).then_inc(rope_read, 1)

            def row_max(it, s, j):
                dve.wait_ge(scores_ready, 4 * (it * NG + s) + j + 1)
                nc.vector.tensor_reduce(negmax[:, j % 2, :], S(j).rearrange("p (q t) -> p q t", q=2), AX, ALU.max, negate=True).then_inc(maxed, 1)

            def scale(it, s, j):
                g = 4 * (it * NG + s) + j
                dve.wait_ge(exp_done, g + 1)
                nc.vector.reciprocal(inv[:, j % 2, :], total[:, j % 2, :]).then_inc(inv_done, 1)
                dve.wait_ge(inv_done, g + 1)
                for q in range(2):
                    ins = nc.vector.tensor_scalar(probs[:, j % 2, q, :], probs[:, j % 2, q, :], inv[:, j % 2, q:q + 1], None, ALU.mult)
                ins.then_inc(scaled, 1)

            def add_out(it, s):
                for i in range(2):
                    dve.wait_ge(out_ready, 2 * (it * NG + s) + i + 1)
                    t = s * TG + 2 * i
                    nc.vector.tensor_tensor(c.x[:, t:t + 2, :], OUT(i).rearrange("p (t d) -> p t d", d=D), c.x[:, t:t + 2, :], ALU.add).then_inc(out_added, 1)

            def pair(it, first, last):
                for s in range(NG):
                    nxt = (it, s + 1) if s + 1 < NG else (it + 1, 0)
                    more = not (last and s == NG - 1)
                    row_max(it, s, 0)
                    row_max(it, s, 1)
                    if not (first and s == 0):
                        add_out(*((it, s - 1) if s else (it - 1, NG - 1)))
                    if s == NG - 1 and more:
                        fold_query(it + 1)
                    scale(it, s, 0)
                    scale(it, s, 1)
                    row_max(it, s, 2)
                    row_max(it, s, 3)
                    scale(it, s, 2)
                    scale(it, s, 3)
                    if more:
                        rope(*nxt, 0, False)
                        rope(*nxt, 1, False)

            fold_query(0)
            rope(0, 0, 0, True)
            rope(0, 0, 1, True)
            pair(0, True, False)
            with dve.Fori(1, HP - 1) as it:
                pair(it, False, False)
            pair(HP - 1, False, True)
            add_out(HP - 1, NG - 1)

        @block.gpsimd
        def _(pool):
            def rotate(n, s, h):
                pool.wait_ge(rope_read, 2 * n + h + 1)
                q = queries[64:128, s % 2, h, :]
                nc.gpsimd.tensor_tensor(q, q, swapped[64:128, h, :], ALU.add).then_inc(rotated, 1)

            with pool.Fori(0, HP) as it:
                for s in range(NG):
                    for h in range(2):
                        rotate(it * NG + s, s, h)


def attention_b(nc, c, name, w_qkv, w_out):
    W = T + P
    with ExitStack() as ctx:
        sem = lambda n: ctx.enter_context(nc.semaphore(f"{name}_{n}"))
        sb = lambda n, s, d=F32: ctx.enter_context(nc.sbuf_tensor(f"{name}_{n}", s, d))
        stage = sb("stage", [P, 3, KD, 2 * P])
        wh, wl = sb("wh", [P, 3, KD, 2 * P], F32R), sb("wl", [P, 3, KD, 2 * P], F32R)
        wo = sb("wo", [P, 2, D])
        qk = sb("qk", [P, 2, 4, G])
        swapped = sb("swapped", [P, 2, G])
        values = sb("values", [P, 2, TG, 2 * P])
        negmax, total, inv = sb("negmax", [P, 2, 2]), sb("total", [P, 2, 2]), sb("inv", [P, 2, 2])
        probs, probsT = sb("probs", [P, 2, W]), sb("probsT", [P, 2, W])
        mixed = sb("mixed", [P, 2, G])
        stage_in, wo_in, w_hi, w_lo = sem("stage_in"), sem("wo_in"), sem("w_hi"), sem("w_lo")
        proj_ready, rope_read, rotated, values_done = sem("proj_ready"), sem("rope_read"), sem("rotated"), sem("values_done")
        scores_ready, maxed, exp_done, inv_done, scaled = sem("scores_ready"), sem("maxed"), sem("exp_done"), sem("inv_done"), sem("scaled")
        turned, probsT_done, pv_done, mixed_done = sem("turned"), sem("probsT_done"), sem("pv_done"), sem("mixed_done")
        vproj_ready, out_ready, out_added = sem("vproj_ready"), sem("out_ready"), sem("out_added")
        S = lambda j: c.ps[:, j % 2, :]
        TURN = c.ps[:, 2, 0:W]
        PROJ = lambda i: c.ps[:, 3 + i % 2, :]
        MIX = c.ps[:, 5, :]
        OUT = lambda i: c.ps[:, 6 + i, :]
        span = [slice(0, P), slice(P, W)]
        block = ctx.enter_context(nc.Block())

        @block.sync
        def _(sp):
            sp.dma_start(stage[:], w_qkv[0]).then_inc(stage_in, 16)
            sp.dma_start(wo[:], w_out[0]).then_inc(wo_in, 16)
            with sp.Fori(1, HP) as it:
                sp.wait_ge(w_lo, it)
                sp.dma_start(stage[:], w_qkv[bass.ds(it, 1)].squeeze(0)).then_inc(stage_in, 16)
                sp.wait_ge(out_ready, 2 * NG * it)
                sp.dma_start(wo[:], w_out[bass.ds(it, 1)].squeeze(0)).then_inc(wo_in, 16)

        @block.tensor
        def _(pe):
            def project(it, s, i, first=False):
                n = it * NG + s
                if i == 0 and s == 0:
                    pe.wait_ge(w_lo, it + 1)
                if i >= 2:
                    pe.wait_ge(rope_read, 4 * n + i - 1)
                elif not first:
                    pe.wait_ge(values_done, 2 * n + i - 1)
                col = slice((i % 2) * P, (i % 2) * P + P)
                g = slice(s * G, (s + 1) * G)
                for k in range(KD):
                    ins = matmul3(nc, PROJ(i), (wh[:, i // 2, k, col], wl[:, i // 2, k, col]), (c.xh[:, k, g], c.xl[:, k, g]), k == 0, k == KD - 1)
                ins.then_inc(proj_ready, 1)

            def project_values(it, s, i):
                n = it * NG + s
                pe.wait_ge(rope_read, 4 * n + 3 + i)
                for t in range(2):
                    tok = slice(s * G + (2 * i + t) * P, s * G + (2 * i + t + 1) * P)
                    for k in range(KD):
                        ins = matmul3(nc, PROJ(i)[:, t * 2 * P:(t + 1) * 2 * P], (c.xh[:, k, tok], c.xl[:, k, tok]), (wh[:, 2, k, :], wl[:, 2, k, :]), k == 0, k == KD - 1)
                ins.then_inc(vproj_ready, 1)

            def scores(it, s, j, first):
                n = it * NG + s
                h, b = j // 2, j % 2
                if j == 0:
                    pe.wait_ge(rotated, 4 * n + 4)
                if not (first and j < 2):
                    pe.wait_ge(exp_done, 4 * n + j - 1)
                for q in range(2):
                    out = S(j)[:, span[q]]
                    nc.tensor.matmul(out, qk[:, s % 2, h, b * T + q * P:b * T + (q + 1) * P], qk[:, s % 2, 2 + h, b * T:b * T + (q + 1) * P], start=True, stop=False)
                    ins = nc.tensor.matmul(out[:, q * P:(q + 1) * P], c.ident16[:], c.mask16[:], start=False, stop=True)
                ins.then_inc(scores_ready, 1)

            def turn(it, s, j, first):
                n = it * NG + s
                pe.wait_ge(scaled, 4 * n + j + 1)
                if not (first and j == 0):
                    pe.wait_ge(probsT_done, 4 * n + j)
                for i in range(3):
                    ins = nc.tensor.transpose(TURN[:, i * P:(i + 1) * P], probs[:, j % 2, i * P:(i + 1) * P], c.ident)
                ins.then_inc(turned, 1)

            def mix(it, s, j, first):
                n = it * NG + s
                h, b = j // 2, j % 2
                pe.wait_ge(probsT_done, 4 * n + j + 1)
                if j == 0:
                    pe.wait_ge(values_done, 2 * n + 2)
                if b == 0 and not (first and j == 0):
                    pe.wait_ge(mixed_done, 2 * n + h)
                out = MIX[:, b * T:(b + 1) * T]
                v = lambda k: values[:, s % 2, 2 * b + k, h * P:(h + 1) * P]
                nc.tensor.matmul(out, v(0), probsT[:, j % 2, 0:T], start=True, stop=False)
                nc.tensor.matmul(out[:, P:T], v(1), probsT[:, j % 2, T:W], start=False, stop=True).then_inc(pv_done, 1)

            def output(it, s, first):
                n = it * NG + s
                pe.wait_ge(mixed_done, 2 * n + 2)
                if s == 0:
                    pe.wait_ge(wo_in, 16 * (it + 1))
                for i in range(2):
                    if not first:
                        pe.wait_ge(out_added, 2 * n + i - 1)
                    for t in range(2):
                        col = (2 * i + t) * P
                        for h in range(2):
                            ins = nc.tensor.matmul(OUT(i)[:, t * D:(t + 1) * D], mixed[:, h, col:col + P], wo[:, h, :], start=(h == 0), stop=(h == 1))
                    ins.then_inc(out_ready, 1)

            def pair(it, first, last):
                for s in range(NG):
                    f = first and s == 0
                    nxt = (it, s + 1) if s + 1 < NG else (it + 1, 0)
                    more = not (last and s == NG - 1)
                    scores(it, s, 0, f)
                    scores(it, s, 1, f)
                    if more:
                        project(*nxt, 0)
                        project(*nxt, 1)
                    turn(it, s, 0, f)
                    scores(it, s, 2, f)
                    turn(it, s, 1, f)
                    mix(it, s, 0, f)
                    if more:
                        project(*nxt, 2)
                    scores(it, s, 3, f)
                    mix(it, s, 1, f)
                    if more:
                        project(*nxt, 3)
                    turn(it, s, 2, f)
                    if more:
                        project_values(*nxt, 0)
                    turn(it, s, 3, f)
                    mix(it, s, 2, f)
                    mix(it, s, 3, f)
                    if more:
                        project_values(*nxt, 1)
                    output(it, s, f)

            project(0, 0, 0, True)
            project(0, 0, 1, True)
            project(0, 0, 2)
            project(0, 0, 3)
            project_values(0, 0, 0)
            project_values(0, 0, 1)
            pair(0, True, False)
            with pe.Fori(1, HP - 1) as it:
                pair(it, False, False)
            pair(HP - 1, False, True)

        @block.scalar
        def _(act):
            def split_hi(it):
                act.wait_ge(stage_in, 16 * (it + 1))
                if not (isinstance(it, int) and it == 0):
                    act.wait_ge(vproj_ready, 2 * NG * it)
                nc.scalar.copy(wh[:].rearrange("p a k d -> p (a k d)"), stage[:].rearrange("p a k d -> p (a k d)")).then_inc(w_hi, 1)

            def exps(it, s, j, first):
                n = it * NG + s
                act.wait_ge(maxed, 4 * n + j + 1)
                if not (first and j < 2):
                    act.wait_ge(turned, 4 * n + j - 1)
                for q in range(2):
                    ins = nc.scalar.activation(probs[:, j % 2, span[q]], S(j)[:, span[q]], ACT.Exp, bias=negmax[:, j % 2, q:q + 1], accum_out=total[:, j % 2, q:q + 1])
                ins.then_inc(exp_done, 1)

            def take_turned(it, s, j, first):
                n = it * NG + s
                act.wait_ge(turned, 4 * n + j + 1)
                if not (first and j < 2):
                    act.wait_ge(pv_done, 4 * n + j - 1)
                nc.scalar.copy(probsT[:, j % 2, :], TURN).then_inc(probsT_done, 1)

            def take_values(it, s, i):
                n = it * NG + s
                act.wait_ge(vproj_ready, 2 * n + i + 1)
                if not (isinstance(it, int) and it == 0 and s < 2):
                    act.wait_ge(pv_done, 4 * (n - 1))
                nc.scalar.copy(values[:, s % 2, 2 * i:2 * i + 2, :], PROJ(i).rearrange("p (t d) -> p t d", t=2)).then_inc(values_done, 1)

            def take_mixed(it, s, h, first):
                n = it * NG + s
                act.wait_ge(pv_done, 4 * n + 2 * h + 2)
                if not first:
                    act.wait_ge(out_ready, 2 * n)
                nc.scalar.copy(mixed[:, h, :], MIX).then_inc(mixed_done, 1)

            def pair(it, first, last):
                for s in range(NG):
                    f = first and s == 0
                    nxt = (it, s + 1) if s + 1 < NG else (it + 1, 0)
                    more = not (last and s == NG - 1)
                    if s == NG - 1 and more:
                        split_hi(it + 1)
                    exps(it, s, 0, f)
                    exps(it, s, 1, f)
                    take_turned(it, s, 0, f)
                    exps(it, s, 2, f)
                    take_turned(it, s, 1, f)
                    exps(it, s, 3, f)
                    take_mixed(it, s, 0, f)
                    take_turned(it, s, 2, f)
                    if more:
                        take_values(*nxt, 0)
                    take_turned(it, s, 3, f)
                    take_mixed(it, s, 1, f)
                    if more:
                        take_values(*nxt, 1)

            split_hi(0)
            take_values(0, 0, 0)
            take_values(0, 0, 1)
            pair(0, True, False)
            with act.Fori(1, HP - 1) as it:
                pair(it, False, False)
            pair(HP - 1, False, True)

        @block.vector
        def _(dve):
            def split_lo(it):
                dve.wait_ge(w_hi, it + 1)
                nc.vector.tensor_tensor(wl[:].rearrange("p a k d -> p (a k d)"), stage[:].rearrange("p a k d -> p (a k d)"), wh[:].rearrange("p a k d -> p (a k d)").bitcast(F32), ALU.subtract).then_inc(w_lo, 1)

            def rope(it, s, i, first=False):
                n = it * NG + s
                dve.wait_ge(proj_ready, 4 * n + i + 1)
                if not (first and i < 2):
                    dve.wait_ge(rotated, 4 * n + i - 1)
                rope_b(nc, c, PROJ(i), qk[:, s % 2, i, :], swapped[:, i % 2, :]).then_inc(rope_read, 1)

            def row_max(it, s, j):
                dve.wait_ge(scores_ready, 4 * (it * NG + s) + j + 1)
                for q in range(2):
                    ins = nc.vector.tensor_reduce(negmax[:, j % 2, q:q + 1], S(j)[:, span[q]], AX, ALU.max, negate=True)
                ins.then_inc(maxed, 1)

            def scale(it, s, j):
                g = 4 * (it * NG + s) + j
                dve.wait_ge(exp_done, g + 1)
                nc.vector.reciprocal(inv[:, j % 2, :], total[:, j % 2, :]).then_inc(inv_done, 1)
                dve.wait_ge(inv_done, g + 1)
                for q in range(2):
                    ins = nc.vector.tensor_scalar(probs[:, j % 2, span[q]], probs[:, j % 2, span[q]], inv[:, j % 2, q:q + 1], None, ALU.mult)
                ins.then_inc(scaled, 1)

            def add_out(it, s):
                for i in range(2):
                    dve.wait_ge(out_ready, 2 * (it * NG + s) + i + 1)
                    t = s * TG + 2 * i
                    nc.vector.tensor_tensor(c.x[:, t:t + 2, :], OUT(i).rearrange("p (t d) -> p t d", d=D), c.x[:, t:t + 2, :], ALU.add).then_inc(out_added, 1)

            def pair(it, first, last):
                for s in range(NG):
                    nxt = (it, s + 1) if s + 1 < NG else (it + 1, 0)
                    more = not (last and s == NG - 1)
                    if s == NG - 1 and more:
                        split_lo(it + 1)
                    row_max(it, s, 0)
                    row_max(it, s, 1)
                    if not (first and s == 0):
                        add_out(*((it, s - 1) if s else (it - 1, NG - 1)))
                    scale(it, s, 0)
                    scale(it, s, 1)
                    if more:
                        rope(*nxt, 0)
                    row_max(it, s, 2)
                    if more:
                        rope(*nxt, 1)
                    scale(it, s, 2)
                    if more:
                        rope(*nxt, 2)
                    row_max(it, s, 3)
                    scale(it, s, 3)
                    if more:
                        rope(*nxt, 3)

            split_lo(0)
            for i in range(4):
                rope(0, 0, i, True)
            pair(0, True, False)
            with dve.Fori(1, HP - 1) as it:
                pair(it, False, False)
            pair(HP - 1, False, True)
            add_out(HP - 1, NG - 1)

        @block.gpsimd
        def _(pool):
            with pool.Fori(0, HP) as it:
                for s in range(NG):
                    for i in range(4):
                        pool.wait_ge(rope_read, 4 * (it * NG + s) + i + 1)
                        q = qk[:, s % 2, i, :]
                        nc.gpsimd.tensor_tensor(q, q, swapped[:, i % 2, :], ALU.add).then_inc(rotated, 1)


def router(nc, c, name):
    with ExitStack() as ctx:
        sem = lambda n: ctx.enter_context(nc.semaphore(f"{name}_{n}"))
        sb = lambda n, s, d=F32: ctx.enter_context(nc.sbuf_tensor(f"{name}_{n}", s, d))
        z, inh, dist, near, far = (sb(n, [P, NT, E]) for n in ("z", "inh", "dist", "near", "far"))
        lo_side, hi_side, top, part = (sb(n, [P, NT, E]) for n in ("lo_side", "hi_side", "top", "part"))
        greater, equal = sb("greater", [P, NT, E, E]), sb("equal", [P, NT, E, E])
        wsum, none, some = sb("wsum", [P, NT]), sb("none", [P, NT]), sb("some", [P, NT])
        logits_ready, chained, exp_done = sem("logits_ready"), sem("chained"), sem("exp_done")
        block = ctx.enter_context(nc.Block())
        per = 4
        W2 = P

        @block.tensor
        def _(pe):
            for t in range(NT):
                tok = slice(t * P, (t + 1) * P)
                out = c.ps[:, t // 2, (t % 2) * 256:(t % 2) * 256 + 256]
                for k in range(KD):
                    nc.tensor.matmul(out, c.xl[:, k, tok], c.wr[:, k, :], start=(k == 0), stop=False)
                    ins = nc.tensor.matmul(out, c.xh[:, k, tok], c.wr[:, k, :], start=False, stop=(k == KD - 1))
            ins.then_inc(logits_ready, 1)

        @block.scalar
        def _(act):
            act.wait_ge(chained, 3)
            nc.scalar.activation(inh[:], z[:], ACT.Exp, scale=-1.0).then_inc(exp_done, 1)
            act.wait_ge(chained, 7)
            nc.scalar.activation(near[:], dist[:], ACT.Exp, scale=-1.0 / 0.1)
            nc.scalar.activation(far[:], dist[:], ACT.Exp, scale=-1.0 / 0.3).then_inc(exp_done, 1)

        @block.vector
        def _(dve):
            done = [0]

            def step(ins):
                done[0] += 1
                ins.then_inc(chained, 1)
                dve.wait_ge(chained, done[0])

            v = nc.vector
            row = lambda ap: ap[:].unsqueeze(2).to_broadcast([P, NT, E])
            dve.wait_ge(logits_ready, 1)
            logits = c.ps[:].rearrange("p b (i w) -> p (b i) w", w=256)
            step(v.tensor_copy(z[:], logits[:, :, 0:E]))
            step(v.tensor_tensor(z[:], logits[:, :, E:2 * E], z[:], ALU.add))
            step(v.tensor_scalar(z[:], z[:], c.inv_temperature[:, 0:1], None, ALU.mult))
            dve.wait_ge(exp_done, 1)
            step(v.tensor_scalar(inh[:], inh[:], 1.0, None, ALU.add))
            step(v.reciprocal(inh[:], inh[:]))
            step(v.tensor_scalar(inh[:], inh[:], GOLDEN_CENTER, None, ALU.subtract))
            step(v.scalar_tensor_tensor(out=dist[:], in0=inh[:], scalar=-1.0, in1=inh[:], op0=ALU.mult, op1=ALU.max))
            step(v.tensor_scalar(lo_side[:], z[:], LOGIT_LOWER, None, ALU.is_ge))
            step(v.tensor_scalar(hi_side[:], z[:], 0.0, None, ALU.is_le))
            step(v.tensor_tensor(lo_side[:], lo_side[:], hi_side[:], ALU.mult))
            dve.wait_ge(exp_done, 2)
            step(v.tensor_tensor(near[:], near[:], lo_side[:], ALU.mult))
            step(v.tensor_reduce(wsum[:], near[:], AX, ALU.add))
            step(v.tensor_scalar(none[:], wsum[:], 1e-8, None, ALU.is_lt))
            mine = far[:].unsqueeze(3).to_broadcast([P, NT, E, E])
            other = far[:].unsqueeze(2).to_broadcast([P, NT, E, E])
            for t in range(NT):
                ins = v.tensor_tensor(greater[:, t], far[:, t].unsqueeze(1).to_broadcast([P, E, E]), far[:, t].unsqueeze(2).to_broadcast([P, E, E]), ALU.is_gt)
            step(ins)
            for t in range(NT):
                ins = v.tensor_tensor(equal[:, t], far[:, t].unsqueeze(1).to_broadcast([P, E, E]), far[:, t].unsqueeze(2).to_broadcast([P, E, E]), ALU.is_equal)
            step(ins)
            step(v.tensor_tensor(equal[:].rearrange("p t e f -> p t (e f)"), equal[:].rearrange("p t e f -> p t (e f)"),
                                 c.before[:].unsqueeze(1).to_broadcast([P, NT, E * E]), ALU.mult))
            step(v.tensor_tensor(greater[:], greater[:], equal[:], ALU.add))
            step(v.tensor_reduce(top[:], greater[:], AX, ALU.add))
            step(v.tensor_scalar(top[:], top[:], 2.0, None, ALU.is_lt))
            step(v.tensor_tensor(part[:], far[:], top[:], ALU.mult))
            step(v.tensor_reduce(some[:], part[:], AX, ALU.add))
            step(v.tensor_scalar(some[:], some[:], 1e-8, None, ALU.max))
            step(v.reciprocal(some[:], some[:]))
            step(v.tensor_tensor(part[:], part[:], row(some), ALU.mult))
            step(v.tensor_tensor(part[:], part[:], row(none), ALU.mult))
            step(v.tensor_scalar(none[:], none[:], -1.0, 1.0, ALU.mult, ALU.add))
            step(v.tensor_tensor(near[:], near[:], row(none), ALU.mult))
            step(v.tensor_tensor(near[:], near[:], part[:], ALU.add))
            step(v.tensor_reduce(wsum[:], near[:], AX, ALU.add))
            step(v.tensor_scalar(wsum[:], wsum[:], 1e-8, None, ALU.max))
            step(v.reciprocal(wsum[:], wsum[:]))
            step(v.tensor_tensor(c.gate[:], near[:], row(wsum), ALU.mult))


def experts(nc, c, name, weights):
    with ExitStack() as ctx:
        sem = lambda n: ctx.enter_context(nc.semaphore(f"{name}_{n}"))
        sb = lambda n, s, d=F32: ctx.enter_context(nc.sbuf_tensor(f"{name}_{n}", s, d))
        stage = sb("stage", [P, 2, 3, KD, F])
        wh, wl = sb("wh", [P, 2, 3, KD, F], F32R), sb("wl", [P, 2, 3, KD, F], F32R)
        col = sb("col", [P, 2, NT])
        silu, hidden = sb("silu", [P, 2, G]), sb("hidden", [P, 2, G])
        hh, hl = sb("hh", [P, 2, 2, G], F32R), sb("hl", [P, 2, 2, G], F32R)
        stage_in = [sem("stage_in_even"), sem("stage_in_odd")]
        w_hi, w_lo, col_done = sem("w_hi"), sem("w_lo"), sem("col_done")
        gated, silu_done, hid_done, hi_done, lo_done = sem("gated"), sem("silu_done"), sem("hid_done"), sem("hi_done"), sem("lo_done")
        out_ready, out_added = sem("out_ready"), sem("out_added")
        GATE = lambda m: c.ps[:, 2 * m, :]
        UP = lambda m: c.ps[:, 2 * m + 1, :]
        OUT = lambda i: c.ps[:, 4 + i, :]
        TURNS = E // 2
        block = ctx.enter_context(nc.Block())
        flat = lambda w, e: w[:, e].rearrange("p a k d -> p (a k d)")


        @block.sync
        def _(sp):
            for e in range(2):
                sp.dma_start(stage[:, e], weights[e]).then_inc(stage_in[e], 16)
            with sp.Fori(1, TURNS) as it:
                for e in range(2):
                    sp.wait_ge(w_lo, 2 * it - 1 + e)
                    sp.dma_start(stage[:, e], weights[bass.ds(2 * it + e, 1)].squeeze(0)).then_inc(stage_in[e], 16)

        @block.tensor
        def _(pe):
            def gate_up(it, e, s, first=False):
                n = 8 * it + 4 * e + s
                if s == 0:
                    pe.wait_ge(w_lo, 2 * it + e + 1)
                g = slice(s * G, (s + 1) * G)
                for m in range(2):
                    if not first:
                        pe.wait_ge(hid_done, 2 * n + m - 1)
                    f = slice(m * P, (m + 1) * P)
                    for a, out in ((0, GATE(m)), (1, UP(m))):
                        for k in range(KD):
                            ins = matmul3(nc, out, (wh[:, e, a, k, f], wl[:, e, a, k, f]), (c.xh[:, k, g], c.xl[:, k, g]), k == 0, k == KD - 1)
                        ins.then_inc(gated, 1)

            def down(it, e, s, first=False):
                n = 8 * it + 4 * e + s
                pe.wait_ge(lo_done, 2 * n + 2)
                for t in range(TG):
                    if not (first and t < 4):
                        pe.wait_ge(out_added, 4 * n + t - 3)
                    tok = slice(t * P, (t + 1) * P)
                    for k in range(KD):
                        ins = matmul3(nc, OUT(t)[:, 0:D], (hh[:, s % 2, k, tok], hl[:, s % 2, k, tok]), (wh[:, e, 2, k, :], wl[:, e, 2, k, :]), k == 0, k == KD - 1)
                    ins.then_inc(out_ready, 1)

            def turn(it, first, last):
                for e in range(2):
                    for s in range(NG):
                        nxt = (it, e, s + 1) if s + 1 < NG else (it, 1, 0) if e == 0 else (it + 1, 0, 0)
                        if not (last and e == 1 and s == NG - 1):
                            gate_up(*nxt)
                        down(it, e, s, first and e == 0 and s == 0)

            gate_up(0, 0, 0, True)
            turn(0, True, False)
            with pe.Fori(1, TURNS - 1) as it:
                turn(it, False, False)
            turn(TURNS - 1, False, True)

        @block.scalar
        def _(act):
            def split_hi(it, e):
                act.wait_ge(stage_in[e], 16 * (it + 1))
                if not (isinstance(it, int) and it == 0):
                    act.wait_ge(out_ready, 4 * (8 * it + 4 * e - 4))
                nc.scalar.copy(flat(wh, e), flat(stage, e)).then_inc(w_hi, 1)

            def activate(it, e, s, m):
                n = 8 * it + 4 * e + s
                act.wait_ge(gated, 4 * n + 2 * m + 1)
                if not (isinstance(it, int) and it == 0 and e == 0 and s == 0):
                    act.wait_ge(hid_done, 2 * n + m - 1)
                nc.scalar.activation(silu[:, m, :], GATE(m), ACT.Silu).then_inc(silu_done, 1)

            def hidden_hi(it, e, s, m):
                n = 8 * it + 4 * e + s
                act.wait_ge(hid_done, 2 * n + m + 1)
                if not (isinstance(it, int) and it == 0 and e == 0 and s < 2):
                    act.wait_ge(out_ready, 4 * (n - 1))
                nc.scalar.copy(hh[:, s % 2, m, :], hidden[:, m, :]).then_inc(hi_done, 1)

            def turn(it, last):
                for e in range(2):
                    for s in range(NG):
                        activate(it, e, s, 0)
                        activate(it, e, s, 1)
                        hidden_hi(it, e, s, 0)
                        hidden_hi(it, e, s, 1)
                        if s == 1 and not (last and e == 1):
                            split_hi(*((it, 1) if e == 0 else (it + 1, 0)))

            split_hi(0, 0)
            turn(0, False)
            with act.Fori(1, TURNS - 1) as it:
                turn(it, False)
            turn(TURNS - 1, True)

        @block.vector
        def _(dve):
            def split_lo(it, e):
                dve.wait_ge(w_hi, 2 * it + e + 1)
                nc.vector.tensor_tensor(flat(wl, e), flat(stage, e), flat(wh, e).bitcast(F32), ALU.subtract).then_inc(w_lo, 1)

            def hidden_rows(it, e, s, m):
                n = 8 * it + 4 * e + s
                dve.wait_ge(gated, 4 * n + 2 * m + 2)
                dve.wait_ge(silu_done, 2 * n + m + 1)
                if not (isinstance(it, int) and it == 0 and e == 0 and s == 0):
                    dve.wait_ge(lo_done, 2 * n + m - 1)
                nc.vector.tensor_tensor(hidden[:, m, :], UP(m), silu[:, m, :], ALU.mult).then_inc(hid_done, 1)

            def hidden_lo(it, e, s, m):
                n = 8 * it + 4 * e + s
                dve.wait_ge(hi_done, 2 * n + m + 1)
                nc.vector.tensor_tensor(hl[:, s % 2, m, :], hidden[:, m, :], hh[:, s % 2, m, :].bitcast(F32), ALU.subtract).then_inc(lo_done, 1)

            def add_out(it, e, s):
                n = 8 * it + 4 * e + s
                if s == 0:
                    dve.wait_ge(col_done, 2 * it + e + 1)
                for t in range(TG):
                    dve.wait_ge(out_ready, 4 * n + t + 1)
                    i = s * TG + t
                    nc.vector.scalar_tensor_tensor(out=c.x[:, i, :], in0=OUT(t)[:, 0:D], scalar=col[:, e, i:i + 1], in1=c.x[:, i, :], op0=ALU.mult, op1=ALU.add).then_inc(out_added, 1)

            def turn(it, first, last):
                for e in range(2):
                    for s in range(NG):
                        hidden_rows(it, e, s, 0)
                        hidden_rows(it, e, s, 1)
                        hidden_lo(it, e, s, 0)
                        hidden_lo(it, e, s, 1)
                        if s == 1 and not (last and e == 1):
                            split_lo(*((it, 1) if e == 0 else (it + 1, 0)))
                        if not (first and e == 0 and s == 0):
                            add_out(*((it, e, s - 1) if s else (it, 0, NG - 1) if e == 1 else (it - 1, 1, NG - 1)))
                        if s == 0:
                            ex = 2 * it + e
                            nc.vector.tensor_copy(col[:, e, :].unsqueeze(2), c.gate[:, :, ex:ex + 1] if isinstance(ex, int) else c.gate[:, :, bass.ds(ex, 1)]).then_inc(col_done, 1)

            split_lo(0, 0)
            turn(0, True, False)
            with dve.Fori(1, TURNS - 1) as it:
                turn(it, False, False)
            turn(TURNS - 1, False, True)
            add_out(TURNS - 1, 1, NG - 1)


def load(nc, c, x, const, small, temperature, before):
    with ExitStack() as ctx:
        small_in = ctx.enter_context(nc.sbuf_tensor("small_in", [P, KD, S_COLS], F32))
        loaded, const_in, hi_done, wr_done = (ctx.enter_context(nc.semaphore(n)) for n in ("loaded", "const_in", "small_hi", "wr_zero"))
        block = ctx.enter_context(nc.Block())

        @block.sync
        def _(sp):
            sp.dma_start(small_in[:], small).then_inc(loaded, 16)
            sp.dma_start(c.const[:], const).then_inc(loaded, 16)
            sp.dma_start(c.before[:], before.to_broadcast([P, E * E])).then_inc(loaded, 16)
            sp.dma_start(c.temperature[:], temperature.to_broadcast([P, 1])).then_inc(loaded, 16)
            sp.dma_start(c.x[:], x.rearrange("(t p) d -> p t d", p=P)).then_inc(const_in, 16)
            sp.wait_ge(const_in, 16)

        @block.scalar
        def _(act):
            act.wait_ge(loaded, 64)
            act.wait_ge(wr_done, 1)
            nc.scalar.copy(c.sh[:], small_in[:, :, 0:S_WR])
            nc.scalar.copy(c.wr[:, :, 0:E], small_in[:, :, S_WR:S_WR + E]).then_inc(hi_done, 1)
            nc.scalar.copy(c.ident16[:], c.const[:, C_IDENT:C_IDENT + P])
            nc.scalar.copy(c.mask16[:], c.const[:, C_MASK:C_MASK + P])

        @block.vector
        def _(dve):
            nc.vector.memset(c.wr[:].bitcast(F32), 0.0).then_inc(wr_done, 1)
            dve.wait_ge(hi_done, 1)
            nc.vector.reciprocal(c.inv_temperature[:], c.temperature[:])
            nc.vector.tensor_tensor(c.sl[:], small_in[:, :, 0:S_WR], c.sh[:].bitcast(F32), ALU.subtract)
            nc.vector.tensor_tensor(c.wr[:, :, E:2 * E], small_in[:, :, S_WR:S_WR + E], c.wr[:, :, 0:E].bitcast(F32), ALU.subtract)


def store(nc, c, out):
    with ExitStack() as ctx:
        stored = ctx.enter_context(nc.semaphore("stored"))
        block = ctx.enter_context(nc.Block())

        @block.sync
        def _(sp):
            sp.dma_start(out.rearrange("(t p) d -> p t d", p=P), c.x[:]).then_inc(stored, 16)
            sp.wait_ge(stored, 16)


def hybrid_kernel(nc, x, const, before, small, temperature, wa, wb_qkv, wb_out, wf, out):
    with ExitStack() as ctx:
        sb = lambda n, s, d=F32: ctx.enter_context(nc.sbuf_tensor(n, s, d))
        c = Core()
        c.x = sb("x", [P, NT, D])
        c.xh, c.xl = sb("xh", [P, KD, N], F32R), sb("xl", [P, KD, N], F32R)
        c.const = sb("const", [P, C_COLS])
        c.ident = c.const[:, C_IDENT:C_IDENT + P]
        c.ident16, c.mask16 = sb("ident16", [P, P], BF16), sb("mask16", [P, P], BF16)
        c.before = sb("before", [P, E * E])
        c.temperature, c.inv_temperature = sb("temperature", [P, 1]), sb("inv_temperature", [P, 1])
        c.sh, c.sl = sb("sh", [P, KD, S_WR], F32R), sb("sl", [P, KD, S_WR], F32R)
        c.wr = sb("wr", [P, KD, 256], F32R)
        c.gate = sb("gate", [P, NT, E])
        c.ps = ctx.enter_context(nc.psum_tensor("ps", [P, 8, 512], F32))

        load(nc, c, x, const, small, temperature, before)
        layer_norm(nc, c, "ln1")
        with ExitStack() as inner:
            sa = lambda n, s, d=F32: inner.enter_context(nc.sbuf_tensor(n, s, d))
            a = Core()
            a.q1h, a.q1l, a.q2 = sa("q1h", [P, N], F32R), sa("q1l", [P, N], F32R), sa("q2", [P, N], F32R)
            a.keys = sa("keys", [P, N])
            a.values = sa("values", [P, NT, KVR])
            latents(nc, c, "lat", a)
            attention_a(nc, c, "aa", a, wa)
        layer_norm(nc, c, "ln2")
        router(nc, c, "r1")
        experts(nc, c, "f1", wf)
        layer_norm(nc, c, "ln3")
        attention_b(nc, c, "ab", wb_qkv, wb_out)
        layer_norm(nc, c, "ln4")
        router(nc, c, "r2")
        experts(nc, c, "f2", wf)
        store(nc, c, out)


def constants():
    const = np.zeros((P, C_COLS), np.float32)
    pos = np.arange(T, dtype=np.float32)
    theta = (1.0 / np.float32(10000.0) ** (np.arange(0, ROT, 2, dtype=np.float32) / ROT)).astype(np.float32)
    ang = (pos[None, :] * theta[:, None]).astype(np.float32)
    const[0:64, C_COSA:C_COSA + T] = 1.0
    const[64:96, C_COSA:C_COSA + T] = np.cos(ang)
    const[96:128, C_COSA:C_COSA + T] = np.cos(ang)
    const[96:128, C_SINA:C_SINA + T] = -np.sin(ang)
    const[64:96, C_SINA:C_SINA + T] = np.sin(ang)
    half = 64
    freqs = np.power(np.float32(10000.0), -np.arange(half, dtype=np.float32) / half).astype(np.float32)
    rad = (pos[None, :] * freqs[:, None]).astype(np.float32)
    mult = np.float32((1.0 / 128.0) ** 0.5)
    for r in (0, 64):
        const[r:r + 64, C_COSB:C_COSB + T] = np.cos(rad) * mult
    const[64:128, C_SINB:C_SINB + T] = -np.sin(rad) * mult
    const[0:64, C_SINB:C_SINB + T] = np.sin(rad) * mult
    const[:, C_IDENT:C_IDENT + P] = np.eye(P, dtype=np.float32)
    const[:, C_MASK:C_MASK + P] = np.triu(np.full((P, P), -1e30, np.float32), 1)
    e = np.arange(E)
    before = (e[None, :] < e[:, None]).astype(np.float32).reshape(1, E * E)
    return const, before


def kernel(**inputs):
    import numpy as _np
    import concourse.bacc as _bacc
    from concourse import mybir as _mybir
    from concourse.bass_utils import run_bass_kernel_spmd as _run

    w = {k: _np.asarray(v) for k, v in inputs.items()}
    const, before = constants()
    pairs = _np.concatenate([_np.arange(0, ROT, 2), _np.arange(1, ROT, 2)])

    qa = w["L0_attn_a_q_a_w"].T
    kva = w["L0_attn_a_kv_a_w"]
    kva = _np.concatenate([kva[:KVR], kva[KVR:][pairs]]).T
    small = _np.concatenate([qa, qa[:, P:QR], kva, w["L0_ffn_Wr"]], axis=1)
    small = _np.ascontiguousarray(small.reshape(KD, P, S_COLS).transpose(1, 0, 2))

    qb = w["L0_attn_a_q_b_w"].reshape(HP, 2, NOPE + ROT, QR)
    qpass = qb[:, :, :NOPE]
    qpass = _np.concatenate([qpass, qpass[..., P:QR]], axis=-1).reshape(HP, P, 256)
    qrot = qb[:, :, NOPE:][:, :, pairs].transpose(0, 3, 1, 2)
    qrot = _np.concatenate([qrot, qrot[:, P:QR]], axis=1).reshape(HP, 2, P, 2 * ROT).transpose(0, 2, 1, 3).reshape(HP, P, 4 * ROT)
    kvb = w["L0_attn_a_kv_b_w"].reshape(HP, 2, NOPE + VD, KVR)
    wk = kvb[:, :, :NOPE].reshape(HP, P, KVR)
    wv = kvb[:, :, NOPE:].transpose(0, 2, 1, 3).reshape(HP, P, 2 * KVR)
    ow = w["L0_attn_a_o_w"].T.reshape(HP, 2, VD, D).transpose(0, 2, 1, 3).reshape(HP, P, 2 * D)
    wa = _np.ascontiguousarray(_np.concatenate([qpass, wk, qrot, wv, ow], axis=2))

    qkv = _np.stack([w["L0_attn_b_wq"], w["L0_attn_b_wk"], w["L0_attn_b_wv"]])
    wb_qkv = _np.ascontiguousarray(qkv.reshape(3, KD, P, HP, 2 * P).transpose(3, 2, 0, 1, 4))
    wb_out = _np.ascontiguousarray(w["L0_attn_b_wo"].reshape(HP, 2, P, D).transpose(0, 2, 1, 3))

    wf = _np.stack([w["L0_ffn_Wg"], w["L0_ffn_Wu"], w["L0_ffn_Wd"]], axis=1)
    wf = _np.ascontiguousarray(wf.reshape(E, 3, KD, P, F).transpose(0, 3, 1, 2, 4))

    nc = _bacc.Bacc("TRN2", target_bir_lowering=False, num_devices=1)
    arrays = {
        "x_in": _np.ascontiguousarray(w["L0_attn_a_x"]).reshape(N, D),
        "const_in": const, "before_in": before, "small_weights": small,
        "temperature_in": w["L0_ffn_temperature"].reshape(1, 1),
        "wa_in": wa, "wb_qkv_in": wb_qkv, "wb_out_in": wb_out, "wf_in": wf,
    }
    args = [nc.dram_tensor(n, a.shape, _mybir.dt.from_np(a.dtype), kind="ExternalInput").ap() for n, a in arrays.items()]
    out = nc.dram_tensor("out_0", (N, D), _mybir.dt.float32, kind="ExternalOutput").ap()
    hybrid_kernel(nc, *args, out)
    r = _run(nc, [arrays], core_ids=[0])
    return r.results[0]["out_0"].reshape(B, T, D)
```

```python
from contextlib import ExitStack

import concourse.bass as bass
from concourse import mybir
import numpy as np

ALU = mybir.AluOpType
ACT = mybir.ActivationFunctionType
AX = mybir.AxisListType.X
F32 = mybir.dt.float32
F32R = mybir.dt.float32r
BF16 = mybir.dt.bfloat16

P = 128
B, T, D = 8, 256, 256
N = B * T
NT = N // P
KD = D // P
G = 512
NG = N // G
TG = G // P
BG = G // T
H = 16
HP = H // 2
QR, KVR, ROT, NOPE, VD = 192, 64, 64, 64, 128
E, F = 8, 256
EPS = 1e-5
GOLDEN_CENTER = 1.0 / np.e
GOLDEN_LOWER = 0.5 - np.log(4.0 / 3.0)
LOGIT_LOWER = float(np.log(GOLDEN_LOWER / (1.0 - GOLDEN_LOWER)))

A_PASS, A_K, A_ROT, A_V, A_O = 0, 256, 320, 576, 704
A_COLS = 1216
C_COSA, C_SINA, C_COSB, C_SINB, C_IDENT, C_MASK = 0, 256, 512, 768, 1024, 1152
C_COLS = 1280
S_QA, S_KVA, S_WR = 0, 256, 384
S_COLS = 392


class Core:
    pass


def layer_norm(nc, c, name, prepare=None):
    with ExitStack() as ctx:
        sem = lambda n: ctx.enter_context(nc.semaphore(f"{name}_{n}"))
        sb = lambda n, s, d=F32: ctx.enter_context(nc.sbuf_tensor(f"{name}_{n}", s, d))
        moments = sb("moments", [P, NT, 6])
        meanvar = sb("meanvar", [P, NT, 2])
        shifted = sb("shifted", [P, NT])
        rstd = sb("rstd", [P, NT])
        minus_half = sb("minus_half", [P, NT])
        normed = sb("normed", [P, 2, TG, D])
        stats_done, var_done, rstd_done = sem("stats_done"), sem("var_done"), sem("rstd_done")
        half_set, normed_done, turned = sem("half_set"), sem("normed_done"), sem("turned")
        hi_done, lo_done = sem("hi_done"), sem("lo_done")

        def bank(g, k):
            return c.ps[:, 4 * (g % 2) + k, :]

        block = ctx.enter_context(nc.Block())

        def lo_parts(dve, g):
            for k in range(KD):
                dve.wait_ge(hi_done, KD * g + k + 1)
                s = slice(g * G, (g + 1) * G)
                nc.vector.tensor_tensor(c.xl[:, k, s], bank(g, k), c.xh[:, k, s].bitcast(F32), ALU.subtract).then_inc(lo_done, 1)

        @block.gpsimd
        def _(pool):
            nc.gpsimd.memset(minus_half[:], -0.5).then_inc(half_set, 1)
            pool.wait_ge(half_set, 1)
            for g in range(NG):
                t = slice(g * TG, (g + 1) * TG)
                pool.wait_ge(var_done, g + 1)
                nc.gpsimd.tensor_tensor(rstd[:, t], shifted[:, t], minus_half[:, t], ALU.pow).then_inc(rstd_done, 1)

        @block.vector
        def _(dve):
            stats = 0
            for g in range(NG):
                for t in range(g * TG, (g + 1) * TG):
                    nc.vector.bn_stats(moments[:, t, :], c.x[:, t, :]).then_inc(stats_done, 1)
                stats += TG
                dve.wait_ge(stats_done, stats)
                for t in range(g * TG, (g + 1) * TG):
                    nc.vector.bn_aggr(meanvar[:, t, :], moments[:, t, :]).then_inc(stats_done, 1)
                stats += TG
                dve.wait_ge(stats_done, stats)
                t = slice(g * TG, (g + 1) * TG)
                nc.vector.tensor_scalar(shifted[:, t], meanvar[:, t, 1], EPS, None, ALU.add).then_inc(var_done, 1)

            for g in range(NG):
                dve.wait_ge(rstd_done, g + 1)
                if g >= 2:
                    dve.wait_ge(turned, KD * (g - 1))
                for i in range(TG):
                    t = g * TG + i
                    ins = nc.vector.tensor_scalar(normed[:, g % 2, i, :], c.x[:, t, :], meanvar[:, t, 0:1], rstd[:, t:t + 1], ALU.subtract, ALU.mult)
                ins.then_inc(normed_done, 1)
                if g >= 1:
                    lo_parts(dve, g - 1)
            lo_parts(dve, NG - 1)

        @block.tensor
        def _(pe):
            for g in range(NG):
                pe.wait_ge(normed_done, g + 1)
                if g >= 2:
                    pe.wait_ge(lo_done, KD * (g - 1))
                for k in range(KD):
                    for i in range(TG):
                        ins = nc.tensor.transpose(bank(g, k)[:, i * P:(i + 1) * P], normed[:, g % 2, i, k * P:(k + 1) * P], c.ident)
                    ins.then_inc(turned, 1)

        @block.scalar
        def _(act):
            for g in range(NG):
                for k in range(KD):
                    act.wait_ge(turned, KD * g + k + 1)
                    nc.scalar.copy(c.xh[:, k, g * G:(g + 1) * G], bank(g, k)).then_inc(hi_done, 1)


def matmul3(nc, out, left, right, start, stop):
    (lh, ll), (rh, rl) = left, right
    nc.tensor.matmul(out, ll, rh, start=start, stop=False)
    nc.tensor.matmul(out, lh, rl, start=False, stop=False)
    return nc.tensor.matmul(out, lh, rh, start=False, stop=stop)


def latents(nc, c, name, a):
    with ExitStack() as ctx:
        sem = lambda n: ctx.enter_context(nc.semaphore(f"{name}_{n}"))
        sb = lambda n, s, d=F32: ctx.enter_context(nc.sbuf_tensor(f"{name}_{n}", s, d))
        swapped = sb("swapped", [P, 2, G])
        proj_ready, hi_done, lo_done = sem("proj_ready"), sem("hi_done"), sem("lo_done")
        rope_read, rotated, turned, values_done = sem("rope_read"), sem("rotated"), sem("turned"), sem("values_done")
        keys_hi, swap_done, sin_done = sem("keys_hi"), sem("swap_done"), sem("sin_done")
        block = ctx.enter_context(nc.Block())

        def slot(g):
            return slice(g * G, (g + 1) * G)

        @block.tensor
        def _(pe):
            for g in range(NG):
                for m in range(3):
                    if g >= 2 and m < 2:
                        pe.wait_ge(lo_done, 2 * (g - 2) + m + 1)
                    if g >= 2 and m == 2:
                        pe.wait_ge(rope_read, g - 1)
                        pe.wait_ge(swap_done, g - 1)
                    out = c.ps[:, 3 * (g % 2) + m, :]
                    col = slice(m * P, (m + 1) * P)
                    for k in range(KD):
                        ins = matmul3(nc, out, (c.sh[:, k, col], c.sl[:, k, col]), (c.xh[:, k, slot(g)], c.xl[:, k, slot(g)]), k == 0, k == KD - 1)
                    ins.then_inc(proj_ready, 1)
            for g in range(NG):
                pe.wait_ge(rope_read, g + 1)
                for i in range(TG):
                    t = g * TG + i
                    ins = nc.tensor.transpose(c.ps[:, 6 + g % 2, i * KVR:(i + 1) * KVR], a.keys[0:KVR, t * P:(t + 1) * P], c.ident[0:KVR, 0:KVR])
                ins.then_inc(turned, 1)
                if g + 2 < NG + 1 and g >= 1:
                    pe.wait_ge(values_done, g)

        @block.scalar
        def _(act):
            for g in range(NG):
                act.wait_ge(proj_ready, 3 * g + 1)
                nc.scalar.copy(a.q1h[:, slot(g)], c.ps[:, 3 * (g % 2), :]).then_inc(hi_done, 1)
                act.wait_ge(proj_ready, 3 * g + 2)
                nc.scalar.copy(a.q2[:, slot(g)], c.ps[:, 3 * (g % 2) + 1, :]).then_inc(hi_done, 1)
                act.wait_ge(rope_read, g + 1)
                if g >= 2:
                    act.wait_ge(rotated, g - 1)
                swap_a(nc, c.ps[:, 3 * (g % 2) + 2, :], swapped[:, g % 2, :]).then_inc(swap_done, 1)
            for g in range(NG):
                act.wait_ge(rotated, g + 1)
                nc.scalar.copy(a.kh[:, slot(g)], a.keys[:, slot(g)]).then_inc(keys_hi, 1)
                act.wait_ge(turned, g + 1)
                nc.scalar.copy(a.values[:, g * TG:(g + 1) * TG, :], c.ps[:, 6 + g % 2, 0:TG * KVR].rearrange("p (t d) -> p t d", d=KVR)).then_inc(values_done, 1)

        @block.vector
        def _(dve):
            for g in range(NG):
                dve.wait_ge(hi_done, 2 * g + 1)
                nc.vector.tensor_tensor(a.q1l[:, slot(g)], c.ps[:, 3 * (g % 2), :], a.q1h[:, slot(g)].bitcast(F32), ALU.subtract).then_inc(lo_done, 1)
                dve.wait_ge(hi_done, 2 * g + 2)
                nc.vector.tensor_tensor(a.q2[64:128, slot(g)], c.ps[64:128, 3 * (g % 2) + 1, :], a.q2[64:128, slot(g)].bitcast(F32), ALU.subtract).then_inc(lo_done, 1)
                dve.wait_ge(proj_ready, 3 * g + 3)
                times_table(nc.vector, c, a.keys[:, slot(g)], c.ps[:, 3 * (g % 2) + 2, :], ALL_ROWS, C_COSA).then_inc(rope_read, 1)

        @block.gpsimd
        def _(pool):
            for g in range(NG):
                pool.wait_ge(swap_done, g + 1)
                rows = swapped[64:128, g % 2, :]
                times_table(nc.gpsimd, c, rows, rows, ROT_ROWS, C_SINA).then_inc(sin_done, 1)
                pool.wait_ge(sin_done, g + 1)
                pool.wait_ge(rope_read, g + 1)
                nc.gpsimd.tensor_tensor(a.keys[64:128, slot(g)], a.keys[64:128, slot(g)], swapped[64:128, g % 2, :], ALU.add).then_inc(rotated, 1)
            pool.wait_ge(rotated, NG)
            for g in range(NG):
                pool.wait_ge(keys_hi, g + 1)
                nc.gpsimd.tensor_tensor(a.kl[:, slot(g)], a.keys[:, slot(g)], a.kh[:, slot(g)].bitcast(F32), ALU.subtract)


ALL_ROWS, ROT_ROWS = slice(0, P), slice(64, P)


def by_batch(ap):
    return ap.rearrange("p (b t) -> p b t", t=T)


def table(c, rows, col):
    return c.const[rows, col:col + T].unsqueeze(1).to_broadcast([rows.stop - rows.start, BG, T])


def swap_a(nc, src, swapped):
    nc.scalar.copy(swapped[64:96], src[96:128])
    return nc.scalar.copy(swapped[96:128], src[64:96])


def swap_b(nc, src, swapped):
    nc.scalar.copy(swapped[0:64], src[64:128])
    return nc.scalar.copy(swapped[64:128], src[0:64])


def times_table(engine, c, out, src, rows, col):
    return engine.tensor_tensor(by_batch(out), by_batch(src), table(c, rows, col), ALU.mult)


def after(engine, semaphore, count):
    if not isinstance(count, int) or count > 0:
        engine.wait_ge(semaphore, count)


PAIRS = 4


def moved(it, s, j, by):
    at = PAIRS * s + j + by
    return it + at // (PAIRS * NG), at // PAIRS % NG, at % PAIRS


def attention_a(nc, c, name, a, weights):
    with ExitStack() as ctx:
        sem = lambda n: ctx.enter_context(nc.semaphore(f"{name}_{n}"))
        sb = lambda n, s, d=F32: ctx.enter_context(nc.sbuf_tensor(f"{name}_{n}", s, d))
        stage = sb("stage", [P, A_COLS])
        wh, wl = sb("wh", [P, 2, 2, P], F32R), sb("wl", [P, 2, 2, P], F32R)
        woh, wol = sb("woh", [P, D], F32R), sb("wol", [P, D], F32R)
        raw = sb("raw", [P, 2, G])
        qh, ql = sb("qh", [P, 2, 2, G], F32R), sb("ql", [P, 2, 2, G], F32R)
        swapped = sb("swapped", [P, 2, G])
        negmax, total, inv = (sb(n, [P, PAIRS, 2]) for n in ("negmax", "total", "inv"))
        probs = sb("probs", [P, PAIRS, 2, T])
        probsT = sb("probsT", [P, 2, 2, T])
        mh, ml = sb("mh", [P, 2, G], F32R), sb("ml", [P, 2, G], F32R)
        stage_in, fold_ready, fold_hi, fold_lo = sem("stage_in"), sem("fold_ready"), sem("fold_hi"), sem("fold_lo")
        wo_ready, wo_hi, wo_lo = sem("wo_ready"), sem("wo_hi"), sem("wo_lo")
        proj_ready, rope_read, rotated, q_hi, q_lo = sem("proj_ready"), sem("rope_read"), sem("rotated"), sem("q_hi"), sem("q_lo")
        scores_ready, maxed, exp_done, inv_done, scaled = sem("scores_ready"), sem("maxed"), sem("exp_done"), sem("inv_done"), sem("scaled")
        turned, probsT_done, pv_done, mix_hi, mix_lo = sem("turned"), sem("probsT_done"), sem("pv_done"), sem("mix_hi"), sem("mix_lo")
        out_ready, out_added, swap_done, sin_done = sem("out_ready"), sem("out_added"), sem("swap_done"), sem("sin_done")
        S = lambda j: c.ps[:, j % 2, :]
        TURN = c.ps[:, 2, :]
        PROJ = lambda h: c.ps[:, 3 + h, :]
        MIX = lambda s: c.ps[:, 5 + s % 2, :]
        OUT = c.ps[:, 7, :]
        fold = lambda h: PROJ(h)[:, 0:2 * KVR].rearrange("p (m d) -> p m d", m=2)
        folded_out = OUT[:, 0:D]
        rot = stage[:, A_ROT:A_ROT + 4 * ROT].rearrange("p (m h d) -> p m h d", m=2, h=2)
        LAST = (HP - 1, NG - 1, PAIRS - 1)
        slot_no = lambda it, s: it * NG + s
        pair_no = lambda it, s, j: (it * NG + s) * PAIRS + j
        block = ctx.enter_context(nc.Block())

        @block.sync
        def _(sp):
            sp.dma_start(stage[:], weights[0]).then_inc(stage_in, 16)
            with sp.Fori(1, HP) as it:
                sp.wait_ge(wo_ready, it)
                sp.dma_start(stage[:], weights[bass.ds(it, 1)].squeeze(0)).then_inc(stage_in, 16)

        @block.tensor
        def _(pe):
            def fold_query(it, h):
                if h == 0:
                    pe.wait_ge(stage_in, 16 * (it + 1))
                after(pe, rope_read, 2 * NG * it + h - 1)
                after(pe, swap_done, 2 * NG * it + h - 1)
                r = slice(64 * h, 64 * h + 64)
                for m in range(2):
                    ins = nc.tensor.matmul(PROJ(h)[:, m * KVR:(m + 1) * KVR], stage[r, A_PASS + m * P:A_PASS + (m + 1) * P], stage[r, A_K:A_K + KVR], start=True, stop=True)
                ins.then_inc(fold_ready, 1)

            def fold_output(it):
                after(pe, out_added, 2 * NG * it)
                for h in range(2):
                    ins = nc.tensor.matmul(folded_out[64 * h:64 * h + 64], stage[:, A_V + h * KVR:A_V + (h + 1) * KVR], stage[:, A_O + h * D:A_O + (h + 1) * D], start=True, stop=True)
                ins.then_inc(wo_ready, 1)

            def project(it, s, h):
                if s == 0:
                    pe.wait_ge(fold_lo, 2 * it + h + 1)
                after(pe, rope_read, 2 * slot_no(it, s) + h - 1)
                after(pe, swap_done, 2 * slot_no(it, s) + h - 1)
                g = slice(s * G, (s + 1) * G)
                out = PROJ(h)
                nc.tensor.matmul(out, wl[:, 0, h, :], a.q1h[:, g], start=True, stop=False)
                nc.tensor.matmul(out, wh[:, 0, h, :], a.q1l[:, g], start=False, stop=False)
                nc.tensor.matmul(out, wl[:, 1, h, :], a.q2[:, g], start=False, stop=False)
                nc.tensor.matmul(out, wh[:, 1, h, :], a.q2[:, g], start=False, stop=False)
                nc.tensor.matmul(out, wh[:, 0, h, :], a.q1h[:, g], start=False, stop=True).then_inc(proj_ready, 1)

            def scores(it, s, j):
                g = pair_no(it, s, j)
                h, b = j // 2, j % 2
                if b == 0:
                    pe.wait_ge(q_lo, 2 * slot_no(it, s) + h + 1)
                after(pe, exp_done, g - 1)
                keys = slice(s * G + b * T, s * G + (b + 1) * T)
                for q in range(2):
                    rows = slice(b * T + q * P, b * T + (q + 1) * P)
                    ins = matmul3(nc, S(j)[:, q * T:(q + 1) * T], (qh[:, s % 2, h, rows], ql[:, s % 2, h, rows]), (a.kh[:, keys], a.kl[:, keys]), True, True)
                ins.then_inc(scores_ready, 1)

            def turn(it, s, j):
                g = pair_no(it, s, j)
                pe.wait_ge(scaled, g + 1)
                after(pe, probsT_done, g)
                for q in range(2):
                    for k in range(2):
                        ins = nc.tensor.transpose(TURN[:, k * T + q * P:k * T + (q + 1) * P], probs[:, j, q, k * P:(k + 1) * P], c.ident)
                ins.then_inc(turned, 1)

            def mix(it, s, j):
                g = pair_no(it, s, j)
                h, b = j // 2, j % 2
                pe.wait_ge(probsT_done, g + 1)
                if j == 0:
                    after(pe, mix_lo, slot_no(it, s) - 1)
                for k in range(2):
                    ins = nc.tensor.matmul(MIX(s)[64 * h:64 * h + 64, b * T:(b + 1) * T], a.values[:, s * TG + b * 2 + k, :], probsT[:, j % 2, k, :], start=(k == 0), stop=(k == 1))
                ins.then_inc(pv_done, 1)

            def output(it, s, i):
                n = slot_no(it, s)
                if i == 0:
                    pe.wait_ge(mix_lo, n + 1)
                    if s == 0:
                        pe.wait_ge(wo_lo, it + 1)
                after(pe, out_added, 2 * n + i)
                for t in range(2):
                    tok = slice((2 * i + t) * P, (2 * i + t + 1) * P)
                    ins = matmul3(nc, OUT[:, t * D:(t + 1) * D], (mh[:, s % 2, tok], ml[:, s % 2, tok]), (woh[:], wol[:]), True, True)
                ins.then_inc(out_ready, 1)

            def step(it, s, j):
                first, last = it == 0 if isinstance(it, int) else False, it == HP - 1 if isinstance(it, int) else False
                if not (last and s == NG - 1 and j >= 2):
                    scores(*moved(it, s, j, 2))
                turn(it, s, j)
                if not (first and s == 0 and j == 0):
                    mix(*moved(it, s, j, -1))
                if j == 0 and not (first and s <= 1):
                    output(*moved(it, s, 0, -2 * PAIRS)[:2], 1)
                if j == 2 and not (first and s == 0):
                    output(*moved(it, s, 0, -PAIRS)[:2], 0)
                if s == 1 and j == 3 and not last:
                    fold_query(it + 1, 0)
                if j in (1, 3) and not (last and s >= NG - 2):
                    project(*moved(it, s, 0, 2 * PAIRS)[:2], j // 2)
                if s == 2 and j == 1 and not last:
                    fold_query(it + 1, 1)
                if s == 1 and j == 1:
                    fold_output(it)

            def head_pair(it):
                for s in range(NG):
                    for j in range(PAIRS):
                        step(it, s, j)

            fold_query(0, 0)
            fold_query(0, 1)
            project(0, 0, 0)
            project(0, 0, 1)
            project(0, 1, 0)
            project(0, 1, 1)
            scores(0, 0, 0)
            scores(0, 0, 1)
            head_pair(0)
            with pe.Fori(1, HP - 1) as it:
                head_pair(it)
            head_pair(HP - 1)
            mix(*LAST)
            output(HP - 1, NG - 2, 1)
            output(HP - 1, NG - 1, 0)
            output(HP - 1, NG - 1, 1)

        @block.scalar
        def _(act):
            def fold_query(it, h):
                act.wait_ge(fold_ready, 2 * it + h + 1)
                nc.scalar.copy(wh[:, :, h, 0:KVR], fold(h))
                nc.scalar.copy(wh[:, :, h, KVR:P], rot[:, :, h]).then_inc(fold_hi, 1)

            def fold_output(it):
                act.wait_ge(wo_ready, it + 1)
                nc.scalar.copy(woh[:], folded_out).then_inc(wo_hi, 1)

            def swap(it, s, h):
                m = 2 * slot_no(it, s) + h
                act.wait_ge(rope_read, m + 1)
                after(act, rotated, m - 1)
                swap_a(nc, PROJ(h), swapped[:, h, :]).then_inc(swap_done, 1)

            def query_hi(it, s, h):
                n = slot_no(it, s)
                act.wait_ge(rotated, 2 * n + h + 1)
                after(act, scores_ready, PAIRS * (n - 2) + 2 * h + 2)
                nc.scalar.copy(qh[:, s % 2, h, :], raw[:, h, :]).then_inc(q_hi, 1)

            def exps(it, s, j):
                g = pair_no(it, s, j)
                act.wait_ge(maxed, g + 1)
                after(act, turned, g - PAIRS + 1)
                for q in range(2):
                    ins = nc.scalar.activation(probs[:, j, q, :], S(j)[:, q * T:(q + 1) * T], ACT.Exp, bias=negmax[:, j, q:q + 1], accum_out=total[:, j, q:q + 1])
                ins.then_inc(exp_done, 1)

            def take_turned(it, s, j):
                g = pair_no(it, s, j)
                act.wait_ge(turned, g + 1)
                after(act, pv_done, g - 1)
                nc.scalar.copy(probsT[:, j % 2].rearrange("p k t -> p (k t)"), TURN).then_inc(probsT_done, 1)

            def mixed_hi(it, s):
                n = slot_no(it, s)
                act.wait_ge(pv_done, PAIRS * (n + 1))
                after(act, out_ready, 2 * (n - 1))
                nc.scalar.copy(mh[:, s % 2, :], MIX(s)).then_inc(mix_hi, 1)

            def step(it, s, j):
                first, last = it == 0 if isinstance(it, int) else False, it == HP - 1 if isinstance(it, int) else False
                take_turned(it, s, j)
                if s == 2 and j in (0, 2) and not last:
                    fold_query(it + 1, j // 2)
                if j == 0 and not (last and s == NG - 1):
                    query_hi(*moved(it, s, 0, PAIRS)[:2], 0)
                if j == 1 and not (first and s == 0):
                    mixed_hi(*moved(it, s, 0, -PAIRS)[:2])
                if j == 2 and not (last and s == NG - 1):
                    query_hi(*moved(it, s, 0, PAIRS)[:2], 1)
                if not (last and s == NG - 1 and j >= 2):
                    exps(*moved(it, s, j, 2))
                if j == 0 and not (last and s == NG - 1):
                    swap(*moved(it, s, 0, PAIRS)[:2], 1)
                if j == 1 and s == 1:
                    fold_output(it)
                if j == 2 and not (last and s >= NG - 2):
                    swap(*moved(it, s, 0, 2 * PAIRS)[:2], 0)

            def head_pair(it):
                for s in range(NG):
                    for j in range(PAIRS):
                        step(it, s, j)

            fold_query(0, 0)
            fold_query(0, 1)
            swap(0, 0, 0)
            query_hi(0, 0, 0)
            swap(0, 0, 1)
            query_hi(0, 0, 1)
            swap(0, 1, 0)
            exps(0, 0, 0)
            exps(0, 0, 1)
            head_pair(0)
            with act.Fori(1, HP - 1) as it:
                head_pair(it)
            head_pair(HP - 1)
            mixed_hi(HP - 1, NG - 1)

        @block.vector
        def _(dve):
            def fold_query(it, h):
                dve.wait_ge(fold_hi, 2 * it + h + 1)
                nc.vector.tensor_tensor(wl[:, :, h, 0:KVR], fold(h), wh[:, :, h, 0:KVR].bitcast(F32), ALU.subtract)
                nc.vector.tensor_tensor(wl[:, :, h, KVR:P], rot[:, :, h], wh[:, :, h, KVR:P].bitcast(F32), ALU.subtract).then_inc(fold_lo, 1)

            def fold_output(it):
                dve.wait_ge(wo_hi, it + 1)
                nc.vector.tensor_tensor(wol[:], folded_out, woh[:].bitcast(F32), ALU.subtract).then_inc(wo_lo, 1)

            def rope(it, s, h):
                m = 2 * slot_no(it, s) + h
                dve.wait_ge(proj_ready, m + 1)
                after(dve, q_lo, m - 1)
                times_table(nc.vector, c, raw[:, h, :], PROJ(h), ALL_ROWS, C_COSA).then_inc(rope_read, 1)

            def row_max(it, s, j):
                dve.wait_ge(scores_ready, pair_no(it, s, j) + 1)
                nc.vector.tensor_reduce(negmax[:, j, :], S(j).rearrange("p (q t) -> p q t", q=2), AX, ALU.max, negate=True).then_inc(maxed, 1)

            def scale(it, s, j):
                g = pair_no(it, s, j)
                dve.wait_ge(exp_done, g + 1)
                nc.vector.reciprocal(inv[:, j, :], total[:, j, :]).then_inc(inv_done, 1)
                dve.wait_ge(inv_done, g + 1)
                for q in range(2):
                    ins = nc.vector.tensor_scalar(probs[:, j, q, :], probs[:, j, q, :], inv[:, j, q:q + 1], None, ALU.mult)
                ins.then_inc(scaled, 1)

            def mixed_lo(it, s):
                n = slot_no(it, s)
                dve.wait_ge(mix_hi, n + 1)
                nc.vector.tensor_tensor(ml[:, s % 2, :], MIX(s), mh[:, s % 2, :].bitcast(F32), ALU.subtract).then_inc(mix_lo, 1)

            def add_out(it, s, i):
                dve.wait_ge(out_ready, 2 * slot_no(it, s) + i + 1)
                t = s * TG + 2 * i
                nc.vector.tensor_tensor(c.x[:, t:t + 2, :], OUT.rearrange("p (t d) -> p t d", d=D), c.x[:, t:t + 2, :], ALU.add).then_inc(out_added, 1)

            def step(it, s, j):
                first, last = it == 0 if isinstance(it, int) else False, it == HP - 1 if isinstance(it, int) else False
                if not (last and s == NG - 1 and j >= 2):
                    row_max(*moved(it, s, j, 2))
                if not (last and s == NG - 1 and j == 3):
                    scale(*moved(it, s, j, 1))
                if s == 2 and j in (0, 2) and not last:
                    fold_query(it + 1, j // 2)
                if j == 0 and not (last and s == NG - 1):
                    rope(*moved(it, s, 0, PAIRS)[:2], 1)
                if j == 1 and not (first and s <= 1):
                    add_out(*moved(it, s, 0, -2 * PAIRS)[:2], 1)
                if j == 2 and not (last and s >= NG - 2):
                    rope(*moved(it, s, 0, 2 * PAIRS)[:2], 0)
                if j == 3 and not (first and s == 0):
                    add_out(*moved(it, s, 0, -PAIRS)[:2], 0)
                if j == 1 and not (first and s == 0):
                    mixed_lo(*moved(it, s, 0, -PAIRS)[:2])
                if s == 1 and j == 1:
                    fold_output(it)

            def head_pair(it):
                for s in range(NG):
                    for j in range(PAIRS):
                        step(it, s, j)

            fold_query(0, 0)
            fold_query(0, 1)
            rope(0, 0, 0)
            rope(0, 0, 1)
            rope(0, 1, 0)
            row_max(0, 0, 0)
            scale(0, 0, 0)
            row_max(0, 0, 1)
            head_pair(0)
            with dve.Fori(1, HP - 1) as it:
                head_pair(it)
            head_pair(HP - 1)
            add_out(HP - 1, NG - 2, 1)
            mixed_lo(HP - 1, NG - 1)
            add_out(HP - 1, NG - 1, 0)
            add_out(HP - 1, NG - 1, 1)

        @block.gpsimd
        def _(pool):
            def finish_queries(n, s, h):
                pool.wait_ge(swap_done, 2 * n + h + 1)
                rows, other = raw[64:128, h, :], swapped[64:128, h, :]
                times_table(nc.gpsimd, c, other, other, ROT_ROWS, C_SINA).then_inc(sin_done, 1)
                pool.wait_ge(sin_done, 2 * n + h + 1)
                pool.wait_ge(rope_read, 2 * n + h + 1)
                nc.gpsimd.tensor_tensor(rows, rows, other, ALU.add).then_inc(rotated, 1)
                pool.wait_ge(q_hi, 2 * n + h + 1)
                nc.gpsimd.tensor_tensor(ql[:, s % 2, h, :], raw[:, h, :], qh[:, s % 2, h, :].bitcast(F32), ALU.subtract).then_inc(q_lo, 1)
                pool.wait_ge(q_lo, 2 * n + h + 1)

            with pool.Fori(0, HP) as it:
                for s in range(NG):
                    for h in range(2):
                        finish_queries(it * NG + s, s, h)


def attention_b(nc, c, name, w_qkv, w_out):
    W = T + P
    with ExitStack() as ctx:
        sem = lambda n: ctx.enter_context(nc.semaphore(f"{name}_{n}"))
        sb = lambda n, s, d=F32: ctx.enter_context(nc.sbuf_tensor(f"{name}_{n}", s, d))
        stage = sb("stage", [P, 3, KD, 2 * P])
        wh, wl = sb("wh", [P, 3, KD, 2 * P], F32R), sb("wl", [P, 3, KD, 2 * P], F32R)
        wo_stage = sb("wo_stage", [P, 2, D])
        woh, wol = sb("woh", [P, 2, D], F32R), sb("wol", [P, 2, D], F32R)
        qk = sb("qk", [P, 2, 4, G])
        swapped = sb("swapped", [P, 2, G])
        values = sb("values", [P, 2, TG, 2 * P])
        negmax, total, inv = (sb(n, [P, PAIRS, 2]) for n in ("negmax", "total", "inv"))
        probs, probsT = sb("probs", [P, PAIRS, W]), sb("probsT", [P, 2, W])
        mh, ml = sb("mh", [P, 2, 2, G], F32R), sb("ml", [P, 2, 2, G], F32R)
        stage_in, wo_in, w_hi, w_lo, wo_hi, wo_lo = sem("stage_in"), sem("wo_in"), sem("w_hi"), sem("w_lo"), sem("wo_hi"), sem("wo_lo")
        proj_ready, rope_read, rotated, values_done = sem("proj_ready"), sem("rope_read"), sem("rotated"), sem("values_done")
        scores_ready, maxed, exp_done, inv_done, scaled = sem("scores_ready"), sem("maxed"), sem("exp_done"), sem("inv_done"), sem("scaled")
        turned, probsT_done, pv_done, mix_hi, mix_lo = sem("turned"), sem("probsT_done"), sem("pv_done"), sem("mix_hi"), sem("mix_lo")
        vproj_ready, out_ready, out_added = sem("vproj_ready"), sem("out_ready"), sem("out_added")
        swap_done, sin_done = sem("swap_done"), sem("sin_done")
        S = lambda j: c.ps[:, j % 2, :]
        TURN = c.ps[:, 2, 0:W]
        PROJ = lambda i: c.ps[:, 3 + i % 2, :]
        MIX = lambda h: c.ps[:, 5 + h, :]
        OUT = c.ps[:, 7, :]
        span = [slice(0, P), slice(P, W)]
        flat = lambda w: w.rearrange("p a k d -> p (a k d)")
        parts = [slice(0, 2), slice(2, 3)]
        LAST = (HP - 1, NG - 1, PAIRS - 1)
        slot_no = lambda it, s: it * NG + s
        pair_no = lambda it, s, j: (it * NG + s) * PAIRS + j
        block = ctx.enter_context(nc.Block())

        @block.sync
        def _(sp):
            sp.dma_start(stage[:], w_qkv[0]).then_inc(stage_in, 16)
            sp.dma_start(wo_stage[:], w_out[0]).then_inc(wo_in, 16)
            with sp.Fori(1, HP) as it:
                sp.wait_ge(w_lo, 2 * it)
                sp.dma_start(stage[:], w_qkv[bass.ds(it, 1)].squeeze(0)).then_inc(stage_in, 16)
                sp.wait_ge(wo_lo, it)
                sp.dma_start(wo_stage[:], w_out[bass.ds(it, 1)].squeeze(0)).then_inc(wo_in, 16)

        @block.tensor
        def _(pe):
            def project(it, s, i):
                n = slot_no(it, s)
                if i == 0 and s == 0:
                    pe.wait_ge(w_lo, 2 * it + 1)
                if i >= 2:
                    pe.wait_ge(rope_read, 4 * n + i - 1)
                    pe.wait_ge(swap_done, 4 * n + i - 1)
                else:
                    after(pe, values_done, 2 * n + i - 1)
                col = slice((i // 2) * P, (i // 2) * P + P)
                g = slice(s * G, (s + 1) * G)
                for k in range(KD):
                    ins = matmul3(nc, PROJ(i), (wh[:, i % 2, k, col], wl[:, i % 2, k, col]), (c.xh[:, k, g], c.xl[:, k, g]), k == 0, k == KD - 1)
                ins.then_inc(proj_ready, 1)

            def project_values(it, s, i):
                n = slot_no(it, s)
                if i == 0 and s == 0:
                    pe.wait_ge(w_lo, 2 * it + 2)
                pe.wait_ge(rope_read, 4 * n + 3 + i)
                pe.wait_ge(swap_done, 4 * n + 3 + i)
                for t in range(2):
                    tok = slice(s * G + (2 * i + t) * P, s * G + (2 * i + t + 1) * P)
                    for k in range(KD):
                        ins = matmul3(nc, PROJ(i)[:, t * 2 * P:(t + 1) * 2 * P], (c.xh[:, k, tok], c.xl[:, k, tok]), (wh[:, 2, k, :], wl[:, 2, k, :]), k == 0, k == KD - 1)
                ins.then_inc(vproj_ready, 1)

            def scores(it, s, j):
                g = pair_no(it, s, j)
                h, b = j // 2, j % 2
                if b == 0:
                    pe.wait_ge(rotated, 4 * slot_no(it, s) + 2 * h + 2)
                after(pe, exp_done, g - 1)
                for q in range(2):
                    out = S(j)[:, span[q]]
                    nc.tensor.matmul(out, qk[:, s % 2, 2 * h, b * T + q * P:b * T + (q + 1) * P], qk[:, s % 2, 2 * h + 1, b * T:b * T + (q + 1) * P], start=True, stop=False)
                    ins = nc.tensor.matmul(out[:, q * P:(q + 1) * P], c.ident16[:], c.mask16[:], start=False, stop=True)
                ins.then_inc(scores_ready, 1)

            def turn(it, s, j):
                g = pair_no(it, s, j)
                pe.wait_ge(scaled, g + 1)
                after(pe, probsT_done, g)
                for i in range(3):
                    ins = nc.tensor.transpose(TURN[:, i * P:(i + 1) * P], probs[:, j, i * P:(i + 1) * P], c.ident)
                ins.then_inc(turned, 1)

            def mix(it, s, j):
                n, g = slot_no(it, s), pair_no(it, s, j)
                h, b = j // 2, j % 2
                pe.wait_ge(probsT_done, g + 1)
                if j == 0:
                    pe.wait_ge(values_done, 2 * n + 2)
                if b == 0:
                    after(pe, mix_lo, 2 * n + h - 1)
                out = MIX(h)[:, b * T:(b + 1) * T]
                v = lambda k: values[:, s % 2, 2 * b + k, h * P:(h + 1) * P]
                nc.tensor.matmul(out, v(0), probsT[:, j % 2, 0:T], start=True, stop=False)
                nc.tensor.matmul(out[:, P:T], v(1), probsT[:, j % 2, T:W], start=False, stop=True).then_inc(pv_done, 1)

            def output(it, s, i):
                n = slot_no(it, s)
                if i == 0:
                    pe.wait_ge(mix_lo, 2 * n + 2)
                    if s == 0:
                        pe.wait_ge(wo_lo, it + 1)
                after(pe, out_added, 2 * n + i)
                for t in range(2):
                    tok = slice((2 * i + t) * P, (2 * i + t + 1) * P)
                    for h in range(2):
                        ins = matmul3(nc, OUT[:, t * D:(t + 1) * D], (mh[:, s % 2, h, tok], ml[:, s % 2, h, tok]), (woh[:, h, :], wol[:, h, :]), h == 0, h == 1)
                ins.then_inc(out_ready, 1)

            def step(it, s, j):
                first, last = it == 0 if isinstance(it, int) else False, it == HP - 1 if isinstance(it, int) else False
                if not (last and s == NG - 1 and j >= 2):
                    scores(*moved(it, s, j, 2))
                turn(it, s, j)
                if not (first and s == 0 and j == 0):
                    mix(*moved(it, s, j, -1))
                nxt = moved(it, s, 0, PAIRS)[:2]
                if j == 0 and not (last and s == NG - 1):
                    project(*nxt, 2)
                    project(*nxt, 3)
                if j in (1, 2) and not (last and s == NG - 1):
                    project_values(*nxt, j - 1)
                if j >= 2 and not (first and s == 0):
                    output(*moved(it, s, 0, -PAIRS)[:2], j - 2)
                if j == 3 and not (last and s >= NG - 2):
                    project(*moved(it, s, 0, 2 * PAIRS)[:2], 0)
                    project(*moved(it, s, 0, 2 * PAIRS)[:2], 1)

            def head_pair(it):
                for s in range(NG):
                    for j in range(PAIRS):
                        step(it, s, j)

            for i in range(4):
                project(0, 0, i)
            project_values(0, 0, 0)
            project_values(0, 0, 1)
            project(0, 1, 0)
            project(0, 1, 1)
            scores(0, 0, 0)
            scores(0, 0, 1)
            head_pair(0)
            with pe.Fori(1, HP - 1) as it:
                head_pair(it)
            head_pair(HP - 1)
            mix(*LAST)
            output(HP - 1, NG - 1, 0)
            output(HP - 1, NG - 1, 1)

        @block.scalar
        def _(act):
            def split_hi(it, part):
                act.wait_ge(stage_in, 16 * (it + 1))
                if part == 0:
                    after(act, proj_ready, 4 * NG * it)
                else:
                    after(act, vproj_ready, 2 * NG * it)
                nc.scalar.copy(flat(wh[:, parts[part]]), flat(stage[:, parts[part]])).then_inc(w_hi, 1)

            def split_wo(it):
                act.wait_ge(wo_in, 16 * (it + 1))
                after(act, out_ready, 2 * NG * it)
                nc.scalar.copy(woh[:], wo_stage[:]).then_inc(wo_hi, 1)

            def swap(it, s, i):
                m = 4 * slot_no(it, s) + i
                act.wait_ge(rope_read, m + 1)
                after(act, rotated, m - 1)
                swap_b(nc, PROJ(i), swapped[:, i % 2, :]).then_inc(swap_done, 1)

            def exps(it, s, j):
                g = pair_no(it, s, j)
                act.wait_ge(maxed, g + 1)
                after(act, turned, g - PAIRS + 1)
                for q in range(2):
                    ins = nc.scalar.activation(probs[:, j, span[q]], S(j)[:, span[q]], ACT.Exp, bias=negmax[:, j, q:q + 1], accum_out=total[:, j, q:q + 1])
                ins.then_inc(exp_done, 1)

            def take_turned(it, s, j):
                g = pair_no(it, s, j)
                act.wait_ge(turned, g + 1)
                after(act, pv_done, g - 1)
                nc.scalar.copy(probsT[:, j % 2, :], TURN).then_inc(probsT_done, 1)

            def take_values(it, s, i):
                n = slot_no(it, s)
                act.wait_ge(vproj_ready, 2 * n + i + 1)
                after(act, pv_done, PAIRS * (n - 1))
                nc.scalar.copy(values[:, s % 2, 2 * i:2 * i + 2, :], PROJ(i).rearrange("p (t d) -> p t d", t=2)).then_inc(values_done, 1)

            def mixed_hi(it, s, h):
                n = slot_no(it, s)
                act.wait_ge(pv_done, PAIRS * n + 2 * h + 2)
                after(act, out_ready, 2 * (n - 1))
                nc.scalar.copy(mh[:, s % 2, h, :], MIX(h)).then_inc(mix_hi, 1)

            def step(it, s, j):
                first, last = it == 0 if isinstance(it, int) else False, it == HP - 1 if isinstance(it, int) else False
                take_turned(it, s, j)
                if not (last and s == NG - 1 and j >= 2):
                    exps(*moved(it, s, j, 2))
                if j == 0 and not (first and s == 0):
                    mixed_hi(*moved(it, s, 0, -PAIRS)[:2], 1)
                if j == 0 and not (last and s == NG - 1):
                    swap(*moved(it, s, 0, PAIRS)[:2], 2)
                    swap(*moved(it, s, 0, PAIRS)[:2], 3)
                if j in (1, 2) and not (last and s == NG - 1):
                    take_values(*moved(it, s, 0, PAIRS)[:2], j - 1)
                if j == 3:
                    mixed_hi(it, s, 0)
                    if not (last and s >= NG - 2):
                        swap(*moved(it, s, 0, 2 * PAIRS)[:2], 0)
                        swap(*moved(it, s, 0, 2 * PAIRS)[:2], 1)
                if s == NG - 2 and not last and j in (1, 3):
                    split_hi(it + 1, j // 2)
                if s == 0 and j == 3:
                    split_wo(it)

            def head_pair(it):
                for s in range(NG):
                    for j in range(PAIRS):
                        step(it, s, j)

            split_hi(0, 0)
            split_hi(0, 1)
            for i in range(4):
                swap(0, 0, i)
            take_values(0, 0, 0)
            take_values(0, 0, 1)
            swap(0, 1, 0)
            swap(0, 1, 1)
            exps(0, 0, 0)
            exps(0, 0, 1)
            head_pair(0)
            with act.Fori(1, HP - 1) as it:
                head_pair(it)
            head_pair(HP - 1)
            mixed_hi(HP - 1, NG - 1, 1)

        @block.vector
        def _(dve):
            def split_lo(it, part):
                dve.wait_ge(w_hi, 2 * it + part + 1)
                nc.vector.tensor_tensor(flat(wl[:, parts[part]]), flat(stage[:, parts[part]]), flat(wh[:, parts[part]]).bitcast(F32), ALU.subtract).then_inc(w_lo, 1)

            def split_wo(it):
                dve.wait_ge(wo_hi, it + 1)
                nc.vector.tensor_tensor(wol[:], wo_stage[:], woh[:].bitcast(F32), ALU.subtract).then_inc(wo_lo, 1)

            def rope(it, s, i):
                m = 4 * slot_no(it, s) + i
                dve.wait_ge(proj_ready, m + 1)
                times_table(nc.vector, c, qk[:, s % 2, i, :], PROJ(i), ALL_ROWS, C_COSB).then_inc(rope_read, 1)

            def row_max(it, s, j):
                dve.wait_ge(scores_ready, pair_no(it, s, j) + 1)
                for q in range(2):
                    ins = nc.vector.tensor_reduce(negmax[:, j, q:q + 1], S(j)[:, span[q]], AX, ALU.max, negate=True)
                ins.then_inc(maxed, 1)

            def scale(it, s, j):
                g = pair_no(it, s, j)
                dve.wait_ge(exp_done, g + 1)
                nc.vector.reciprocal(inv[:, j, :], total[:, j, :]).then_inc(inv_done, 1)
                dve.wait_ge(inv_done, g + 1)
                for q in range(2):
                    ins = nc.vector.tensor_scalar(probs[:, j, span[q]], probs[:, j, span[q]], inv[:, j, q:q + 1], None, ALU.mult)
                ins.then_inc(scaled, 1)

            def mixed_lo(it, s, h):
                n = slot_no(it, s)
                dve.wait_ge(mix_hi, 2 * n + h + 1)
                nc.vector.tensor_tensor(ml[:, s % 2, h, :], MIX(h), mh[:, s % 2, h, :].bitcast(F32), ALU.subtract).then_inc(mix_lo, 1)

            def add_out(it, s, i):
                dve.wait_ge(out_ready, 2 * slot_no(it, s) + i + 1)
                t = s * TG + 2 * i
                nc.vector.tensor_tensor(c.x[:, t:t + 2, :], OUT.rearrange("p (t d) -> p t d", d=D), c.x[:, t:t + 2, :], ALU.add).then_inc(out_added, 1)

            def step(it, s, j):
                first, last = it == 0 if isinstance(it, int) else False, it == HP - 1 if isinstance(it, int) else False
                if not (last and s == NG - 1 and j == 3):
                    scale(*moved(it, s, j, 1))
                if j == 0 and not (first and s <= 1):
                    add_out(*moved(it, s, 0, -2 * PAIRS)[:2], 1)
                if j == 3 and not (first and s == 0):
                    add_out(*moved(it, s, 0, -PAIRS)[:2], 0)
                if not (last and s == NG - 1 and j >= 2):
                    row_max(*moved(it, s, j, 2))
                if j == 0:
                    if not (last and s == NG - 1):
                        rope(*moved(it, s, 0, PAIRS)[:2], 2)
                        rope(*moved(it, s, 0, PAIRS)[:2], 3)
                    if s == NG - 1 and not last:
                        split_lo(it + 1, 1)
                if j == 1 and not (first and s == 0):
                    mixed_lo(*moved(it, s, 0, -PAIRS)[:2], 1)
                if s == NG - 2 and not last and j == 2:
                    split_lo(it + 1, 0)
                if j == 3:
                    mixed_lo(it, s, 0)
                    if not (last and s >= NG - 2):
                        rope(*moved(it, s, 0, 2 * PAIRS)[:2], 0)
                        rope(*moved(it, s, 0, 2 * PAIRS)[:2], 1)
                if s == 1 and j == 0:
                    split_wo(it)

            def head_pair(it):
                for s in range(NG):
                    for j in range(PAIRS):
                        step(it, s, j)

            split_lo(0, 0)
            split_lo(0, 1)
            for i in range(4):
                rope(0, 0, i)
            rope(0, 1, 0)
            rope(0, 1, 1)
            row_max(0, 0, 0)
            row_max(0, 0, 1)
            scale(0, 0, 0)
            head_pair(0)
            with dve.Fori(1, HP - 1) as it:
                head_pair(it)
            head_pair(HP - 1)
            add_out(HP - 1, NG - 2, 1)
            mixed_lo(HP - 1, NG - 1, 1)
            add_out(HP - 1, NG - 1, 0)
            add_out(HP - 1, NG - 1, 1)

        @block.gpsimd
        def _(pool):
            with pool.Fori(0, HP) as it:
                for s in range(NG):
                    for i in range(4):
                        m = 4 * (it * NG + s) + i
                        pool.wait_ge(swap_done, m + 1)
                        rows, other = qk[:, s % 2, i, :], swapped[:, i % 2, :]
                        times_table(nc.gpsimd, c, other, other, ALL_ROWS, C_SINB).then_inc(sin_done, 1)
                        pool.wait_ge(sin_done, m + 1)
                        pool.wait_ge(rope_read, m + 1)
                        nc.gpsimd.tensor_tensor(rows, rows, other, ALU.add).then_inc(rotated, 1)


def router(nc, c, name):
    with ExitStack() as ctx:
        sem = lambda n: ctx.enter_context(nc.semaphore(f"{name}_{n}"))
        sb = lambda n, s, d=F32: ctx.enter_context(nc.sbuf_tensor(f"{name}_{n}", s, d))
        z, inh, dist, near, far = (sb(n, [P, NT, E]) for n in ("z", "inh", "dist", "near", "far"))
        lo_side, hi_side, top, part = (sb(n, [P, NT, E]) for n in ("lo_side", "hi_side", "top", "part"))
        greater, equal = sb("greater", [P, NT, E, E]), sb("equal", [P, NT, E, E])
        wsum, none, some = sb("wsum", [P, NT]), sb("none", [P, NT]), sb("some", [P, NT])
        logits_ready, chained, exp_done = sem("logits_ready"), sem("chained"), sem("exp_done")
        block = ctx.enter_context(nc.Block())

        @block.tensor
        def _(pe):
            for t in range(NT):
                tok = slice(t * P, (t + 1) * P)
                out = c.ps[:, t // 2, (t % 2) * 256:(t % 2) * 256 + 256]
                for k in range(KD):
                    nc.tensor.matmul(out, c.xl[:, k, tok], c.wr[:, k, :], start=(k == 0), stop=False)
                    ins = nc.tensor.matmul(out, c.xh[:, k, tok], c.wr[:, k, :], start=False, stop=(k == KD - 1))
            ins.then_inc(logits_ready, 1)

        @block.scalar
        def _(act):
            act.wait_ge(chained, 3)
            nc.scalar.activation(inh[:], z[:], ACT.Exp, scale=-1.0).then_inc(exp_done, 1)
            act.wait_ge(chained, 7)
            nc.scalar.activation(near[:], dist[:], ACT.Exp, scale=-1.0 / 0.1)
            nc.scalar.activation(far[:], dist[:], ACT.Exp, scale=-1.0 / 0.3).then_inc(exp_done, 1)

        @block.vector
        def _(dve):
            done = [0]

            def step(ins):
                done[0] += 1
                ins.then_inc(chained, 1)
                dve.wait_ge(chained, done[0])

            v = nc.vector
            row = lambda ap: ap[:].unsqueeze(2).to_broadcast([P, NT, E])
            dve.wait_ge(logits_ready, 1)
            logits = c.ps[:].rearrange("p b (i w) -> p (b i) w", w=256)
            step(v.tensor_copy(z[:], logits[:, :, 0:E]))
            step(v.tensor_tensor(z[:], logits[:, :, E:2 * E], z[:], ALU.add))
            step(v.tensor_scalar(z[:], z[:], c.inv_temperature[:, 0:1], None, ALU.mult))
            dve.wait_ge(exp_done, 1)
            step(v.tensor_scalar(inh[:], inh[:], 1.0, None, ALU.add))
            step(v.reciprocal(inh[:], inh[:]))
            step(v.tensor_scalar(inh[:], inh[:], GOLDEN_CENTER, None, ALU.subtract))
            step(v.scalar_tensor_tensor(out=dist[:], in0=inh[:], scalar=-1.0, in1=inh[:], op0=ALU.mult, op1=ALU.max))
            step(v.tensor_scalar(lo_side[:], z[:], LOGIT_LOWER, None, ALU.is_ge))
            step(v.tensor_scalar(hi_side[:], z[:], 0.0, None, ALU.is_le))
            step(v.tensor_tensor(lo_side[:], lo_side[:], hi_side[:], ALU.mult))
            dve.wait_ge(exp_done, 2)
            step(v.tensor_tensor(near[:], near[:], lo_side[:], ALU.mult))
            step(v.tensor_reduce(wsum[:], near[:], AX, ALU.add))
            step(v.tensor_scalar(none[:], wsum[:], 1e-8, None, ALU.is_lt))
            for t in range(NT):
                ins = v.tensor_tensor(greater[:, t], far[:, t].unsqueeze(1).to_broadcast([P, E, E]), far[:, t].unsqueeze(2).to_broadcast([P, E, E]), ALU.is_gt)
            step(ins)
            for t in range(NT):
                ins = v.tensor_tensor(equal[:, t], far[:, t].unsqueeze(1).to_broadcast([P, E, E]), far[:, t].unsqueeze(2).to_broadcast([P, E, E]), ALU.is_equal)
            step(ins)
            step(v.tensor_tensor(equal[:].rearrange("p t e f -> p t (e f)"), equal[:].rearrange("p t e f -> p t (e f)"),
                                 c.before[:].unsqueeze(1).to_broadcast([P, NT, E * E]), ALU.mult))
            step(v.tensor_tensor(greater[:], greater[:], equal[:], ALU.add))
            step(v.tensor_reduce(top[:], greater[:], AX, ALU.add))
            step(v.tensor_scalar(top[:], top[:], 2.0, None, ALU.is_lt))
            step(v.tensor_tensor(part[:], far[:], top[:], ALU.mult))
            step(v.tensor_reduce(some[:], part[:], AX, ALU.add))
            step(v.tensor_scalar(some[:], some[:], 1e-8, None, ALU.max))
            step(v.reciprocal(some[:], some[:]))
            step(v.tensor_tensor(part[:], part[:], row(some), ALU.mult))
            step(v.tensor_tensor(part[:], part[:], row(none), ALU.mult))
            step(v.tensor_scalar(none[:], none[:], -1.0, 1.0, ALU.mult, ALU.add))
            step(v.tensor_tensor(near[:], near[:], row(none), ALU.mult))
            step(v.tensor_tensor(near[:], near[:], part[:], ALU.add))
            step(v.tensor_reduce(wsum[:], near[:], AX, ALU.add))
            step(v.tensor_scalar(wsum[:], wsum[:], 1e-8, None, ALU.max))
            step(v.reciprocal(wsum[:], wsum[:]))
            step(v.tensor_tensor(c.gate[:], near[:], row(wsum), ALU.mult))


def experts(nc, c, name, weights):
    with ExitStack() as ctx:
        sem = lambda n: ctx.enter_context(nc.semaphore(f"{name}_{n}"))
        sb = lambda n, s, d=F32: ctx.enter_context(nc.sbuf_tensor(f"{name}_{n}", s, d))
        stage = sb("stage", [P, 2, 3, KD, F])
        wh, wl = sb("wh", [P, 2, 3, KD, F], F32R), sb("wl", [P, 2, 3, KD, F], F32R)
        col = sb("col", [P, 2, NT])
        silu, hidden = sb("silu", [P, 2, G]), sb("hidden", [P, 2, G])
        hh, hl = sb("hh", [P, 2, 2, G], F32R), sb("hl", [P, 2, 2, G], F32R)
        stage_in = [sem("stage_in_even"), sem("stage_in_odd")]
        w_hi, w_lo, col_done = sem("w_hi"), sem("w_lo"), sem("col_done")
        gated, silu_done, hid_done, hi_done, lo_done = sem("gated"), sem("silu_done"), sem("hid_done"), sem("hi_done"), sem("lo_done")
        out_ready, out_added = sem("out_ready"), sem("out_added")
        GATE = lambda m: c.ps[:, 2 * m, :]
        UP = lambda m: c.ps[:, 2 * m + 1, :]
        OUT = lambda i: c.ps[:, 4 + i, :]
        TURNS = E // 2
        block = ctx.enter_context(nc.Block())
        flat = lambda w, e: w[:, e].rearrange("p a k d -> p (a k d)")


        @block.sync
        def _(sp):
            for e in range(2):
                sp.dma_start(stage[:, e], weights[e]).then_inc(stage_in[e], 16)
            with sp.Fori(1, TURNS) as it:
                for e in range(2):
                    sp.wait_ge(w_lo, 2 * it - 1 + e)
                    sp.dma_start(stage[:, e], weights[bass.ds(2 * it + e, 1)].squeeze(0)).then_inc(stage_in[e], 16)

        @block.tensor
        def _(pe):
            def gate_up(it, e, s, first=False):
                n = 8 * it + 4 * e + s
                if s == 0:
                    pe.wait_ge(w_lo, 2 * it + e + 1)
                g = slice(s * G, (s + 1) * G)
                for m in range(2):
                    if not first:
                        pe.wait_ge(hid_done, 2 * n + m - 1)
                    f = slice(m * P, (m + 1) * P)
                    for a, out in ((0, GATE(m)), (1, UP(m))):
                        for k in range(KD):
                            ins = matmul3(nc, out, (wh[:, e, a, k, f], wl[:, e, a, k, f]), (c.xh[:, k, g], c.xl[:, k, g]), k == 0, k == KD - 1)
                        ins.then_inc(gated, 1)

            def down(it, e, s, first=False):
                n = 8 * it + 4 * e + s
                pe.wait_ge(lo_done, 2 * n + 2)
                for t in range(TG):
                    if not (first and t < 4):
                        pe.wait_ge(out_added, 4 * n + t - 3)
                    tok = slice(t * P, (t + 1) * P)
                    for k in range(KD):
                        ins = matmul3(nc, OUT(t)[:, 0:D], (hh[:, s % 2, k, tok], hl[:, s % 2, k, tok]), (wh[:, e, 2, k, :], wl[:, e, 2, k, :]), k == 0, k == KD - 1)
                    ins.then_inc(out_ready, 1)

            def turn(it, first, last):
                for e in range(2):
                    for s in range(NG):
                        nxt = (it, e, s + 1) if s + 1 < NG else (it, 1, 0) if e == 0 else (it + 1, 0, 0)
                        if not (last and e == 1 and s == NG - 1):
                            gate_up(*nxt)
                        down(it, e, s, first and e == 0 and s == 0)

            gate_up(0, 0, 0, True)
            turn(0, True, False)
            with pe.Fori(1, TURNS - 1) as it:
                turn(it, False, False)
            turn(TURNS - 1, False, True)

        @block.scalar
        def _(act):
            def split_hi(it, e):
                act.wait_ge(stage_in[e], 16 * (it + 1))
                if not (isinstance(it, int) and it == 0):
                    act.wait_ge(out_ready, 4 * (8 * it + 4 * e - 4))
                nc.scalar.copy(flat(wh, e), flat(stage, e)).then_inc(w_hi, 1)

            def activate(it, e, s, m):
                n = 8 * it + 4 * e + s
                act.wait_ge(gated, 4 * n + 2 * m + 1)
                if not (isinstance(it, int) and it == 0 and e == 0 and s == 0):
                    act.wait_ge(hid_done, 2 * n + m - 1)
                nc.scalar.activation(silu[:, m, :], GATE(m), ACT.Silu).then_inc(silu_done, 1)

            def hidden_hi(it, e, s, m):
                n = 8 * it + 4 * e + s
                act.wait_ge(hid_done, 2 * n + m + 1)
                if not (isinstance(it, int) and it == 0 and e == 0 and s < 2):
                    act.wait_ge(out_ready, 4 * (n - 1))
                nc.scalar.copy(hh[:, s % 2, m, :], hidden[:, m, :]).then_inc(hi_done, 1)

            def turn(it, last):
                for e in range(2):
                    for s in range(NG):
                        activate(it, e, s, 0)
                        activate(it, e, s, 1)
                        hidden_hi(it, e, s, 0)
                        hidden_hi(it, e, s, 1)
                        if s == 1 and not (last and e == 1):
                            split_hi(*((it, 1) if e == 0 else (it + 1, 0)))

            split_hi(0, 0)
            turn(0, False)
            with act.Fori(1, TURNS - 1) as it:
                turn(it, False)
            turn(TURNS - 1, True)

        @block.vector
        def _(dve):
            def split_lo(it, e):
                dve.wait_ge(w_hi, 2 * it + e + 1)
                nc.vector.tensor_tensor(flat(wl, e), flat(stage, e), flat(wh, e).bitcast(F32), ALU.subtract).then_inc(w_lo, 1)

            def hidden_rows(it, e, s, m):
                n = 8 * it + 4 * e + s
                dve.wait_ge(gated, 4 * n + 2 * m + 2)
                dve.wait_ge(silu_done, 2 * n + m + 1)
                if not (isinstance(it, int) and it == 0 and e == 0 and s == 0):
                    dve.wait_ge(lo_done, 2 * n + m - 1)
                nc.vector.tensor_tensor(hidden[:, m, :], UP(m), silu[:, m, :], ALU.mult).then_inc(hid_done, 1)

            def hidden_lo(it, e, s, m):
                n = 8 * it + 4 * e + s
                dve.wait_ge(hi_done, 2 * n + m + 1)
                nc.vector.tensor_tensor(hl[:, s % 2, m, :], hidden[:, m, :], hh[:, s % 2, m, :].bitcast(F32), ALU.subtract).then_inc(lo_done, 1)

            def add_out(it, e, s):
                n = 8 * it + 4 * e + s
                if s == 0:
                    dve.wait_ge(col_done, 2 * it + e + 1)
                for t in range(TG):
                    dve.wait_ge(out_ready, 4 * n + t + 1)
                    i = s * TG + t
                    nc.vector.scalar_tensor_tensor(out=c.x[:, i, :], in0=OUT(t)[:, 0:D], scalar=col[:, e, i:i + 1], in1=c.x[:, i, :], op0=ALU.mult, op1=ALU.add).then_inc(out_added, 1)

            def turn(it, first, last):
                for e in range(2):
                    for s in range(NG):
                        hidden_rows(it, e, s, 0)
                        hidden_rows(it, e, s, 1)
                        hidden_lo(it, e, s, 0)
                        hidden_lo(it, e, s, 1)
                        if s == 1 and not (last and e == 1):
                            split_lo(*((it, 1) if e == 0 else (it + 1, 0)))
                        if not (first and e == 0 and s == 0):
                            add_out(*((it, e, s - 1) if s else (it, 0, NG - 1) if e == 1 else (it - 1, 1, NG - 1)))
                        if s == 0:
                            ex = 2 * it + e
                            nc.vector.tensor_copy(col[:, e, :].unsqueeze(2), c.gate[:, :, ex:ex + 1] if isinstance(ex, int) else c.gate[:, :, bass.ds(ex, 1)]).then_inc(col_done, 1)

            split_lo(0, 0)
            turn(0, True, False)
            with dve.Fori(1, TURNS - 1) as it:
                turn(it, False, False)
            turn(TURNS - 1, False, True)
            add_out(TURNS - 1, 1, NG - 1)


def load(nc, c, x, const, small, temperature, before):
    with ExitStack() as ctx:
        small_in = ctx.enter_context(nc.sbuf_tensor("small_in", [P, KD, S_COLS], F32))
        loaded, const_in, hi_done, wr_done = (ctx.enter_context(nc.semaphore(n)) for n in ("loaded", "const_in", "small_hi", "wr_zero"))
        block = ctx.enter_context(nc.Block())

        @block.sync
        def _(sp):
            sp.dma_start(small_in[:], small).then_inc(loaded, 16)
            sp.dma_start(c.const[:], const).then_inc(loaded, 16)
            sp.dma_start(c.before[:], before.to_broadcast([P, E * E])).then_inc(loaded, 16)
            sp.dma_start(c.temperature[:], temperature.to_broadcast([P, 1])).then_inc(loaded, 16)
            sp.dma_start(c.x[:], x.rearrange("(t p) d -> p t d", p=P)).then_inc(const_in, 16)
            sp.wait_ge(const_in, 16)

        @block.scalar
        def _(act):
            act.wait_ge(loaded, 64)
            act.wait_ge(wr_done, 1)
            nc.scalar.copy(c.sh[:], small_in[:, :, 0:S_WR])
            nc.scalar.copy(c.wr[:, :, 0:E], small_in[:, :, S_WR:S_WR + E]).then_inc(hi_done, 1)
            nc.scalar.copy(c.ident16[:], c.const[:, C_IDENT:C_IDENT + P])
            nc.scalar.copy(c.mask16[:], c.const[:, C_MASK:C_MASK + P])

        @block.vector
        def _(dve):
            nc.vector.memset(c.wr[:].bitcast(F32), 0.0).then_inc(wr_done, 1)
            dve.wait_ge(hi_done, 1)
            nc.vector.reciprocal(c.inv_temperature[:], c.temperature[:])
            nc.vector.tensor_tensor(c.sl[:], small_in[:, :, 0:S_WR], c.sh[:].bitcast(F32), ALU.subtract)
            nc.vector.tensor_tensor(c.wr[:, :, E:2 * E], small_in[:, :, S_WR:S_WR + E], c.wr[:, :, 0:E].bitcast(F32), ALU.subtract)


def store(nc, c, out):
    with ExitStack() as ctx:
        stored = ctx.enter_context(nc.semaphore("stored"))
        block = ctx.enter_context(nc.Block())

        @block.sync
        def _(sp):
            sp.dma_start(out.rearrange("(t p) d -> p t d", p=P), c.x[:]).then_inc(stored, 16)
            sp.wait_ge(stored, 16)


def hybrid_kernel(nc, x, const, before, small, temperature, wa, wb_qkv, wb_out, wf, out):
    with ExitStack() as ctx:
        sb = lambda n, s, d=F32: ctx.enter_context(nc.sbuf_tensor(n, s, d))
        c = Core()
        c.x = sb("x", [P, NT, D])
        c.xh, c.xl = sb("xh", [P, KD, N], F32R), sb("xl", [P, KD, N], F32R)
        c.const = sb("const", [P, C_COLS])
        c.ident = c.const[:, C_IDENT:C_IDENT + P]
        c.ident16, c.mask16 = sb("ident16", [P, P], BF16), sb("mask16", [P, P], BF16)
        c.before = sb("before", [P, E * E])
        c.temperature, c.inv_temperature = sb("temperature", [P, 1]), sb("inv_temperature", [P, 1])
        c.sh, c.sl = sb("sh", [P, KD, S_WR], F32R), sb("sl", [P, KD, S_WR], F32R)
        c.wr = sb("wr", [P, KD, 256], F32R)
        c.gate = sb("gate", [P, NT, E])
        c.ps = ctx.enter_context(nc.psum_tensor("ps", [P, 8, 512], F32))

        load(nc, c, x, const, small, temperature, before)
        layer_norm(nc, c, "ln1")
        with ExitStack() as inner:
            sa = lambda n, s, d=F32: inner.enter_context(nc.sbuf_tensor(n, s, d))
            a = Core()
            a.q1h, a.q1l, a.q2 = sa("q1h", [P, N], F32R), sa("q1l", [P, N], F32R), sa("q2", [P, N], F32R)
            a.keys, a.kh, a.kl = sa("keys", [P, N]), sa("kh", [P, N], F32R), sa("kl", [P, N], F32R)
            a.values = sa("values", [P, NT, KVR])
            latents(nc, c, "lat", a)
            attention_a(nc, c, "aa", a, wa)
        layer_norm(nc, c, "ln2")
        router(nc, c, "r1")
        experts(nc, c, "f1", wf)
        layer_norm(nc, c, "ln3")
        attention_b(nc, c, "ab", wb_qkv, wb_out)
        layer_norm(nc, c, "ln4")
        router(nc, c, "r2")
        experts(nc, c, "f2", wf)
        store(nc, c, out)


def constants():
    const = np.zeros((P, C_COLS), np.float32)
    pos = np.arange(T, dtype=np.float32)
    theta = (1.0 / np.float32(10000.0) ** (np.arange(0, ROT, 2, dtype=np.float32) / ROT)).astype(np.float32)
    ang = (pos[None, :] * theta[:, None]).astype(np.float32)
    const[0:64, C_COSA:C_COSA + T] = 1.0
    const[64:96, C_COSA:C_COSA + T] = np.cos(ang)
    const[96:128, C_COSA:C_COSA + T] = np.cos(ang)
    const[64:96, C_SINA:C_SINA + T] = -np.sin(ang)
    const[96:128, C_SINA:C_SINA + T] = np.sin(ang)
    half = 64
    freqs = np.power(np.float32(10000.0), -np.arange(half, dtype=np.float32) / half).astype(np.float32)
    rad = (pos[None, :] * freqs[:, None]).astype(np.float32)
    mult = np.float32((1.0 / 128.0) ** 0.5)
    for r in (0, 64):
        const[r:r + 64, C_COSB:C_COSB + T] = np.cos(rad) * mult
    const[0:64, C_SINB:C_SINB + T] = -np.sin(rad) * mult
    const[64:128, C_SINB:C_SINB + T] = np.sin(rad) * mult
    const[:, C_IDENT:C_IDENT + P] = np.eye(P, dtype=np.float32)
    const[:, C_MASK:C_MASK + P] = np.triu(np.full((P, P), -1e30, np.float32), 1)
    e = np.arange(E)
    before = (e[None, :] < e[:, None]).astype(np.float32).reshape(1, E * E)
    return const, before


def kernel(**inputs):
    import numpy as _np
    import concourse.bacc as _bacc
    from concourse import mybir as _mybir
    from concourse.bass_utils import run_bass_kernel_spmd as _run

    w = {k: _np.asarray(v) for k, v in inputs.items()}
    const, before = constants()
    pairs = _np.concatenate([_np.arange(0, ROT, 2), _np.arange(1, ROT, 2)])

    qa = w["L0_attn_a_q_a_w"].T
    kva = w["L0_attn_a_kv_a_w"]
    kva = _np.concatenate([kva[:KVR], kva[KVR:][pairs]]).T
    small = _np.concatenate([qa, qa[:, P:QR], kva, w["L0_ffn_Wr"]], axis=1)
    small = _np.ascontiguousarray(small.reshape(KD, P, S_COLS).transpose(1, 0, 2))

    qb = w["L0_attn_a_q_b_w"].reshape(HP, 2, NOPE + ROT, QR)
    qpass = qb[:, :, :NOPE]
    qpass = _np.concatenate([qpass, qpass[..., P:QR]], axis=-1).reshape(HP, P, 256)
    qrot = qb[:, :, NOPE:][:, :, pairs].transpose(0, 3, 1, 2)
    qrot = _np.concatenate([qrot, qrot[:, P:QR]], axis=1).reshape(HP, 2, P, 2 * ROT).transpose(0, 2, 1, 3).reshape(HP, P, 4 * ROT)
    kvb = w["L0_attn_a_kv_b_w"].reshape(HP, 2, NOPE + VD, KVR)
    wk = kvb[:, :, :NOPE].reshape(HP, P, KVR)
    wv = kvb[:, :, NOPE:].transpose(0, 2, 1, 3).reshape(HP, P, 2 * KVR)
    ow = w["L0_attn_a_o_w"].T.reshape(HP, 2, VD, D).transpose(0, 2, 1, 3).reshape(HP, P, 2 * D)
    wa = _np.ascontiguousarray(_np.concatenate([qpass, wk, qrot, wv, ow], axis=2))

    qkv = _np.stack([w["L0_attn_b_wq"], w["L0_attn_b_wk"], w["L0_attn_b_wv"]])
    wb_qkv = _np.ascontiguousarray(qkv.reshape(3, KD, P, HP, 2 * P).transpose(3, 2, 0, 1, 4))
    wb_out = _np.ascontiguousarray(w["L0_attn_b_wo"].reshape(HP, 2, P, D).transpose(0, 2, 1, 3))

    wf = _np.stack([w["L0_ffn_Wg"], w["L0_ffn_Wu"], w["L0_ffn_Wd"]], axis=1)
    wf = _np.ascontiguousarray(wf.reshape(E, 3, KD, P, F).transpose(0, 3, 1, 2, 4))

    nc = _bacc.Bacc("TRN2", target_bir_lowering=False, num_devices=1)
    arrays = {
        "x_in": _np.ascontiguousarray(w["L0_attn_a_x"]).reshape(N, D),
        "const_in": const, "before_in": before, "small_weights": small,
        "temperature_in": w["L0_ffn_temperature"].reshape(1, 1),
        "wa_in": wa, "wb_qkv_in": wb_qkv, "wb_out_in": wb_out, "wf_in": wf,
    }
    args = [nc.dram_tensor(n, a.shape, _mybir.dt.from_np(a.dtype), kind="ExternalInput").ap() for n, a in arrays.items()]
    out = nc.dram_tensor("out_0", (N, D), _mybir.dt.float32, kind="ExternalOutput").ap()
    hybrid_kernel(nc, *args, out)
    r = _run(nc, [arrays], core_ids=[0])
    return r.results[0]["out_0"].reshape(B, T, D)
```

```python
from contextlib import ExitStack

import concourse.bass as bass
from concourse import mybir
import numpy as np

ALU = mybir.AluOpType
ACT = mybir.ActivationFunctionType
AX = mybir.AxisListType.X
F32 = mybir.dt.float32
F32R = mybir.dt.float32r
BF16 = mybir.dt.bfloat16

P = 128
B, T, D = 8, 256, 256
N = B * T
NT = N // P
KD = D // P
G = 512
NG = N // G
TG = G // P
BG = G // T
H = 16
HP = H // 2
QR, KVR, ROT, NOPE, VD = 192, 64, 64, 64, 128
E, F = 8, 256
EPS = 1e-5
GOLDEN_CENTER = 1.0 / np.e
GOLDEN_LOWER = 0.5 - np.log(4.0 / 3.0)
LOGIT_LOWER = float(np.log(GOLDEN_LOWER / (1.0 - GOLDEN_LOWER)))

A_PASS, A_K, A_ROT, A_V, A_O = 0, 256, 320, 576, 704
A_COLS = 1216
C_COSA, C_SINA, C_COSB, C_SINB, C_IDENT, C_MASK = 0, 256, 512, 768, 1024, 1152
C_COLS = 1280
S_QA, S_KVA, S_WR = 0, 256, 384
S_COLS = 392


class Core:
    pass


def norm_signals(nc, ctx, c, name):
    sem = lambda n: ctx.enter_context(nc.semaphore(f"{name}_{n}"))
    v = Core()
    v.moments, v.meanvar, v.shifted, v.rstd, v.normed = c.moments, c.meanvar, c.shifted, c.rstd, c.normed
    v.stats_done, v.var_done, v.rstd_done = sem("stats_done"), sem("var_done"), sem("rstd_done")
    v.normed_done, v.turned, v.hi_done, v.lo_done = sem("normed_done"), sem("turned"), sem("hi_done"), sem("lo_done")
    return v


def norm_stats(nc, c, v, dve, s):
    for i in range(TG):
        nc.vector.bn_stats(v.moments[:, i, :], c.x[:, s * TG + i, :]).then_inc(v.stats_done, 1)
    dve.wait_ge(v.stats_done, (2 * s + 1) * TG)
    for i in range(TG):
        nc.vector.bn_aggr(v.meanvar[:, s % 2, i, :], v.moments[:, i, :]).then_inc(v.stats_done, 1)
    dve.wait_ge(v.stats_done, (2 * s + 2) * TG)
    nc.vector.tensor_scalar(v.shifted[:, s % 2], v.meanvar[:, s % 2, :, 1], EPS, None, ALU.add).then_inc(v.var_done, 1)


def norm_rstd(nc, c, v, pool, s):
    pool.wait_ge(v.var_done, s + 1)
    nc.gpsimd.tensor_tensor(v.rstd[:, s % 2], v.shifted[:, s % 2], c.minus_half[:], ALU.pow).then_inc(v.rstd_done, 1)


def norm_rows(nc, c, v, dve, s):
    dve.wait_ge(v.rstd_done, s + 1)
    after(dve, v.turned, KD * s)
    for i in range(TG):
        ins = nc.vector.tensor_scalar(v.normed[:, i, :], c.x[:, s * TG + i, :], v.meanvar[:, s % 2, i, 0:1], v.rstd[:, s % 2, i:i + 1], ALU.subtract, ALU.mult)
    ins.then_inc(v.normed_done, 1)


def norm_turn(nc, c, v, pe, s, banks):
    pe.wait_ge(v.normed_done, s + 1)
    after(pe, v.lo_done, KD * s)
    for k in range(KD):
        for i in range(TG):
            ins = nc.tensor.transpose(banks[k][:, i * P:(i + 1) * P], v.normed[:, i, k * P:(k + 1) * P], c.ident)
        ins.then_inc(v.turned, 1)


def norm_hi(nc, c, v, act, s, banks):
    for k in range(KD):
        act.wait_ge(v.turned, KD * s + k + 1)
        nc.scalar.copy(c.xh[:, k, s * G:(s + 1) * G], banks[k]).then_inc(v.hi_done, 1)


def norm_lo(nc, c, v, dve, s, banks):
    for k in range(KD):
        dve.wait_ge(v.hi_done, KD * s + k + 1)
        g = slice(s * G, (s + 1) * G)
        nc.vector.tensor_tensor(c.xl[:, k, g], banks[k], c.xh[:, k, g].bitcast(F32), ALU.subtract).then_inc(v.lo_done, 1)


def matmul3(nc, out, left, right, start, stop):
    (lh, ll), (rh, rl) = left, right
    nc.tensor.matmul(out, ll, rh, start=start, stop=False)
    nc.tensor.matmul(out, lh, rl, start=False, stop=False)
    return nc.tensor.matmul(out, lh, rh, start=False, stop=stop)


def opening(nc, c, name, a, x, const, small, temperature, order, weights, stage, stage_in):
    with ExitStack() as ctx:
        sem = lambda n: ctx.enter_context(nc.semaphore(f"{name}_{n}"))
        sb = lambda n, s, d=F32: ctx.enter_context(nc.sbuf_tensor(f"{name}_{n}", s, d))
        small_in = sb("small_in", [P, KD, S_COLS])
        swapped = sb("swapped", [P, 2, G])
        x_in = [sem(f"x_in_{s}") for s in range(NG)]
        const_in, small_read, others_in, small_hi, small_lo = sem("const_in"), sem("small_read"), sem("others_in"), sem("small_hi"), sem("small_lo")
        half_set, wr_zero = sem("half_set"), sem("wr_zero")
        q1_ready, q2_ready, keys_ready = sem("q1_ready"), sem("q2_ready"), sem("keys_ready")
        q1_hi, q1_lo, q2_hi, q2_lo = sem("q1_hi"), sem("q1_lo"), sem("q2_hi"), sem("q2_lo")
        rope_read, swap_done, sin_done, rotated = sem("rope_read"), sem("swap_done"), sem("sin_done"), sem("rotated")
        keys_hi, keys_lo, turned, values_done = sem("keys_hi"), sem("keys_lo"), sem("turned"), sem("values_done")
        fold_ready, fold_hi = sem("fold_ready"), sem("fold_hi")
        norm, norm_banks = norm_signals(nc, ctx, c, "norm1"), [c.ps[:, 0, :], c.ps[:, 1, :]]
        Q1, Q2 = c.ps[:, 2, :], c.ps[:, 3, :]
        KEYS = lambda s: c.ps[:, 4 + s % 2, :]
        TURNED = lambda s: c.ps[:, 6 + s % 2, 0:TG * KVR]
        slot = lambda s: slice(s * G, (s + 1) * G)
        block = ctx.enter_context(nc.Block())

        @block.sync
        def _(sp):
            tiles = lambda s: slice(s * TG, (s + 1) * TG)
            rows = x.rearrange("(t p) d -> p t d", p=P)
            sp.dma_start(c.x[:, tiles(0), :], rows[:, tiles(0), :]).then_inc(x_in[0], 16)
            sp.dma_start(c.const[:], const).then_inc(const_in, 16)
            sp.dma_start(c.x[:, tiles(1), :], rows[:, tiles(1), :]).then_inc(x_in[1], 16)
            sp.dma_start(small_in[:], small).then_inc(small_read, 16)
            for s in range(2, NG):
                sp.dma_start(c.x[:, tiles(s), :], rows[:, tiles(s), :]).then_inc(x_in[s], 16)
            sp.dma_start(c.order[:], order.to_broadcast([P, E])).then_inc(others_in, 16)
            sp.dma_start(c.temperature[:], temperature.to_broadcast([P, 1])).then_inc(others_in, 16)
            sp.dma_start(stage[:], weights[0]).then_inc(stage_in, 16)

        @block.tensor
        def _(pe):
            def turn_rows(s):
                if s == 0:
                    pe.wait_ge(const_in, 16)
                norm_turn(nc, c, norm, pe, s, norm_banks)

            def project(s, parts):
                pe.wait_ge(norm.lo_done, KD * (s + 1))
                if s == 0:
                    pe.wait_ge(small_lo, 1)
                for m, out, read, count, ready in ((0, Q1, q1_lo, s, q1_ready), (1, Q2, q2_lo, s, q2_ready), (2, KEYS(s), swap_done, s - 1, keys_ready))[parts]:
                    after(pe, read, count)
                    col = slice(m * P, (m + 1) * P)
                    for k in range(KD):
                        ins = matmul3(nc, out, (c.sh[:, k, col], c.sl[:, k, col]), (c.xh[:, k, slot(s)], c.xl[:, k, slot(s)]), k == 0, k == KD - 1)
                    ins.then_inc(ready, 1)

            def turn_keys(s):
                pe.wait_ge(rope_read, s + 1)
                after(pe, values_done, s - 1)
                for i in range(TG):
                    t = s * TG + i
                    ins = nc.tensor.transpose(TURNED(s)[:, i * KVR:(i + 1) * KVR], a.keys[0:KVR, t * P:(t + 1) * P], c.ident[0:KVR, 0:KVR])
                ins.then_inc(turned, 1)

            turn_rows(0)
            project(0, slice(0, 2))
            turn_rows(1)
            project(0, slice(2, 3))
            for s in range(1, NG):
                if s + 1 < NG:
                    turn_rows(s + 1)
                project(s, slice(0, 3))
                turn_keys(s - 1)
            pe.wait_ge(stage_in, 16)
            pe.wait_ge(q2_lo, NG)
            for h, bank in ((0, Q1), (1, Q2)):
                fold_product(nc, bank, stage, h).then_inc(fold_ready, 1)
            turn_keys(NG - 1)

        @block.scalar
        def _(act):
            def split_small():
                act.wait_ge(small_read, 16)
                act.wait_ge(wr_zero, 1)
                nc.scalar.copy(c.sh[:], small_in[:, :, 0:S_WR])
                nc.scalar.copy(c.wr[:, :, 0:E], small_in[:, :, S_WR:S_WR + E]).then_inc(small_hi, 1)

            def queries(s):
                act.wait_ge(q1_ready, s + 1)
                nc.scalar.copy(a.q1h[:, slot(s)], Q1).then_inc(q1_hi, 1)
                act.wait_ge(q2_ready, s + 1)
                nc.scalar.copy(a.q2[:, slot(s)], Q2).then_inc(q2_hi, 1)
                act.wait_ge(rope_read, s + 1)
                after(act, rotated, s - 1)
                swap_a(nc, KEYS(s), swapped[:, s % 2, :]).then_inc(swap_done, 1)

            def keys_values(s):
                act.wait_ge(rotated, s + 1)
                nc.scalar.copy(a.kh[:, slot(s)], a.keys[:, slot(s)]).then_inc(keys_hi, 1)
                act.wait_ge(turned, s + 1)
                nc.scalar.copy(a.values[:, s * TG:(s + 1) * TG, :], TURNED(s).rearrange("p (t d) -> p t d", d=KVR)).then_inc(values_done, 1)

            norm_hi(nc, c, norm, act, 0, norm_banks)
            split_small()
            for s in range(NG):
                if s + 1 < NG:
                    norm_hi(nc, c, norm, act, s + 1, norm_banks)
                queries(s)
                if s >= 1:
                    keys_values(s - 1)
            for h, bank in ((0, Q1), (1, Q2)):
                act.wait_ge(fold_ready, h + 1)
                fold_upper(nc, bank, stage, a.wh, h).then_inc(fold_hi, 1)
            keys_values(NG - 1)
            nc.scalar.copy(c.ident16[:], c.const[:, C_IDENT:C_IDENT + P])
            nc.scalar.copy(c.mask16[:], c.const[:, C_MASK:C_MASK + P])

        @block.vector
        def _(dve):
            def stats(s):
                dve.wait_ge(x_in[s], 16)
                norm_stats(nc, c, norm, dve, s)

            def split_small():
                dve.wait_ge(small_hi, 1)
                nc.vector.tensor_tensor(c.sl[:], small_in[:, :, 0:S_WR], c.sh[:].bitcast(F32), ALU.subtract)
                nc.vector.tensor_tensor(c.wr[:, :, E:2 * E], small_in[:, :, S_WR:S_WR + E], c.wr[:, :, 0:E].bitcast(F32), ALU.subtract).then_inc(small_lo, 1)

            def queries(s):
                dve.wait_ge(q1_hi, s + 1)
                nc.vector.tensor_tensor(a.q1l[:, slot(s)], Q1, a.q1h[:, slot(s)].bitcast(F32), ALU.subtract).then_inc(q1_lo, 1)
                dve.wait_ge(q2_hi, s + 1)
                nc.vector.tensor_tensor(a.q2[64:128, slot(s)], Q2[64:128], a.q2[64:128, slot(s)].bitcast(F32), ALU.subtract).then_inc(q2_lo, 1)
                dve.wait_ge(keys_ready, s + 1)
                times_table(nc.vector, c, a.keys[:, slot(s)], KEYS(s), ALL_ROWS, C_COSA).then_inc(rope_read, 1)

            nc.vector.memset(c.minus_half[:], -0.5).then_inc(half_set, 1)
            nc.vector.memset(c.wr[:].bitcast(F32), 0.0).then_inc(wr_zero, 1)
            stats(0)
            norm_rows(nc, c, norm, dve, 0)
            stats(1)
            norm_lo(nc, c, norm, dve, 0, norm_banks)
            split_small()
            norm_rows(nc, c, norm, dve, 1)
            for s in range(NG):
                if s + 2 < NG:
                    stats(s + 2)
                if s + 1 < NG:
                    norm_lo(nc, c, norm, dve, s + 1, norm_banks)
                if s + 2 < NG:
                    norm_rows(nc, c, norm, dve, s + 2)
                queries(s)
            dve.wait_ge(others_in, 32)
            nc.vector.reciprocal(c.inv_temperature[:], c.temperature[:])
            for h, bank in ((0, Q1), (1, Q2)):
                dve.wait_ge(fold_hi, h + 1)
                fold_lower(nc, bank, stage, a.wh, a.wl, h)
            dve.wait_ge(keys_hi, NG)
            keys_lo_parts(nc.vector, c, a, slot(NG - 1))

        @block.gpsimd
        def _(pool):
            def rotate(s):
                pool.wait_ge(swap_done, s + 1)
                after(pool, keys_lo, s - 1)
                rows = swapped[64:128, s % 2, :]
                times_table(nc.gpsimd, c, rows, rows, ROT_ROWS, C_SINA).then_inc(sin_done, 1)
                pool.wait_ge(sin_done, s + 1)
                pool.wait_ge(rope_read, s + 1)
                nc.gpsimd.tensor_tensor(a.keys[64:128, slot(s)], a.keys[64:128, slot(s)], swapped[64:128, s % 2, :], ALU.add).then_inc(rotated, 1)

            pool.wait_ge(half_set, 1)
            norm_rstd(nc, c, norm, pool, 0)
            norm_rstd(nc, c, norm, pool, 1)
            for s in range(NG):
                if s + 2 < NG:
                    norm_rstd(nc, c, norm, pool, s + 2)
                    pool.wait_ge(norm.rstd_done, s + 3)
                rotate(s)
                pool.wait_ge(rotated, s + 1)
                if s >= 1:
                    pool.wait_ge(keys_hi, s)
                    keys_lo_parts(nc.gpsimd, c, a, slot(s - 1)).then_inc(keys_lo, 1)


def keys_lo_parts(engine, c, a, slot):
    return engine.tensor_tensor(a.kl[:, slot], a.keys[:, slot], a.kh[:, slot].bitcast(F32), ALU.subtract)


def fold_product(nc, bank, stage, h):
    r = slice(64 * h, 64 * h + 64)
    for m in range(2):
        ins = nc.tensor.matmul(bank[:, m * KVR:(m + 1) * KVR], stage[r, A_PASS + m * P:A_PASS + (m + 1) * P], stage[r, A_K:A_K + KVR], start=True, stop=True)
    return ins


def fold_parts(bank, stage, w, h):
    rot = stage[:, A_ROT:A_ROT + 4 * ROT].rearrange("p (m h d) -> p m h d", m=2, h=2)
    return ((w[:, :, h, 0:KVR], bank[:, 0:2 * KVR].rearrange("p (m d) -> p m d", m=2)), (w[:, :, h, KVR:P], rot[:, :, h]))


def fold_upper(nc, bank, stage, wh, h):
    for upper, source in fold_parts(bank, stage, wh, h):
        ins = nc.scalar.copy(upper, source)
    return ins


def fold_lower(nc, bank, stage, wh, wl, h):
    for (upper, source), (lower, _) in zip(fold_parts(bank, stage, wh, h), fold_parts(bank, stage, wl, h)):
        ins = nc.vector.tensor_tensor(lower, source, upper.bitcast(F32), ALU.subtract)
    return ins


def fetch(sp, ahead):
    for buffer, source, signal in ahead:
        sp.dma_start(buffer, source).then_inc(signal, 16)


ALL_ROWS, ROT_ROWS = slice(0, P), slice(64, P)


def by_batch(ap):
    return ap.rearrange("p (b t) -> p b t", t=T)


def table(c, rows, col):
    return c.const[rows, col:col + T].unsqueeze(1).to_broadcast([rows.stop - rows.start, BG, T])


def swap_a(nc, src, swapped):
    nc.scalar.copy(swapped[64:96], src[96:128])
    return nc.scalar.copy(swapped[96:128], src[64:96])


def swap_b(nc, src, swapped):
    nc.scalar.copy(swapped[0:64], src[64:128])
    return nc.scalar.copy(swapped[64:128], src[0:64])


def times_table(engine, c, out, src, rows, col):
    return engine.tensor_tensor(by_batch(out), by_batch(src), table(c, rows, col), ALU.mult)


def after(engine, semaphore, count):
    if not isinstance(count, int) or count > 0:
        engine.wait_ge(semaphore, count)


PAIRS = 4


def moved(it, s, j, by):
    at = PAIRS * s + j + by
    return it + at // (PAIRS * NG), at // PAIRS % NG, at % PAIRS


def attention_a(nc, c, name, a, weights, stage, stage_in, norm, ahead):
    with ExitStack() as ctx:
        sem = lambda n: ctx.enter_context(nc.semaphore(f"{name}_{n}"))
        sb = lambda n, s, d=F32: ctx.enter_context(nc.sbuf_tensor(f"{name}_{n}", s, d))
        wh, wl = a.wh, a.wl
        woh, wol = sb("woh", [P, D], F32R), sb("wol", [P, D], F32R)
        raw = sb("raw", [P, 2, G])
        qh, ql = sb("qh", [P, 2, 2, G], F32R), sb("ql", [P, 2, 2, G], F32R)
        swapped = sb("swapped", [P, 2, G])
        negmax, total, inv = (sb(n, [P, PAIRS, 2]) for n in ("negmax", "total", "inv"))
        probs = sb("probs", [P, PAIRS, 2, T])
        probsT = sb("probsT", [P, 2, 2, T])
        mh, ml = sb("mh", [P, 2, G], F32R), sb("ml", [P, 2, G], F32R)
        fold_ready, fold_hi, fold_lo = sem("fold_ready"), sem("fold_hi"), sem("fold_lo")
        wo_ready, wo_hi, wo_lo = sem("wo_ready"), sem("wo_hi"), sem("wo_lo")
        proj_ready, rope_read, rotated, q_hi, q_lo = sem("proj_ready"), sem("rope_read"), sem("rotated"), sem("q_hi"), sem("q_lo")
        scores_ready, maxed, exp_done, inv_done, scaled = sem("scores_ready"), sem("maxed"), sem("exp_done"), sem("inv_done"), sem("scaled")
        turned, probsT_done, pv_done, mix_hi, mix_lo = sem("turned"), sem("probsT_done"), sem("pv_done"), sem("mix_hi"), sem("mix_lo")
        out_ready, out_added, swap_done, sin_done = sem("out_ready"), sem("out_added"), sem("swap_done"), sem("sin_done")
        S = lambda j: c.ps[:, j % 2, :]
        TURN = c.ps[:, 2, :]
        PROJ = lambda h: c.ps[:, 3 + h, :]
        MIX = lambda s: c.ps[:, 5 + s % 2, :]
        OUT = c.ps[:, 7, :]
        folded_out = OUT[:, 0:D]
        LAST = (HP - 1, NG - 1, PAIRS - 1)
        slot_no = lambda it, s: it * NG + s
        pair_no = lambda it, s, j: (it * NG + s) * PAIRS + j
        norm_banks = [PROJ(0), PROJ(1)]
        block = ctx.enter_context(nc.Block())

        @block.sync
        def _(sp):
            fetch(sp, ahead)
            with sp.Fori(1, HP) as it:
                sp.wait_ge(wo_ready, it)
                sp.dma_start(stage[:], weights[bass.ds(it, 1)].squeeze(0)).then_inc(stage_in, 16)

        @block.tensor
        def _(pe):
            def fold_query(it, h):
                if h == 0:
                    pe.wait_ge(stage_in, 16 * (it + 1))
                after(pe, rope_read, 2 * NG * it + h - 1)
                after(pe, swap_done, 2 * NG * it + h - 1)
                fold_product(nc, PROJ(h), stage, h).then_inc(fold_ready, 1)

            def fold_output(it):
                after(pe, out_added, 2 * NG * it)
                for h in range(2):
                    ins = nc.tensor.matmul(folded_out[64 * h:64 * h + 64], stage[:, A_V + h * KVR:A_V + (h + 1) * KVR], stage[:, A_O + h * D:A_O + (h + 1) * D], start=True, stop=True)
                ins.then_inc(wo_ready, 1)

            def project(it, s, h):
                if s == 0:
                    after(pe, fold_lo, 2 * it + h - 1)
                after(pe, rope_read, 2 * slot_no(it, s) + h - 1)
                after(pe, swap_done, 2 * slot_no(it, s) + h - 1)
                g = slice(s * G, (s + 1) * G)
                out = PROJ(h)
                nc.tensor.matmul(out, wl[:, 0, h, :], a.q1h[:, g], start=True, stop=False)
                nc.tensor.matmul(out, wh[:, 0, h, :], a.q1l[:, g], start=False, stop=False)
                nc.tensor.matmul(out, wl[:, 1, h, :], a.q2[:, g], start=False, stop=False)
                nc.tensor.matmul(out, wh[:, 1, h, :], a.q2[:, g], start=False, stop=False)
                nc.tensor.matmul(out, wh[:, 0, h, :], a.q1h[:, g], start=False, stop=True).then_inc(proj_ready, 1)

            def scores(it, s, j):
                g = pair_no(it, s, j)
                h, b = j // 2, j % 2
                if b == 0:
                    pe.wait_ge(q_lo, 2 * slot_no(it, s) + h + 1)
                after(pe, exp_done, g - 1)
                keys = slice(s * G + b * T, s * G + (b + 1) * T)
                for q in range(2):
                    rows = slice(b * T + q * P, b * T + (q + 1) * P)
                    ins = matmul3(nc, S(j)[:, q * T:(q + 1) * T], (qh[:, s % 2, h, rows], ql[:, s % 2, h, rows]), (a.kh[:, keys], a.kl[:, keys]), True, True)
                ins.then_inc(scores_ready, 1)

            def turn(it, s, j):
                g = pair_no(it, s, j)
                pe.wait_ge(scaled, g + 1)
                after(pe, probsT_done, g)
                for q in range(2):
                    for k in range(2):
                        ins = nc.tensor.transpose(TURN[:, k * T + q * P:k * T + (q + 1) * P], probs[:, j, q, k * P:(k + 1) * P], c.ident)
                ins.then_inc(turned, 1)

            def mix(it, s, j):
                g = pair_no(it, s, j)
                h, b = j // 2, j % 2
                pe.wait_ge(probsT_done, g + 1)
                if j == 0:
                    after(pe, mix_lo, slot_no(it, s) - 1)
                for k in range(2):
                    ins = nc.tensor.matmul(MIX(s)[64 * h:64 * h + 64, b * T:(b + 1) * T], a.values[:, s * TG + b * 2 + k, :], probsT[:, j % 2, k, :], start=(k == 0), stop=(k == 1))
                ins.then_inc(pv_done, 1)

            def output(it, s, i, bank=OUT):
                n = slot_no(it, s)
                if i == 0:
                    pe.wait_ge(mix_lo, n + 1)
                    if s == 0:
                        pe.wait_ge(wo_lo, it + 1)
                if bank is OUT:
                    after(pe, out_added, 2 * n + i)
                else:
                    pe.wait_ge(exp_done, PAIRS * NG * HP)
                for t in range(2):
                    tok = slice((2 * i + t) * P, (2 * i + t + 1) * P)
                    ins = matmul3(nc, bank[:, t * D:(t + 1) * D], (mh[:, s % 2, tok], ml[:, s % 2, tok]), (woh[:], wol[:]), True, True)
                ins.then_inc(out_ready, 1)

            def step(it, s, j):
                first, last = it == 0 if isinstance(it, int) else False, it == HP - 1 if isinstance(it, int) else False
                if not (last and s == NG - 1 and j >= 2):
                    scores(*moved(it, s, j, 2))
                turn(it, s, j)
                if not (first and s == 0 and j == 0):
                    mix(*moved(it, s, j, -1))
                if j == 0 and not (first and s <= 1):
                    output(*moved(it, s, 0, -2 * PAIRS)[:2], 1)
                if j == 2 and not (first and s == 0):
                    output(*moved(it, s, 0, -PAIRS)[:2], 0)
                if j in (1, 3) and not (last and s >= NG - 2):
                    project(*moved(it, s, 0, 2 * PAIRS)[:2], j // 2)
                if s == 1 and j == 3 and not last:
                    fold_query(it + 1, 0)
                if s == 2 and j == 1 and not last:
                    fold_query(it + 1, 1)
                if s == 1 and j == 1:
                    fold_output(it)
                if last and s == 3 and j == 0:
                    pe.wait_ge(swap_done, 2 * NG * HP)
                    norm_turn(nc, c, norm, pe, 0, norm_banks)

            def head_pair(it):
                for s in range(NG):
                    for j in range(PAIRS):
                        step(it, s, j)

            project(0, 0, 0)
            project(0, 0, 1)
            project(0, 1, 0)
            project(0, 1, 1)
            scores(0, 0, 0)
            scores(0, 0, 1)
            head_pair(0)
            with pe.Fori(1, HP - 1) as it:
                head_pair(it)
            head_pair(HP - 1)
            mix(*LAST)
            output(HP - 1, NG - 2, 1)
            norm_turn(nc, c, norm, pe, 1, norm_banks)
            output(HP - 1, NG - 1, 0, S(0))
            output(HP - 1, NG - 1, 1, S(1))
            norm_turn(nc, c, norm, pe, 2, norm_banks)

        @block.scalar
        def _(act):
            def fold_query(it, h):
                act.wait_ge(fold_ready, 2 * it + h - 1)
                fold_upper(nc, PROJ(h), stage, wh, h).then_inc(fold_hi, 1)

            def fold_output(it):
                act.wait_ge(wo_ready, it + 1)
                nc.scalar.copy(woh[:], folded_out).then_inc(wo_hi, 1)

            def swap(it, s, h):
                m = 2 * slot_no(it, s) + h
                act.wait_ge(rope_read, m + 1)
                after(act, rotated, m - 1)
                swap_a(nc, PROJ(h), swapped[:, h, :]).then_inc(swap_done, 1)

            def query_hi(it, s, h):
                n = slot_no(it, s)
                act.wait_ge(rotated, 2 * n + h + 1)
                after(act, scores_ready, PAIRS * (n - 2) + 2 * h + 2)
                nc.scalar.copy(qh[:, s % 2, h, :], raw[:, h, :]).then_inc(q_hi, 1)

            def exps(it, s, j):
                g = pair_no(it, s, j)
                act.wait_ge(maxed, g + 1)
                after(act, turned, g - PAIRS + 1)
                for q in range(2):
                    ins = nc.scalar.activation(probs[:, j, q, :], S(j)[:, q * T:(q + 1) * T], ACT.Exp, bias=negmax[:, j, q:q + 1], accum_out=total[:, j, q:q + 1])
                ins.then_inc(exp_done, 1)

            def take_turned(it, s, j):
                g = pair_no(it, s, j)
                act.wait_ge(turned, g + 1)
                after(act, pv_done, g - 1)
                nc.scalar.copy(probsT[:, j % 2].rearrange("p k t -> p (k t)"), TURN).then_inc(probsT_done, 1)

            def mixed_hi(it, s):
                n = slot_no(it, s)
                act.wait_ge(pv_done, PAIRS * (n + 1))
                after(act, out_ready, 2 * (n - 1))
                nc.scalar.copy(mh[:, s % 2, :], MIX(s)).then_inc(mix_hi, 1)

            def step(it, s, j):
                first, last = it == 0 if isinstance(it, int) else False, it == HP - 1 if isinstance(it, int) else False
                take_turned(it, s, j)
                if s == 2 and j in (0, 2) and not last:
                    fold_query(it + 1, j // 2)
                if j == 1 and not (first and s == 0):
                    mixed_hi(*moved(it, s, 0, -PAIRS)[:2])
                if j == 2 and not (last and s == NG - 1):
                    query_hi(*moved(it, s, 0, PAIRS)[:2], 1)
                if not (last and s == NG - 1 and j >= 2):
                    exps(*moved(it, s, j, 2))
                if j == 0 and not (last and s == NG - 1):
                    query_hi(*moved(it, s, 0, PAIRS)[:2], 0)
                if j == 0 and not (last and s == NG - 1):
                    swap(*moved(it, s, 0, PAIRS)[:2], 1)
                if last and s == 3 and j == 0:
                    norm_hi(nc, c, norm, act, 0, norm_banks)
                if j == 1 and s == 1:
                    fold_output(it)
                if j == 2 and not (last and s >= NG - 2):
                    swap(*moved(it, s, 0, 2 * PAIRS)[:2], 0)

            def head_pair(it):
                for s in range(NG):
                    for j in range(PAIRS):
                        step(it, s, j)

            swap(0, 0, 0)
            query_hi(0, 0, 0)
            swap(0, 0, 1)
            query_hi(0, 0, 1)
            swap(0, 1, 0)
            exps(0, 0, 0)
            exps(0, 0, 1)
            head_pair(0)
            with act.Fori(1, HP - 1) as it:
                head_pair(it)
            head_pair(HP - 1)
            mixed_hi(HP - 1, NG - 1)
            for s in range(1, NG - 1):
                norm_hi(nc, c, norm, act, s, norm_banks)

        @block.vector
        def _(dve):
            def fold_query(it, h):
                dve.wait_ge(fold_hi, 2 * it + h - 1)
                fold_lower(nc, PROJ(h), stage, wh, wl, h).then_inc(fold_lo, 1)

            def fold_output(it):
                dve.wait_ge(wo_hi, it + 1)
                nc.vector.tensor_tensor(wol[:], folded_out, woh[:].bitcast(F32), ALU.subtract).then_inc(wo_lo, 1)

            def rope(it, s, h):
                m = 2 * slot_no(it, s) + h
                dve.wait_ge(proj_ready, m + 1)
                after(dve, q_lo, m - 1)
                times_table(nc.vector, c, raw[:, h, :], PROJ(h), ALL_ROWS, C_COSA).then_inc(rope_read, 1)

            def row_max(it, s, j):
                dve.wait_ge(scores_ready, pair_no(it, s, j) + 1)
                nc.vector.tensor_reduce(negmax[:, j, :], S(j).rearrange("p (q t) -> p q t", q=2), AX, ALU.max, negate=True).then_inc(maxed, 1)

            def scale(it, s, j):
                g = pair_no(it, s, j)
                dve.wait_ge(exp_done, g + 1)
                nc.vector.reciprocal(inv[:, j, :], total[:, j, :]).then_inc(inv_done, 1)
                dve.wait_ge(inv_done, g + 1)
                for q in range(2):
                    ins = nc.vector.tensor_scalar(probs[:, j, q, :], probs[:, j, q, :], inv[:, j, q:q + 1], None, ALU.mult)
                ins.then_inc(scaled, 1)

            def mixed_lo(it, s):
                n = slot_no(it, s)
                dve.wait_ge(mix_hi, n + 1)
                nc.vector.tensor_tensor(ml[:, s % 2, :], MIX(s), mh[:, s % 2, :].bitcast(F32), ALU.subtract).then_inc(mix_lo, 1)

            def add_out(it, s, i, bank=OUT):
                dve.wait_ge(out_ready, 2 * slot_no(it, s) + i + 1)
                t = s * TG + 2 * i
                nc.vector.tensor_tensor(c.x[:, t:t + 2, :], bank.rearrange("p (t d) -> p t d", d=D), c.x[:, t:t + 2, :], ALU.add).then_inc(out_added, 1)

            def step(it, s, j):
                first, last = it == 0 if isinstance(it, int) else False, it == HP - 1 if isinstance(it, int) else False
                if j == 1 and not (first and s <= 1):
                    add_out(*moved(it, s, 0, -2 * PAIRS)[:2], 1)
                if not (last and s == NG - 1 and j >= 2):
                    row_max(*moved(it, s, j, 2))
                if not (last and s == NG - 1 and j == 3):
                    scale(*moved(it, s, j, 1))
                if s == 2 and j in (0, 2) and not last:
                    fold_query(it + 1, j // 2)
                if j == 0 and not (last and s == NG - 1):
                    rope(*moved(it, s, 0, PAIRS)[:2], 1)
                if j == 2 and not (last and s >= NG - 2):
                    rope(*moved(it, s, 0, 2 * PAIRS)[:2], 0)
                if j == 3 and not (first and s == 0):
                    add_out(*moved(it, s, 0, -PAIRS)[:2], 0)
                if j == 1 and not (first and s == 0):
                    mixed_lo(*moved(it, s, 0, -PAIRS)[:2])
                if s == 1 and j == 1:
                    fold_output(it)
                if last and s >= 2 and j == 2:
                    normalise_stats(s - 2)
                if last and s >= 2 and j == 3:
                    norm_rows(nc, c, norm, dve, s - 2)
                if last and s == 3 and j == 1:
                    norm_lo(nc, c, norm, dve, 0, norm_banks)

            def normalise_stats(s):
                dve.wait_ge(out_added, 2 * slot_no(HP - 1, s) + 2)
                norm_stats(nc, c, norm, dve, s)

            def head_pair(it):
                for s in range(NG):
                    for j in range(PAIRS):
                        step(it, s, j)

            rope(0, 0, 0)
            rope(0, 0, 1)
            rope(0, 1, 0)
            row_max(0, 0, 0)
            scale(0, 0, 0)
            row_max(0, 0, 1)
            head_pair(0)
            with dve.Fori(1, HP - 1) as it:
                head_pair(it)
            head_pair(HP - 1)
            add_out(HP - 1, NG - 2, 1)
            mixed_lo(HP - 1, NG - 1)
            normalise_stats(NG - 2)
            norm_lo(nc, c, norm, dve, 1, norm_banks)
            norm_rows(nc, c, norm, dve, NG - 2)
            add_out(HP - 1, NG - 1, 0, S(0))
            add_out(HP - 1, NG - 1, 1, S(1))
            normalise_stats(NG - 1)
            norm_lo(nc, c, norm, dve, NG - 2, norm_banks)

        @block.gpsimd
        def _(pool):
            def finish_queries(n, s, h):
                pool.wait_ge(swap_done, 2 * n + h + 1)
                rows, other = raw[64:128, h, :], swapped[64:128, h, :]
                times_table(nc.gpsimd, c, other, other, ROT_ROWS, C_SINA).then_inc(sin_done, 1)
                pool.wait_ge(sin_done, 2 * n + h + 1)
                pool.wait_ge(rope_read, 2 * n + h + 1)
                nc.gpsimd.tensor_tensor(rows, rows, other, ALU.add).then_inc(rotated, 1)
                pool.wait_ge(q_hi, 2 * n + h + 1)
                nc.gpsimd.tensor_tensor(ql[:, s % 2, h, :], raw[:, h, :], qh[:, s % 2, h, :].bitcast(F32), ALU.subtract).then_inc(q_lo, 1)
                pool.wait_ge(q_lo, 2 * n + h + 1)

            with pool.Fori(0, HP) as it:
                for s in range(NG):
                    for h in range(2):
                        finish_queries(it * NG + s, s, h)
            for s in range(NG):
                norm_rstd(nc, c, norm, pool, s)


def attention_b(nc, c, name, w_qkv, w_out, stage, wo_stage, stage_in, wo_in, own_norm, norm, ahead):
    W = T + P
    with ExitStack() as ctx:
        sem = lambda n: ctx.enter_context(nc.semaphore(f"{name}_{n}"))
        sb = lambda n, s, d=F32: ctx.enter_context(nc.sbuf_tensor(f"{name}_{n}", s, d))
        wh, wl = sb("wh", [P, 3, KD, 2 * P], F32R), sb("wl", [P, 3, KD, 2 * P], F32R)
        woh, wol = sb("woh", [P, 2, D], F32R), sb("wol", [P, 2, D], F32R)
        qk = sb("qk", [P, 2, 4, G])
        swapped = sb("swapped", [P, 2, G])
        values = sb("values", [P, 2, TG, 2 * P])
        negmax, total, inv = (sb(n, [P, PAIRS, 2]) for n in ("negmax", "total", "inv"))
        probs, probsT = sb("probs", [P, PAIRS, W]), sb("probsT", [P, 2, W])
        mh, ml = sb("mh", [P, 2, 2, G], F32R), sb("ml", [P, 2, 2, G], F32R)
        w_hi, w_lo, wo_hi, wo_lo = sem("w_hi"), sem("w_lo"), sem("wo_hi"), sem("wo_lo")
        proj_ready, rope_read, rotated, values_done = sem("proj_ready"), sem("rope_read"), sem("rotated"), sem("values_done")
        scores_ready, maxed, exp_done, inv_done, scaled = sem("scores_ready"), sem("maxed"), sem("exp_done"), sem("inv_done"), sem("scaled")
        turned, probsT_done, pv_done, mix_hi, mix_lo = sem("turned"), sem("probsT_done"), sem("pv_done"), sem("mix_hi"), sem("mix_lo")
        vproj_ready, out_ready, out_added = sem("vproj_ready"), sem("out_ready"), sem("out_added")
        swap_done, sin_done = sem("swap_done"), sem("sin_done")
        S = lambda j: c.ps[:, j % 2, :]
        TURN = c.ps[:, 2, 0:W]
        PROJ = lambda i: c.ps[:, 3 + i % 2, :]
        MIX = lambda h: c.ps[:, 5 + h, :]
        OUT = c.ps[:, 7, :]
        span = [slice(0, P), slice(P, W)]
        flat = lambda w: w.rearrange("p a k d -> p (a k d)")
        parts = [slice(0, 2), slice(2, 3)]
        LAST = (HP - 1, NG - 1, PAIRS - 1)
        slot_no = lambda it, s: it * NG + s
        pair_no = lambda it, s, j: (it * NG + s) * PAIRS + j
        norm_banks = [PROJ(0), PROJ(1)]
        own_banks = [MIX(1), OUT]
        block = ctx.enter_context(nc.Block())

        @block.sync
        def _(sp):
            fetch(sp, ahead)
            with sp.Fori(1, HP) as it:
                sp.wait_ge(w_lo, 2 * it)
                sp.dma_start(stage[:], w_qkv[bass.ds(it, 1)].squeeze(0)).then_inc(stage_in, 16)
                sp.wait_ge(wo_lo, it)
                sp.dma_start(wo_stage[:], w_out[bass.ds(it, 1)].squeeze(0)).then_inc(wo_in, 16)

        @block.tensor
        def _(pe):
            def project(it, s, i):
                n = slot_no(it, s)
                if i == 0 and s == 0:
                    pe.wait_ge(w_lo, 2 * it + 1)
                if i >= 2:
                    pe.wait_ge(rope_read, 4 * n + i - 1)
                    pe.wait_ge(swap_done, 4 * n + i - 1)
                else:
                    after(pe, values_done, 2 * n + i - 1)
                col = slice((i // 2) * P, (i // 2) * P + P)
                g = slice(s * G, (s + 1) * G)
                for k in range(KD):
                    ins = matmul3(nc, PROJ(i), (wh[:, i % 2, k, col], wl[:, i % 2, k, col]), (c.xh[:, k, g], c.xl[:, k, g]), k == 0, k == KD - 1)
                ins.then_inc(proj_ready, 1)

            def project_values(it, s, i):
                n = slot_no(it, s)
                if i == 0 and s == 0:
                    pe.wait_ge(w_lo, 2 * it + 2)
                pe.wait_ge(rope_read, 4 * n + 3 + i)
                pe.wait_ge(swap_done, 4 * n + 3 + i)
                for t in range(2):
                    tok = slice(s * G + (2 * i + t) * P, s * G + (2 * i + t + 1) * P)
                    for k in range(KD):
                        ins = matmul3(nc, PROJ(i)[:, t * 2 * P:(t + 1) * 2 * P], (c.xh[:, k, tok], c.xl[:, k, tok]), (wh[:, 2, k, :], wl[:, 2, k, :]), k == 0, k == KD - 1)
                ins.then_inc(vproj_ready, 1)

            def scores(it, s, j):
                g = pair_no(it, s, j)
                h, b = j // 2, j % 2
                if b == 0:
                    pe.wait_ge(rotated, 4 * slot_no(it, s) + 2 * h + 2)
                after(pe, exp_done, g - 1)
                for q in range(2):
                    out = S(j)[:, span[q]]
                    nc.tensor.matmul(out, qk[:, s % 2, 2 * h, b * T + q * P:b * T + (q + 1) * P], qk[:, s % 2, 2 * h + 1, b * T:b * T + (q + 1) * P], start=True, stop=False)
                    ins = nc.tensor.matmul(out[:, q * P:(q + 1) * P], c.ident16[:], c.mask16[:], start=False, stop=True)
                ins.then_inc(scores_ready, 1)

            def turn(it, s, j):
                g = pair_no(it, s, j)
                pe.wait_ge(scaled, g + 1)
                after(pe, probsT_done, g)
                for i in range(3):
                    ins = nc.tensor.transpose(TURN[:, i * P:(i + 1) * P], probs[:, j, i * P:(i + 1) * P], c.ident)
                ins.then_inc(turned, 1)

            def mix(it, s, j):
                n, g = slot_no(it, s), pair_no(it, s, j)
                h, b = j // 2, j % 2
                pe.wait_ge(probsT_done, g + 1)
                if j == 0:
                    pe.wait_ge(values_done, 2 * n + 2)
                if b == 0:
                    after(pe, mix_lo, 2 * n + h - 1)
                out = MIX(h)[:, b * T:(b + 1) * T]
                v = lambda k: values[:, s % 2, 2 * b + k, h * P:(h + 1) * P]
                nc.tensor.matmul(out, v(0), probsT[:, j % 2, 0:T], start=True, stop=False)
                nc.tensor.matmul(out[:, P:T], v(1), probsT[:, j % 2, T:W], start=False, stop=True).then_inc(pv_done, 1)

            def output(it, s, i, bank=OUT):
                n = slot_no(it, s)
                if i == 0:
                    pe.wait_ge(mix_lo, 2 * n + 2)
                    if s == 0:
                        pe.wait_ge(wo_lo, it + 1)
                if bank is OUT:
                    after(pe, out_added, 2 * n + i)
                else:
                    pe.wait_ge(exp_done, PAIRS * NG * HP)
                for t in range(2):
                    tok = slice((2 * i + t) * P, (2 * i + t + 1) * P)
                    for h in range(2):
                        ins = matmul3(nc, bank[:, t * D:(t + 1) * D], (mh[:, s % 2, h, tok], ml[:, s % 2, h, tok]), (woh[:, h, :], wol[:, h, :]), h == 0, h == 1)
                ins.then_inc(out_ready, 1)

            def step(it, s, j):
                first, last = it == 0 if isinstance(it, int) else False, it == HP - 1 if isinstance(it, int) else False
                if not (last and s == NG - 1 and j >= 2):
                    scores(*moved(it, s, j, 2))
                turn(it, s, j)
                if not (first and s == 0 and j == 0):
                    mix(*moved(it, s, j, -1))
                nxt = moved(it, s, 0, PAIRS)[:2]
                if j == 0 and not (last and s == NG - 1):
                    project(*nxt, 2)
                    project(*nxt, 3)
                if j in (1, 2) and not (last and s == NG - 1):
                    project_values(*nxt, j - 1)
                if j >= 2 and not (first and s == 0) and not (last and s == NG - 1 and j == 3):
                    output(*moved(it, s, 0, -PAIRS)[:2], j - 2)
                if j == 3 and not (last and s >= NG - 2):
                    project(*moved(it, s, 0, 2 * PAIRS)[:2], 0)
                    project(*moved(it, s, 0, 2 * PAIRS)[:2], 1)
                if last and s == 3 and j == 0:
                    pe.wait_ge(values_done, 2 * NG * HP)
                    norm_turn(nc, c, norm, pe, 0, norm_banks)

            def head_pair(it):
                for s in range(NG):
                    for j in range(PAIRS):
                        step(it, s, j)

            project(0, 0, 0)
            project(0, 0, 1)
            project(0, 0, 2)
            project(0, 0, 3)
            norm_turn(nc, c, own_norm, pe, 2, own_banks)
            project_values(0, 0, 0)
            project_values(0, 0, 1)
            norm_turn(nc, c, own_norm, pe, 3, own_banks)
            project(0, 1, 0)
            project(0, 1, 1)
            scores(0, 0, 0)
            scores(0, 0, 1)
            pe.wait_ge(own_norm.lo_done, KD * NG)
            head_pair(0)
            with pe.Fori(1, HP - 1) as it:
                head_pair(it)
            head_pair(HP - 1)
            mix(*LAST)
            output(HP - 1, NG - 2, 1)
            norm_turn(nc, c, norm, pe, 1, norm_banks)
            output(HP - 1, NG - 1, 0, S(0))
            output(HP - 1, NG - 1, 1, S(1))
            norm_turn(nc, c, norm, pe, 2, norm_banks)

        @block.scalar
        def _(act):
            def split_hi(it, part):
                act.wait_ge(stage_in, 16 * (it + 1))
                if part == 0:
                    after(act, proj_ready, 4 * NG * it)
                else:
                    after(act, vproj_ready, 2 * NG * it)
                nc.scalar.copy(flat(wh[:, parts[part]]), flat(stage[:, parts[part]])).then_inc(w_hi, 1)

            def split_wo(it):
                act.wait_ge(wo_in, 16 * (it + 1))
                after(act, out_ready, 2 * NG * it)
                nc.scalar.copy(woh[:], wo_stage[:]).then_inc(wo_hi, 1)

            def swap(it, s, i):
                m = 4 * slot_no(it, s) + i
                act.wait_ge(rope_read, m + 1)
                after(act, rotated, m - 1)
                swap_b(nc, PROJ(i), swapped[:, i % 2, :]).then_inc(swap_done, 1)

            def exps(it, s, j):
                g = pair_no(it, s, j)
                act.wait_ge(maxed, g + 1)
                after(act, turned, g - PAIRS + 1)
                for q in range(2):
                    ins = nc.scalar.activation(probs[:, j, span[q]], S(j)[:, span[q]], ACT.Exp, bias=negmax[:, j, q:q + 1], accum_out=total[:, j, q:q + 1])
                ins.then_inc(exp_done, 1)

            def take_turned(it, s, j):
                g = pair_no(it, s, j)
                act.wait_ge(turned, g + 1)
                after(act, pv_done, g - 1)
                nc.scalar.copy(probsT[:, j % 2, :], TURN).then_inc(probsT_done, 1)

            def take_values(it, s, i):
                n = slot_no(it, s)
                act.wait_ge(vproj_ready, 2 * n + i + 1)
                after(act, pv_done, PAIRS * (n - 1))
                nc.scalar.copy(values[:, s % 2, 2 * i:2 * i + 2, :], PROJ(i).rearrange("p (t d) -> p t d", t=2)).then_inc(values_done, 1)

            def mixed_hi(it, s, h):
                n = slot_no(it, s)
                act.wait_ge(pv_done, PAIRS * n + 2 * h + 2)
                after(act, out_ready, 2 * (n - 1))
                nc.scalar.copy(mh[:, s % 2, h, :], MIX(h)).then_inc(mix_hi, 1)

            def step(it, s, j):
                first, last = it == 0 if isinstance(it, int) else False, it == HP - 1 if isinstance(it, int) else False
                take_turned(it, s, j)
                if not (last and s == NG - 1 and j >= 2):
                    exps(*moved(it, s, j, 2))
                if j == 0 and not (first and s == 0):
                    mixed_hi(*moved(it, s, 0, -PAIRS)[:2], 1)
                if j == 0 and not (last and s == NG - 1):
                    swap(*moved(it, s, 0, PAIRS)[:2], 2)
                    swap(*moved(it, s, 0, PAIRS)[:2], 3)
                if j == 2:
                    mixed_hi(it, s, 0)
                if j in (1, 2) and not (last and s == NG - 1):
                    take_values(*moved(it, s, 0, PAIRS)[:2], j - 1)
                if j == 3 and not (last and s >= NG - 2):
                    swap(*moved(it, s, 0, 2 * PAIRS)[:2], 0)
                    swap(*moved(it, s, 0, 2 * PAIRS)[:2], 1)
                if s == NG - 2 and not last and j in (1, 3):
                    split_hi(it + 1, j // 2)
                if s == 0 and j == 3:
                    split_wo(it)
                if last and s == 3 and j == 0:
                    norm_hi(nc, c, norm, act, 0, norm_banks)

            def head_pair(it):
                for s in range(NG):
                    for j in range(PAIRS):
                        step(it, s, j)

            split_hi(0, 0)
            split_hi(0, 1)
            swap(0, 0, 0)
            swap(0, 0, 1)
            swap(0, 0, 2)
            swap(0, 0, 3)
            norm_hi(nc, c, own_norm, act, 2, own_banks)
            take_values(0, 0, 0)
            take_values(0, 0, 1)
            norm_hi(nc, c, own_norm, act, 3, own_banks)
            swap(0, 1, 0)
            swap(0, 1, 1)
            exps(0, 0, 0)
            exps(0, 0, 1)
            head_pair(0)
            with act.Fori(1, HP - 1) as it:
                head_pair(it)
            head_pair(HP - 1)
            mixed_hi(HP - 1, NG - 1, 1)
            for s in range(1, NG - 1):
                norm_hi(nc, c, norm, act, s, norm_banks)

        @block.vector
        def _(dve):
            def split_lo(it, part):
                dve.wait_ge(w_hi, 2 * it + part + 1)
                nc.vector.tensor_tensor(flat(wl[:, parts[part]]), flat(stage[:, parts[part]]), flat(wh[:, parts[part]]).bitcast(F32), ALU.subtract).then_inc(w_lo, 1)

            def split_wo(it):
                dve.wait_ge(wo_hi, it + 1)
                nc.vector.tensor_tensor(wol[:], wo_stage[:], woh[:].bitcast(F32), ALU.subtract).then_inc(wo_lo, 1)

            def rope(it, s, i):
                m = 4 * slot_no(it, s) + i
                dve.wait_ge(proj_ready, m + 1)
                times_table(nc.vector, c, qk[:, s % 2, i, :], PROJ(i), ALL_ROWS, C_COSB).then_inc(rope_read, 1)

            def row_max(it, s, j):
                dve.wait_ge(scores_ready, pair_no(it, s, j) + 1)
                for q in range(2):
                    ins = nc.vector.tensor_reduce(negmax[:, j, q:q + 1], S(j)[:, span[q]], AX, ALU.max, negate=True)
                ins.then_inc(maxed, 1)

            def scale(it, s, j):
                g = pair_no(it, s, j)
                dve.wait_ge(exp_done, g + 1)
                nc.vector.reciprocal(inv[:, j, :], total[:, j, :]).then_inc(inv_done, 1)
                dve.wait_ge(inv_done, g + 1)
                for q in range(2):
                    ins = nc.vector.tensor_scalar(probs[:, j, span[q]], probs[:, j, span[q]], inv[:, j, q:q + 1], None, ALU.mult)
                ins.then_inc(scaled, 1)

            def mixed_lo(it, s, h):
                n = slot_no(it, s)
                dve.wait_ge(mix_hi, 2 * n + h + 1)
                nc.vector.tensor_tensor(ml[:, s % 2, h, :], MIX(h), mh[:, s % 2, h, :].bitcast(F32), ALU.subtract).then_inc(mix_lo, 1)

            def add_out(it, s, i, bank=OUT):
                dve.wait_ge(out_ready, 2 * slot_no(it, s) + i + 1)
                t = s * TG + 2 * i
                nc.vector.tensor_tensor(c.x[:, t:t + 2, :], bank.rearrange("p (t d) -> p t d", d=D), c.x[:, t:t + 2, :], ALU.add).then_inc(out_added, 1)

            def step(it, s, j):
                first, last = it == 0 if isinstance(it, int) else False, it == HP - 1 if isinstance(it, int) else False
                if not (last and s == NG - 1 and j == 3):
                    scale(*moved(it, s, j, 1))
                if j == 0 and not (first and s <= 1):
                    add_out(*moved(it, s, 0, -2 * PAIRS)[:2], 1)
                if j == 3 and not (first and s == 0):
                    add_out(*moved(it, s, 0, -PAIRS)[:2], 0)
                if not (last and s == NG - 1 and j >= 2):
                    row_max(*moved(it, s, j, 2))
                if j == 0:
                    if not (last and s == NG - 1):
                        rope(*moved(it, s, 0, PAIRS)[:2], 2)
                        rope(*moved(it, s, 0, PAIRS)[:2], 3)
                    if s == NG - 1 and not last:
                        split_lo(it + 1, 1)
                if j == 1 and not (first and s == 0):
                    mixed_lo(*moved(it, s, 0, -PAIRS)[:2], 1)
                if s == NG - 2 and not last and j == 2:
                    split_lo(it + 1, 0)
                if j == 3:
                    mixed_lo(it, s, 0)
                    if last and s >= 2:
                        norm_rows(nc, c, norm, dve, s - 2)
                    if not (last and s >= NG - 2):
                        rope(*moved(it, s, 0, 2 * PAIRS)[:2], 0)
                        rope(*moved(it, s, 0, 2 * PAIRS)[:2], 1)
                if s == 1 and j == 0:
                    split_wo(it)
                if last and (s, j) in ((2, 1), (3, 1)):
                    normalise_stats(s - 2)
                if last and s == 3 and j == 1:
                    norm_lo(nc, c, norm, dve, 0, norm_banks)

            def normalise_stats(s):
                dve.wait_ge(out_added, 2 * slot_no(HP - 1, s) + 2)
                norm_stats(nc, c, norm, dve, s)

            def head_pair(it):
                for s in range(NG):
                    for j in range(PAIRS):
                        step(it, s, j)

            norm_stats(nc, c, own_norm, dve, 2)
            split_lo(0, 0)
            norm_rows(nc, c, own_norm, dve, 2)
            split_lo(0, 1)
            norm_stats(nc, c, own_norm, dve, 3)
            for i in range(4):
                rope(0, 0, i)
            norm_lo(nc, c, own_norm, dve, 2, own_banks)
            norm_rows(nc, c, own_norm, dve, 3)
            norm_lo(nc, c, own_norm, dve, 3, own_banks)
            rope(0, 1, 0)
            rope(0, 1, 1)
            row_max(0, 0, 0)
            row_max(0, 0, 1)
            scale(0, 0, 0)
            head_pair(0)
            with dve.Fori(1, HP - 1) as it:
                head_pair(it)
            head_pair(HP - 1)
            mixed_lo(HP - 1, NG - 1, 1)
            add_out(HP - 1, NG - 2, 1)
            normalise_stats(NG - 2)
            norm_lo(nc, c, norm, dve, 1, norm_banks)
            norm_rows(nc, c, norm, dve, NG - 2)
            add_out(HP - 1, NG - 1, 0, S(0))
            add_out(HP - 1, NG - 1, 1, S(1))
            normalise_stats(NG - 1)
            norm_lo(nc, c, norm, dve, NG - 2, norm_banks)

        @block.gpsimd
        def _(pool):
            norm_rstd(nc, c, own_norm, pool, 2)
            norm_rstd(nc, c, own_norm, pool, 3)
            pool.wait_ge(own_norm.rstd_done, NG)
            with pool.Fori(0, HP) as it:
                for s in range(NG):
                    for i in range(4):
                        m = 4 * (it * NG + s) + i
                        pool.wait_ge(swap_done, m + 1)
                        rows, other = qk[:, s % 2, i, :], swapped[:, i % 2, :]
                        times_table(nc.gpsimd, c, other, other, ALL_ROWS, C_SINB).then_inc(sin_done, 1)
                        pool.wait_ge(sin_done, m + 1)
                        pool.wait_ge(rope_read, m + 1)
                        nc.gpsimd.tensor_tensor(rows, rows, other, ALU.add).then_inc(rotated, 1)
            for s in range(NG):
                norm_rstd(nc, c, norm, pool, s)


def experts(nc, c, name, weights, stage, stage_in, own_norm, ahead=(), norm=None, result=None):
    with ExitStack() as ctx:
        sem = lambda n: ctx.enter_context(nc.semaphore(f"{name}_{n}"))
        sb = lambda n, s, d=F32: ctx.enter_context(nc.sbuf_tensor(f"{name}_{n}", s, d))
        flat_logits = sb("flat_logits", [2 * E, N])
        z, inh, dist, near, far = (sb(n, [P, NT, E]) for n in ("z", "inh", "dist", "near", "far"))
        lo_side, hi_side, part, place, rest = (sb(n, [P, NT, E]) for n in ("lo_side", "hi_side", "part", "place", "rest"))
        greatest, second = sb("greatest", [P, NT, E]), sb("second", [P, NT, E])
        wsum, none, some, most = (sb(n, [P, NT]) for n in ("wsum", "none", "some", "most"))
        gate = sb("gate", [P, NT, E])
        products_ready, flat_done, logits_ready = sem("products_ready"), sem("flat_done"), sem("logits_ready")
        chained, distances_exp = sem("chained"), sem("distances_exp")
        wh, wl = sb("wh", [P, 2, 3, KD, F], F32R), sb("wl", [P, 2, 3, KD, F], F32R)
        col = sb("col", [P, 2, NT])
        silu, hidden = sb("silu", [P, 2, G]), sb("hidden", [P, 2, G])
        hh, hl = sb("hh", [P, 2, 2, G], F32R), sb("hl", [P, 2, 2, G], F32R)
        w_hi, w_lo, col_done = sem("w_hi"), sem("w_lo"), sem("col_done")
        gated, silu_done, hid_done, hi_done, lo_done = sem("gated"), sem("silu_done"), sem("hid_done"), sem("hi_done"), sem("lo_done")
        out_ready, out_added, stored = sem("out_ready"), sem("out_added"), sem("stored")
        GATE = lambda m: c.ps[:, 2 * m, :]
        UP = lambda m: c.ps[:, 2 * m + 1, :]
        OUT = lambda i: c.ps[:, 4 + i, :].rearrange("p (t d) -> p t d", d=D)
        norm_banks, own_banks = [c.ps[:, 6, :], c.ps[:, 7, :]], [GATE(1), UP(1)]
        PRODUCTS = lambda s: c.ps[:, 4 + s, :]
        LOGITS = c.ps[:, 4, 0:NT * 2 * E].rearrange("p (t w) -> p t w", w=2 * E)
        TURNS = E // 2
        block = ctx.enter_context(nc.Block())
        flat = lambda w, e: w[:, e].rearrange("p a k d -> p (a k d)")


        @block.sync
        def _(sp):
            fetch(sp, ahead)
            with sp.Fori(1, TURNS) as it:
                for e in range(2):
                    sp.wait_ge(w_lo, 2 * it - 1 + e)
                    sp.dma_start(stage[:, e], weights[bass.ds(2 * it + e, 1)].squeeze(0)).then_inc(stage_in[e], 16)
            if result:
                out, stored = result
                for s in range(NG):
                    sp.wait_ge(out_added, 2 * (8 * (TURNS - 1) + 4 + s) + 2)
                    t = slice(s * TG, (s + 1) * TG)
                    sp.dma_start(out[:, t, :], c.x[:, t, :]).then_inc(stored[s], 16)
                for s in range(NG):
                    sp.wait_ge(stored[s], 16)

        if norm:
            @block.gpsimd
            def _(pool):
                for s in range(2):
                    norm_rstd(nc, c, norm, pool, s)

        @block.tensor
        def _(pe):
            def router_products():
                for s in range(NG):
                    if s == 1:
                        norm_turn(nc, c, own_norm, pe, NG - 1, own_banks)
                    if s == NG - 1:
                        pe.wait_ge(own_norm.lo_done, KD * NG)
                    g = slice(s * G, (s + 1) * G)
                    for k in range(KD):
                        nc.tensor.matmul(PRODUCTS(s), c.wr[:, k, :], c.xl[:, k, g], start=(k == 0), stop=False)
                        ins = nc.tensor.matmul(PRODUCTS(s), c.wr[:, k, :], c.xh[:, k, g], start=False, stop=(k == KD - 1))
                    ins.then_inc(products_ready, 1)

            def router_turn():
                pe.wait_ge(flat_done, NG)
                for t in range(NT):
                    ins = nc.tensor.transpose(LOGITS[:, t, :], flat_logits[:, t * P:(t + 1) * P], c.ident[0:2 * E, 0:2 * E])
                ins.then_inc(logits_ready, 1)

            def gate_up(it, e, s, first=False):
                n = 8 * it + 4 * e + s
                if s == 0:
                    pe.wait_ge(w_lo, 2 * it + e + 1)
                g = slice(s * G, (s + 1) * G)
                for m in range(2):
                    if not first:
                        pe.wait_ge(hid_done, 2 * n + m - 1)
                    f = slice(m * P, (m + 1) * P)
                    for a, out in ((0, GATE(m)), (1, UP(m))):
                        for k in range(KD):
                            ins = matmul3(nc, out, (wh[:, e, a, k, f], wl[:, e, a, k, f]), (c.xh[:, k, g], c.xl[:, k, g]), k == 0, k == KD - 1)
                        ins.then_inc(gated, 1)

            def down(it, e, s, first=False):
                n = 8 * it + 4 * e + s
                pe.wait_ge(lo_done, 2 * n + 2)
                if first:
                    pe.wait_ge(chained, 2)
                for i in range(2):
                    if not first:
                        pe.wait_ge(out_added, 2 * n + i - 1)
                    for t in range(2):
                        tok = slice((2 * i + t) * P, (2 * i + t + 1) * P)
                        for k in range(KD):
                            ins = matmul3(nc, OUT(i)[:, t, :], (hh[:, s % 2, k, tok], hl[:, s % 2, k, tok]), (wh[:, e, 2, k, :], wl[:, e, 2, k, :]), k == 0, k == KD - 1)
                    ins.then_inc(out_ready, 1)

            def turn(it, first, last):
                for e in range(2):
                    for s in range(NG):
                        nxt = (it, e, s + 1) if s + 1 < NG else (it, 1, 0) if e == 0 else (it + 1, 0, 0)
                        if not (last and e == 1 and s == NG - 1):
                            gate_up(*nxt)
                        down(it, e, s, first and e == 0 and s == 0)
                        if last and e == 1 and s in (1, 3) and norm:
                            norm_turn(nc, c, norm, pe, s // 2, norm_banks)

            router_products()
            router_turn()
            gate_up(0, 0, 0, True)
            turn(0, True, False)
            with pe.Fori(1, TURNS - 1) as it:
                turn(it, False, False)
            turn(TURNS - 1, False, True)

        @block.scalar
        def _(act):
            def router_flat():
                for s in range(NG):
                    act.wait_ge(products_ready, s + 1)
                    nc.scalar.copy(flat_logits[:, s * G:(s + 1) * G], PRODUCTS(s)[0:2 * E]).then_inc(flat_done, 1)

            def router_exps():
                act.wait_ge(chained, 3)
                nc.scalar.activation(inh[:], z[:], ACT.Exp, scale=-1.0).then_inc(distances_exp, 1)
                act.wait_ge(chained, 7)
                nc.scalar.activation(near[:], dist[:], ACT.Exp, scale=-1.0 / 0.1)
                nc.scalar.activation(far[:], dist[:], ACT.Exp, scale=-1.0 / 0.3).then_inc(distances_exp, 1)

            def split_hi(it, e):
                act.wait_ge(stage_in[e], 16 * (it + 1))
                if not (isinstance(it, int) and it == 0):
                    act.wait_ge(out_ready, 2 * (8 * it + 4 * e - 4))
                nc.scalar.copy(flat(wh, e), flat(stage, e)).then_inc(w_hi, 1)

            def activate(it, e, s, m):
                n = 8 * it + 4 * e + s
                act.wait_ge(gated, 4 * n + 2 * m + 1)
                if not (isinstance(it, int) and it == 0 and e == 0 and s == 0):
                    act.wait_ge(hid_done, 2 * n + m - 1)
                nc.scalar.activation(silu[:, m, :], GATE(m), ACT.Silu).then_inc(silu_done, 1)

            def hidden_hi(it, e, s, m):
                n = 8 * it + 4 * e + s
                act.wait_ge(hid_done, 2 * n + m + 1)
                if not (isinstance(it, int) and it == 0 and e == 0 and s < 2):
                    act.wait_ge(out_ready, 2 * (n - 1))
                nc.scalar.copy(hh[:, s % 2, m, :], hidden[:, m, :]).then_inc(hi_done, 1)

            def turn(it, last):
                for e in range(2):
                    for s in range(NG):
                        activate(it, e, s, 0)
                        activate(it, e, s, 1)
                        hidden_hi(it, e, s, 0)
                        hidden_hi(it, e, s, 1)
                        if s == 1 and not (last and e == 1):
                            split_hi(*((it, 1) if e == 0 else (it + 1, 0)))
                        if last and e == 1 and s == 2 and norm:
                            norm_hi(nc, c, norm, act, 0, norm_banks)

            split_hi(0, 0)
            norm_hi(nc, c, own_norm, act, NG - 1, own_banks)
            router_flat()
            router_exps()
            turn(0, False)
            with act.Fori(1, TURNS - 1) as it:
                turn(it, False)
            turn(TURNS - 1, True)
            if norm:
                norm_hi(nc, c, norm, act, 1, norm_banks)

        @block.vector
        def _(dve):
            done = [0]

            def step(ins):
                done[0] += 1
                ins.then_inc(chained, 1)
                dve.wait_ge(chained, done[0])

            v = nc.vector
            row = lambda ap: ap[:].unsqueeze(2).to_broadcast([P, NT, E])

            def router_distances():
                dve.wait_ge(logits_ready, 1)
                step(v.tensor_copy(z[:], LOGITS[:, :, 0:E]))
                step(v.tensor_tensor(z[:], LOGITS[:, :, E:2 * E], z[:], ALU.add))
                step(v.tensor_scalar(z[:], z[:], c.inv_temperature[:, 0:1], None, ALU.mult))
                dve.wait_ge(distances_exp, 1)
                step(v.tensor_scalar(inh[:], inh[:], 1.0, None, ALU.add))
                step(v.reciprocal(inh[:], inh[:]))
                step(v.tensor_scalar(inh[:], inh[:], GOLDEN_CENTER, None, ALU.subtract))
                step(v.scalar_tensor_tensor(out=dist[:], in0=inh[:], scalar=-1.0, in1=inh[:], op0=ALU.mult, op1=ALU.max))
                step(v.tensor_scalar(lo_side[:], z[:], LOGIT_LOWER, None, ALU.is_ge))
                step(v.tensor_scalar(hi_side[:], z[:], 0.0, None, ALU.is_le))
                step(v.tensor_tensor(lo_side[:], lo_side[:], hi_side[:], ALU.mult))
                dve.wait_ge(distances_exp, 2)
                step(v.tensor_tensor(near[:], near[:], lo_side[:], ALU.mult))
                step(v.tensor_reduce(wsum[:], near[:], AX, ALU.add))
                step(v.tensor_scalar(none[:], wsum[:], 1e-8, None, ALU.is_lt))

            def pick(chosen, among):
                step(v.tensor_reduce(most[:], among[:], AX, ALU.max))
                step(v.tensor_tensor(place[:], among[:], row(most), ALU.is_equal))
                step(v.tensor_tensor(place[:], place[:], c.order[:].unsqueeze(1).to_broadcast([P, NT, E]), ALU.mult))
                step(v.tensor_reduce(most[:], place[:], AX, ALU.max))
                step(v.tensor_tensor(chosen[:], place[:], row(most), ALU.is_equal))

            def router_picks():
                pick(greatest, far)
                step(v.scalar_tensor_tensor(out=rest[:], in0=greatest[:], scalar=-4.0, in1=far[:], op0=ALU.mult, op1=ALU.add))
                pick(second, rest)
                step(v.tensor_tensor(greatest[:], greatest[:], second[:], ALU.add))

            def router_weights():
                step(v.tensor_tensor(part[:], far[:], greatest[:], ALU.mult))
                step(v.tensor_reduce(some[:], part[:], AX, ALU.add))
                step(v.tensor_scalar(some[:], some[:], 1e-8, None, ALU.max))
                step(v.reciprocal(some[:], some[:]))
                step(v.tensor_tensor(part[:], part[:], row(some), ALU.mult))
                step(v.tensor_tensor(part[:], part[:], row(none), ALU.mult))
                step(v.tensor_scalar(none[:], none[:], -1.0, 1.0, ALU.mult, ALU.add))
                step(v.tensor_tensor(near[:], near[:], row(none), ALU.mult))
                step(v.tensor_tensor(near[:], near[:], part[:], ALU.add))
                step(v.tensor_reduce(wsum[:], near[:], AX, ALU.add))
                step(v.tensor_scalar(wsum[:], wsum[:], 1e-8, None, ALU.max))
                step(v.reciprocal(wsum[:], wsum[:]))
                step(v.tensor_tensor(gate[:], near[:], row(wsum), ALU.mult))

            def split_lo(it, e):
                dve.wait_ge(w_hi, 2 * it + e + 1)
                nc.vector.tensor_tensor(flat(wl, e), flat(stage, e), flat(wh, e).bitcast(F32), ALU.subtract).then_inc(w_lo, 1)

            def hidden_rows(it, e, s, m):
                n = 8 * it + 4 * e + s
                dve.wait_ge(gated, 4 * n + 2 * m + 2)
                dve.wait_ge(silu_done, 2 * n + m + 1)
                if not (isinstance(it, int) and it == 0 and e == 0 and s == 0):
                    dve.wait_ge(lo_done, 2 * n + m - 1)
                nc.vector.tensor_tensor(hidden[:, m, :], UP(m), silu[:, m, :], ALU.mult).then_inc(hid_done, 1)

            def hidden_lo(it, e, s, m):
                n = 8 * it + 4 * e + s
                dve.wait_ge(hi_done, 2 * n + m + 1)
                nc.vector.tensor_tensor(hl[:, s % 2, m, :], hidden[:, m, :], hh[:, s % 2, m, :].bitcast(F32), ALU.subtract).then_inc(lo_done, 1)

            def add_out(it, e, s):
                n = 8 * it + 4 * e + s
                if s == 0:
                    dve.wait_ge(col_done, 2 * it + e + 1)
                for i in range(2):
                    dve.wait_ge(out_ready, 2 * n + i + 1)
                    for t in range(2):
                        at = s * TG + 2 * i + t
                        ins = nc.vector.scalar_tensor_tensor(out=c.x[:, at, :], in0=OUT(i)[:, t, :], scalar=col[:, e, at:at + 1], in1=c.x[:, at, :], op0=ALU.mult, op1=ALU.add)
                    ins.then_inc(out_added, 1)

            def take_weights(it, e):
                ex = 2 * it + e
                nc.vector.tensor_copy(col[:, e, :].unsqueeze(2), gate[:, :, ex:ex + 1] if isinstance(ex, int) else gate[:, :, bass.ds(ex, 1)]).then_inc(col_done, 1)

            def normalise(s):
                dve.wait_ge(out_added, 2 * (8 * (TURNS - 1) + 4 + s) + 2)
                norm_stats(nc, c, norm, dve, s)
                norm_rows(nc, c, norm, dve, s)

            def turn(it, first, last):
                for e in range(2):
                    for s in range(NG):
                        hidden_rows(it, e, s, 0)
                        hidden_rows(it, e, s, 1)
                        hidden_lo(it, e, s, 0)
                        hidden_lo(it, e, s, 1)
                        if s == 1 and not (last and e == 1):
                            split_lo(*((it, 1) if e == 0 else (it + 1, 0)))
                        if last and e == 1 and s == 2 and norm:
                            norm_lo(nc, c, norm, dve, 0, norm_banks)
                        if first and e == 0 and s == 0:
                            router_picks()
                        if first and e == 0 and s == 1:
                            router_weights()
                            take_weights(0, 0)
                        if not (first and e == 0 and s == 0):
                            add_out(*((it, e, s - 1) if s else (it, 0, NG - 1) if e == 1 else (it - 1, 1, NG - 1)))
                        if s == 0 and not (first and e == 0):
                            take_weights(it, e)
                        if last and e == 1 and s in (1, 3) and norm:
                            normalise(s // 2)

            norm_rows(nc, c, own_norm, dve, NG - 1)
            split_lo(0, 0)
            norm_lo(nc, c, own_norm, dve, NG - 1, own_banks)
            router_distances()
            turn(0, True, False)
            with dve.Fori(1, TURNS - 1) as it:
                turn(it, False, False)
            turn(TURNS - 1, False, True)
            add_out(TURNS - 1, 1, NG - 1)
            if norm:
                norm_lo(nc, c, norm, dve, 1, norm_banks)


def hybrid_kernel(nc, x, const, order, small, temperature, wa, wb_qkv, wb_out, wf, out):
    with ExitStack() as ctx:
        sb = lambda n, s, d=F32: ctx.enter_context(nc.sbuf_tensor(n, s, d))
        c = Core()
        c.x = sb("x", [P, NT, D])
        c.xh, c.xl = sb("xh", [P, KD, N], F32R), sb("xl", [P, KD, N], F32R)
        c.const = sb("const", [P, C_COLS])
        c.ident = c.const[:, C_IDENT:C_IDENT + P]
        c.ident16, c.mask16 = sb("ident16", [P, P], BF16), sb("mask16", [P, P], BF16)
        c.order = sb("order", [P, E])
        c.temperature, c.inv_temperature = sb("temperature", [P, 1]), sb("inv_temperature", [P, 1])
        c.sh, c.sl = sb("sh", [P, KD, S_WR], F32R), sb("sl", [P, KD, S_WR], F32R)
        c.wr = sb("wr", [P, KD, P], F32R)
        c.minus_half = sb("minus_half", [P, TG])
        a_stage = sb("a_stage", [P, A_COLS])
        b_stage = sb("b_stage", [P, 3, KD, 2 * P])
        bo_stage = sb("bo_stage", [P, 2, D])
        f_stage = sb("f_stage", [P, 2, 3, KD, F])
        a_in, b_in, bo_in = (ctx.enter_context(nc.semaphore(n)) for n in ("a_weights_in", "b_weights_in", "b_output_weights_in"))
        f1_in, f2_in = ([ctx.enter_context(nc.semaphore(f"{f}_weights_in_{e}")) for e in ("even", "odd")] for f in ("f1", "f2"))
        stored = [ctx.enter_context(nc.semaphore(f"stored_{s}")) for s in range(NG)]
        c.moments, c.meanvar = sb("moments", [P, TG, 6]), sb("meanvar", [P, 2, TG, 2])
        c.shifted, c.rstd = sb("shifted", [P, 2, TG]), sb("rstd", [P, 2, TG])
        c.normed = sb("normed", [P, TG, D])
        norm2, norm3, norm4 = (norm_signals(nc, ctx, c, n) for n in ("norm2", "norm3", "norm4"))
        c.ps = ctx.enter_context(nc.psum_tensor("ps", [P, 8, 512], F32))

        with ExitStack() as inner:
            sa = lambda n, s, d=F32: inner.enter_context(nc.sbuf_tensor(n, s, d))
            a = Core()
            a.q1h, a.q1l, a.q2 = sa("q1h", [P, N], F32R), sa("q1l", [P, N], F32R), sa("q2", [P, N], F32R)
            a.keys, a.kh, a.kl = sa("keys", [P, N]), sa("kh", [P, N], F32R), sa("kl", [P, N], F32R)
            a.wh, a.wl = sa("a_wh", [P, 2, 2, P], F32R), sa("a_wl", [P, 2, 2, P], F32R)
            a.values = sa("values", [P, NT, KVR])
            opening(nc, c, "open", a, x, const, small, temperature, order, wa, a_stage, a_in)
            attention_a(nc, c, "aa", a, wa, a_stage, a_in, norm2, [(f_stage[:, e], wf[e], f1_in[e]) for e in range(2)])
        experts(nc, c, "f1", wf, f_stage, f1_in, norm2, ahead=[(b_stage[:], wb_qkv[0], b_in), (bo_stage[:], wb_out[0], bo_in)], norm=norm3)
        attention_b(nc, c, "ab", wb_qkv, wb_out, b_stage, bo_stage, b_in, bo_in, norm3, norm4, [(f_stage[:, e], wf[e], f2_in[e]) for e in range(2)])
        experts(nc, c, "f2", wf, f_stage, f2_in, norm4, result=(out.rearrange("(t p) d -> p t d", p=P), stored))


def constants():
    const = np.zeros((P, C_COLS), np.float32)
    pos = np.arange(T, dtype=np.float32)
    theta = (1.0 / np.float32(10000.0) ** (np.arange(0, ROT, 2, dtype=np.float32) / ROT)).astype(np.float32)
    ang = (pos[None, :] * theta[:, None]).astype(np.float32)
    const[0:64, C_COSA:C_COSA + T] = 1.0
    const[64:96, C_COSA:C_COSA + T] = np.cos(ang)
    const[96:128, C_COSA:C_COSA + T] = np.cos(ang)
    const[64:96, C_SINA:C_SINA + T] = -np.sin(ang)
    const[96:128, C_SINA:C_SINA + T] = np.sin(ang)
    half = 64
    freqs = np.power(np.float32(10000.0), -np.arange(half, dtype=np.float32) / half).astype(np.float32)
    rad = (pos[None, :] * freqs[:, None]).astype(np.float32)
    mult = np.float32((1.0 / 128.0) ** 0.5)
    for r in (0, 64):
        const[r:r + 64, C_COSB:C_COSB + T] = np.cos(rad) * mult
    const[0:64, C_SINB:C_SINB + T] = -np.sin(rad) * mult
    const[64:128, C_SINB:C_SINB + T] = np.sin(rad) * mult
    const[:, C_IDENT:C_IDENT + P] = np.eye(P, dtype=np.float32)
    const[:, C_MASK:C_MASK + P] = np.triu(np.full((P, P), -1e30, np.float32), 1)
    order = np.arange(E, 0, -1, dtype=np.float32).reshape(1, E)
    return const, order


def kernel(**inputs):
    import numpy as _np
    import concourse.bacc as _bacc
    from concourse import mybir as _mybir
    from concourse.bass_utils import run_bass_kernel_spmd as _run

    w = {k: _np.asarray(v) for k, v in inputs.items()}
    const, order = constants()
    pairs = _np.concatenate([_np.arange(0, ROT, 2), _np.arange(1, ROT, 2)])

    qa = w["L0_attn_a_q_a_w"].T
    kva = w["L0_attn_a_kv_a_w"]
    kva = _np.concatenate([kva[:KVR], kva[KVR:][pairs]]).T
    small = _np.concatenate([qa, qa[:, P:QR], kva, w["L0_ffn_Wr"]], axis=1)
    small = _np.ascontiguousarray(small.reshape(KD, P, S_COLS).transpose(1, 0, 2))

    qb = w["L0_attn_a_q_b_w"].reshape(HP, 2, NOPE + ROT, QR)
    qpass = qb[:, :, :NOPE]
    qpass = _np.concatenate([qpass, qpass[..., P:QR]], axis=-1).reshape(HP, P, 256)
    qrot = qb[:, :, NOPE:][:, :, pairs].transpose(0, 3, 1, 2)
    qrot = _np.concatenate([qrot, qrot[:, P:QR]], axis=1).reshape(HP, 2, P, 2 * ROT).transpose(0, 2, 1, 3).reshape(HP, P, 4 * ROT)
    kvb = w["L0_attn_a_kv_b_w"].reshape(HP, 2, NOPE + VD, KVR)
    wk = kvb[:, :, :NOPE].reshape(HP, P, KVR)
    wv = kvb[:, :, NOPE:].transpose(0, 2, 1, 3).reshape(HP, P, 2 * KVR)
    ow = w["L0_attn_a_o_w"].T.reshape(HP, 2, VD, D).transpose(0, 2, 1, 3).reshape(HP, P, 2 * D)
    wa = _np.ascontiguousarray(_np.concatenate([qpass, wk, qrot, wv, ow], axis=2))

    qkv = _np.stack([w["L0_attn_b_wq"], w["L0_attn_b_wk"], w["L0_attn_b_wv"]])
    wb_qkv = _np.ascontiguousarray(qkv.reshape(3, KD, P, HP, 2 * P).transpose(3, 2, 0, 1, 4))
    wb_out = _np.ascontiguousarray(w["L0_attn_b_wo"].reshape(HP, 2, P, D).transpose(0, 2, 1, 3))

    wf = _np.stack([w["L0_ffn_Wg"], w["L0_ffn_Wu"], w["L0_ffn_Wd"]], axis=1)
    wf = _np.ascontiguousarray(wf.reshape(E, 3, KD, P, F).transpose(0, 3, 1, 2, 4))

    nc = _bacc.Bacc("TRN2", target_bir_lowering=False, num_devices=1)
    arrays = {
        "x_in": _np.ascontiguousarray(w["L0_attn_a_x"]).reshape(N, D),
        "const_in": const, "order_in": order, "small_weights": small,
        "temperature_in": w["L0_ffn_temperature"].reshape(1, 1),
        "wa_in": wa, "wb_qkv_in": wb_qkv, "wb_out_in": wb_out, "wf_in": wf,
    }
    args = [nc.dram_tensor(n, a.shape, _mybir.dt.from_np(a.dtype), kind="ExternalInput").ap() for n, a in arrays.items()]
    out = nc.dram_tensor("out_0", (N, D), _mybir.dt.float32, kind="ExternalOutput").ap()
    hybrid_kernel(nc, *args, out)
    r = _run(nc, [arrays], core_ids=[0])
    return r.results[0]["out_0"].reshape(B, T, D)
```
